# Optimizing a Trainium2 kernel written in Bass

```python
import numpy as np
import jax
import jax.numpy as jnp

def _softmax(x, axis=-1):
    return jax.nn.softmax(x, axis=axis)

def _gelu(x):
    return jax.nn.gelu(x, approximate=True)

def _silu(x):
    return jax.nn.silu(x)

def _sigmoid(x):
    return jax.nn.sigmoid(x)

def _layernorm(x, axis=-1, eps=1e-05):
    m = jnp.mean(x, axis=axis, keepdims=True)
    v = jnp.var(x, axis=axis, keepdims=True)
    return (x - m) / jnp.sqrt(v + eps)

def _scatter_add(tgt, idx, src, axis=0):
    return tgt.at[idx].add(src)

def _segment_sum(src, seg, n):
    return jax.ops.segment_sum(src, seg, n)
kernel_name = 'mk_seq_postln_d1_jaxref_r4_ca74e2'

def setup_inputs(seed: int=0):
    np.random.seed(seed)
    _w = jnp.asarray

    def _L0_attn_setup():
        import jax, jax.numpy as jnp
        import numpy as np
        EMBED = 256
        HEADS = 16
        HEAD_DIM = EMBED // HEADS
        RANK = 8
        ALPHA = 16
        SCALE_LORA = ALPHA / RANK

        def _lora_linear(x, W, b, A, B):
            return x @ W.T + b + SCALE_LORA * (x @ A.T @ B.T)
        key = jax.random.key(seed)
        ks = jax.random.split(key, 17)
        d = {'x': jax.random.normal(ks[0], (2, 512, EMBED), dtype=jnp.float32)}
        names = ['q', 'k', 'v', 'o']
        i = 1
        for n in names:
            d[f'W{n}'] = jax.random.normal(ks[i], (EMBED, EMBED), dtype=jnp.float32) * 0.02
            i += 1
            d[f'b{n}'] = jnp.zeros((EMBED,), dtype=jnp.float32)
            d[f'A{n}'] = jax.random.normal(ks[i], (RANK, EMBED), dtype=jnp.float32) * 0.02
            i += 1
            d[f'B{n}'] = jax.random.normal(ks[i], (EMBED, RANK), dtype=jnp.float32) * 0.02
            i += 1
        return d
    _L0_attn_in = _L0_attn_setup()

    def _L0_ffn_setup():
        import jax, jax.numpy as jnp
        import numpy as np
        DIM = 256
        H = 8
        DH = 64
        W = 64
        NQ = 128
        NKV = 256
        EPS = 1.0
        NITERS = 50
        FETCH = 9.0 / 8.0
        SCALE = DH ** (-0.5)

        def _ln(x, w, b):
            m = x.mean(-1, keepdims=True)
            v = ((x - m) ** 2).mean(-1, keepdims=True)
            return (x - m) * jax.lax.rsqrt(v + 1e-05) * w + b

        def _rms(x, g):
            n = jnp.maximum(jnp.linalg.norm(x, axis=-1, keepdims=True), 1e-12)
            return x / n * np.sqrt(DIM).astype(np.float32) * g

        def local_attn(x, Wqkv, Wout):
            b, n, _ = x.shape
            nw = n // W
            qkv = x @ Wqkv.T
            q, k, v = jnp.split(qkv, 3, axis=-1)

            def towin(t):
                return t.reshape(b, nw, W, H, DH).transpose(0, 3, 1, 2, 4)
            q, k, v = map(towin, (q, k, v))

            def expand(t):
                tp = jnp.pad(t, ((0, 0), (0, 0), (1, 1), (0, 0), (0, 0)))
                return jnp.concatenate([tp[:, :, :-2], tp[:, :, 1:-1], tp[:, :, 2:]], axis=3)
            ke, ve = (expand(k), expand(v))
            sim = jnp.einsum('bhnid,bhnjd->bhnij', q, ke) * SCALE
            win = jnp.arange(nw)
            valid = jnp.concatenate([jnp.repeat((win > 0)[:, None], W, 1), jnp.ones((nw, W), bool), jnp.repeat((win < nw - 1)[:, None], W, 1)], axis=1)
            sim = jnp.where(valid[None, None, :, None, :], sim, -1000000000.0)
            attn = jax.nn.softmax(sim, axis=-1)
            o = jnp.einsum('bhnij,bhnjd->bhnid', attn, ve)
            o = o.transpose(0, 2, 3, 1, 4).reshape(b, n, H * DH)
            return o @ Wout.T

        def route(x, routing_token, num_tokens):
            s = jnp.einsum('bnd,rd->brn', x, routing_token).reshape(x.shape[0], x.shape[1])
            n = s.shape[-1]
            logk = jnp.log(jnp.asarray(min(num_tokens * FETCH, float(n)), s.dtype))

            def body(ab, _):
                a, bb = ab
                a = EPS * (logk - jax.nn.logsumexp((s + bb) / EPS, axis=-1, keepdims=True))
                bb = -jax.nn.relu(s + a)
                return ((a, bb), None)
            (a, bb), _ = jax.lax.scan(body, (jnp.zeros((s.shape[0], 1), s.dtype), -s), None, length=NITERS)
            scores = jnp.exp((s + a + bb) / EPS)
            sel_scores, sel_idx = jax.lax.top_k(scores, num_tokens)
            sel_scores = sel_scores + jax.lax.stop_gradient(1.0 - sel_scores)
            return (sel_scores, sel_idx)

        def heavy_attn(xq, ctx, scores_kv, gamma, Wq, Wkv, Wout, null_kv):
            b = xq.shape[0]
            xq = _rms(xq, gamma)
            ctx = _rms(ctx, gamma)
            q = (xq @ Wq.T).reshape(b, -1, H, DH).transpose(0, 2, 1, 3)
            kv = (ctx @ Wkv.T).reshape(b, -1, H, 2 * DH).transpose(0, 2, 1, 3)
            k, v = (kv[..., :DH], kv[..., DH:])
            v = v * scores_kv[:, None, :, None]
            nk = jnp.broadcast_to(null_kv[0][None, :, None, :], (b, H, 1, DH))
            nv = jnp.broadcast_to(null_kv[1][None, :, None, :], (b, H, 1, DH))
            k = jnp.concatenate([nk, k], axis=2)
            v = jnp.concatenate([nv, v], axis=2)
            sim = jnp.einsum('bhid,bhjd->bhij', q, k) * SCALE
            attn = jax.nn.softmax(sim, axis=-1)
            o = jnp.einsum('bhij,bhjd->bhid', attn, v)
            o = o.transpose(0, 2, 1, 3).reshape(b, -1, H * DH)
            return o @ Wout.T
        key = jax.random.key(seed)
        ks = jax.random.split(key, 12)
        D, IN = (DIM, H * DH)
        w = lambda k, shape: jax.random.normal(k, shape, jnp.float32) * 0.02
        return {'x': jax.random.normal(ks[0], (4, 1024, D), jnp.float32), 'ln_w': jnp.ones((D,), jnp.float32), 'ln_b': jnp.zeros((D,), jnp.float32), 'Wqkv': w(ks[1], (3 * IN, D)), 'Wout_l': w(ks[2], (D, IN)), 'rt_q': jax.random.normal(ks[3], (1, D), jnp.float32), 'rt_kv': jax.random.normal(ks[4], (1, D), jnp.float32), 'gamma': jnp.ones((D,), jnp.float32), 'Wq': w(ks[5], (IN, D)), 'Wkv': w(ks[6], (2 * IN, D)), 'Wout_h': w(ks[7], (D, IN)), 'null_kv': jax.random.normal(ks[8], (2, H, DH), jnp.float32), 'null_q': jax.random.normal(ks[9], (D,), jnp.float32)}
    _L0_ffn_in = _L0_ffn_setup()
    _d = {'L0_attn_x': _L0_attn_in['x'], 'L0_attn_Wq': _L0_attn_in['Wq'], 'L0_attn_bq': _L0_attn_in['bq'], 'L0_attn_Aq': _L0_attn_in['Aq'], 'L0_attn_Bq': _L0_attn_in['Bq'], 'L0_attn_Wk': _L0_attn_in['Wk'], 'L0_attn_bk': _L0_attn_in['bk'], 'L0_attn_Ak': _L0_attn_in['Ak'], 'L0_attn_Bk': _L0_attn_in['Bk'], 'L0_attn_Wv': _L0_attn_in['Wv'], 'L0_attn_bv': _L0_attn_in['bv'], 'L0_attn_Av': _L0_attn_in['Av'], 'L0_attn_Bv': _L0_attn_in['Bv'], 'L0_attn_Wo': _L0_attn_in['Wo'], 'L0_attn_bo': _L0_attn_in['bo'], 'L0_attn_Ao': _L0_attn_in['Ao'], 'L0_attn_Bo': _L0_attn_in['Bo'], 'L0_ffn_ln_w': _L0_ffn_in['ln_w'], 'L0_ffn_ln_b': _L0_ffn_in['ln_b'], 'L0_ffn_Wqkv': _L0_ffn_in['Wqkv'], 'L0_ffn_Wout_l': _L0_ffn_in['Wout_l'], 'L0_ffn_rt_q': _L0_ffn_in['rt_q'], 'L0_ffn_rt_kv': _L0_ffn_in['rt_kv'], 'L0_ffn_gamma': _L0_ffn_in['gamma'], 'L0_ffn_Wq': _L0_ffn_in['Wq'], 'L0_ffn_Wkv': _L0_ffn_in['Wkv'], 'L0_ffn_Wout_h': _L0_ffn_in['Wout_h'], 'L0_ffn_null_kv': _L0_ffn_in['null_kv'], 'L0_ffn_null_q': _L0_ffn_in['null_q']}
    _x0 = _d['L0_attn_x']
    _d['L0_attn_x'] = jax.random.normal(jax.random.fold_in(jax.random.key(seed), 1), (32, 512, 256), dtype=_x0.dtype)
    del _x0
    return _d

def reference(L0_attn_x, L0_attn_Wq, L0_attn_bq, L0_attn_Aq, L0_attn_Bq, L0_attn_Wk, L0_attn_bk, L0_attn_Ak, L0_attn_Bk, L0_attn_Wv, L0_attn_bv, L0_attn_Av, L0_attn_Bv, L0_attn_Wo, L0_attn_bo, L0_attn_Ao, L0_attn_Bo, L0_ffn_ln_w, L0_ffn_ln_b, L0_ffn_Wqkv, L0_ffn_Wout_l, L0_ffn_rt_q, L0_ffn_rt_kv, L0_ffn_gamma, L0_ffn_Wq, L0_ffn_Wkv, L0_ffn_Wout_h, L0_ffn_null_kv, L0_ffn_null_q):

    def _L0_attn_ref(x, Wq, bq, Aq, Bq, Wk, bk, Ak, Bk, Wv, bv, Av, Bv, Wo, bo, Ao, Bo):
        import jax, jax.numpy as jnp
        import numpy as np
        EMBED = 256
        HEADS = 16
        HEAD_DIM = EMBED // HEADS
        RANK = 8
        ALPHA = 16
        SCALE_LORA = ALPHA / RANK

        def _lora_linear(x, W, b, A, B):
            return x @ W.T + b + SCALE_LORA * (x @ A.T @ B.T)
        N, S, _ = x.shape
        Q = _lora_linear(x, Wq, bq, Aq, Bq).reshape(N, S, HEADS, HEAD_DIM)
        K = _lora_linear(x, Wk, bk, Ak, Bk).reshape(N, S, HEADS, HEAD_DIM)
        V = _lora_linear(x, Wv, bv, Av, Bv).reshape(N, S, HEADS, HEAD_DIM)
        energy = jnp.einsum('nqhd,nkhd->nhqk', Q, K) / jnp.sqrt(jnp.float32(HEAD_DIM))
        attn = jax.nn.softmax(energy, axis=-1)
        out = jnp.einsum('nhqk,nkhd->nqhd', attn, V).reshape(N, S, EMBED)
        return _lora_linear(out, Wo, bo, Ao, Bo)

    def _L0_ffn_ref(x, ln_w, ln_b, Wqkv, Wout_l, rt_q, rt_kv, gamma, Wq, Wkv, Wout_h, null_kv, null_q):
        import jax, jax.numpy as jnp
        import numpy as np
        DIM = 256
        H = 8
        DH = 64
        W = 64
        NQ = 128
        NKV = 256
        EPS = 1.0
        NITERS = 50
        FETCH = 9.0 / 8.0
        SCALE = DH ** (-0.5)

        def _ln(x, w, b):
            m = x.mean(-1, keepdims=True)
            v = ((x - m) ** 2).mean(-1, keepdims=True)
            return (x - m) * jax.lax.rsqrt(v + 1e-05) * w + b

        def _rms(x, g):
            n = jnp.maximum(jnp.linalg.norm(x, axis=-1, keepdims=True), 1e-12)
            return x / n * np.sqrt(DIM).astype(np.float32) * g

        def local_attn(x, Wqkv, Wout):
            b, n, _ = x.shape
            nw = n // W
            qkv = x @ Wqkv.T
            q, k, v = jnp.split(qkv, 3, axis=-1)

            def towin(t):
                return t.reshape(b, nw, W, H, DH).transpose(0, 3, 1, 2, 4)
            q, k, v = map(towin, (q, k, v))

            def expand(t):
                tp = jnp.pad(t, ((0, 0), (0, 0), (1, 1), (0, 0), (0, 0)))
                return jnp.concatenate([tp[:, :, :-2], tp[:, :, 1:-1], tp[:, :, 2:]], axis=3)
            ke, ve = (expand(k), expand(v))
            sim = jnp.einsum('bhnid,bhnjd->bhnij', q, ke) * SCALE
            win = jnp.arange(nw)
            valid = jnp.concatenate([jnp.repeat((win > 0)[:, None], W, 1), jnp.ones((nw, W), bool), jnp.repeat((win < nw - 1)[:, None], W, 1)], axis=1)
            sim = jnp.where(valid[None, None, :, None, :], sim, -1000000000.0)
            attn = jax.nn.softmax(sim, axis=-1)
            o = jnp.einsum('bhnij,bhnjd->bhnid', attn, ve)
            o = o.transpose(0, 2, 3, 1, 4).reshape(b, n, H * DH)
            return o @ Wout.T

        def route(x, routing_token, num_tokens):
            s = jnp.einsum('bnd,rd->brn', x, routing_token).reshape(x.shape[0], x.shape[1])
            n = s.shape[-1]
            logk = jnp.log(jnp.asarray(min(num_tokens * FETCH, float(n)), s.dtype))

            def body(ab, _):
                a, bb = ab
                a = EPS * (logk - jax.nn.logsumexp((s + bb) / EPS, axis=-1, keepdims=True))
                bb = -jax.nn.relu(s + a)
                return ((a, bb), None)
            (a, bb), _ = jax.lax.scan(body, (jnp.zeros((s.shape[0], 1), s.dtype), -s), None, length=NITERS)
            scores = jnp.exp((s + a + bb) / EPS)
            sel_scores, sel_idx = jax.lax.top_k(scores, num_tokens)
            sel_scores = sel_scores + jax.lax.stop_gradient(1.0 - sel_scores)
            return (sel_scores, sel_idx)

        def heavy_attn(xq, ctx, scores_kv, gamma, Wq, Wkv, Wout, null_kv):
            b = xq.shape[0]
            xq = _rms(xq, gamma)
            ctx = _rms(ctx, gamma)
            q = (xq @ Wq.T).reshape(b, -1, H, DH).transpose(0, 2, 1, 3)
            kv = (ctx @ Wkv.T).reshape(b, -1, H, 2 * DH).transpose(0, 2, 1, 3)
            k, v = (kv[..., :DH], kv[..., DH:])
            v = v * scores_kv[:, None, :, None]
            nk = jnp.broadcast_to(null_kv[0][None, :, None, :], (b, H, 1, DH))
            nv = jnp.broadcast_to(null_kv[1][None, :, None, :], (b, H, 1, DH))
            k = jnp.concatenate([nk, k], axis=2)
            v = jnp.concatenate([nv, v], axis=2)
            sim = jnp.einsum('bhid,bhjd->bhij', q, k) * SCALE
            attn = jax.nn.softmax(sim, axis=-1)
            o = jnp.einsum('bhij,bhjd->bhid', attn, v)
            o = o.transpose(0, 2, 1, 3).reshape(b, -1, H * DH)
            return o @ Wout.T
        b, n, d = x.shape
        light = local_attn(_ln(x, ln_w, ln_b), Wqkv, Wout_l)
        sq, iq = route(x, rt_q, NQ)
        skv, ikv = route(x, rt_kv, NKV)
        br = jnp.arange(b)[:, None]
        xq = x[br, iq]
        xkv = x[br, ikv]
        heavy = heavy_attn(xq, xkv, skv, gamma, Wq, Wkv, Wout_h, null_kv)
        heavy = heavy * sq[..., None]
        out = jnp.broadcast_to(null_q[None, None, :], (b, n, d))
        out = out.at[br, iq].set(heavy)
        return out + light
    x = L0_attn_x
    x = _layernorm(x + _L0_attn_ref(x, L0_attn_Wq, L0_attn_bq, L0_attn_Aq, L0_attn_Bq, L0_attn_Wk, L0_attn_bk, L0_attn_Ak, L0_attn_Bk, L0_attn_Wv, L0_attn_bv, L0_attn_Av, L0_attn_Bv, L0_attn_Wo, L0_attn_bo, L0_attn_Ao, L0_attn_Bo), axis=-1)
    x = _layernorm(x + _L0_ffn_ref(x, L0_ffn_ln_w, L0_ffn_ln_b, L0_ffn_Wqkv, L0_ffn_Wout_l, L0_ffn_rt_q, L0_ffn_rt_kv, L0_ffn_gamma, L0_ffn_Wq, L0_ffn_Wkv, L0_ffn_Wout_h, L0_ffn_null_kv, L0_ffn_null_q), axis=-1)
    return x

_drawn_inputs = setup_inputs


def setup_inputs(seed=0):
    import zlib

    import numpy as np

    out = dict(_drawn_inputs(seed))
    spreads = {'L0_attn_bq': (0.0, 0.8),
     'L0_attn_bk': (0.0, 0.8),
     'L0_attn_bv': (0.0, 0.1),
     'L0_attn_bo': (0.0, 0.1),
     'L0_ffn_ln_w': (1.0, 0.6),
     'L0_ffn_ln_b': (0.0, 0.722),
     'L0_ffn_gamma': (1.0, 0.6)}
    factors = {'L0_attn_Wq': 5.379,
     'L0_attn_Aq': 8.0,
     'L0_attn_Bq': 8.0,
     'L0_attn_Wk': 4.668,
     'L0_attn_Ak': 8.0,
     'L0_attn_Bk': 8.0,
     'L0_attn_Wv': 4.423,
     'L0_attn_Av': 8.0,
     'L0_attn_Bv': 8.0,
     'L0_attn_Ao': 8.0,
     'L0_attn_Bo': 8.0,
     'L0_ffn_Wqkv': 3.297,
     'L0_ffn_Wout_l': 3.06,
     'L0_ffn_rt_kv': 8.0,
     'L0_ffn_Wq': 8.0,
     'L0_ffn_Wkv': 6.17,
     'L0_ffn_Wout_h': 6.021,
     'L0_ffn_null_kv': 8.0}
    for name, (base, spread) in spreads.items():
        noise = np.random.default_rng([zlib.crc32(name.encode()), seed]).standard_normal(out[name].shape)
        drawn = base * np.exp(spread * noise) if base else spread * noise
        out[name] = jnp.asarray(drawn.astype(out[name].dtype))
    for name, factor in factors.items():
        out[name] = (out[name] * factor).astype(out[name].dtype)
    return out
```

```python
import math
from contextlib import ExitStack

import concourse.bass as bass
from concourse import mybir

F32 = mybir.dt.float32
BF16 = mybir.dt.bfloat16
ALU = mybir.AluOpType
ACT = mybir.ActivationFunctionType
AX = mybir.AxisListType

P = 128
NB = 32
S = 512
E = 256
T = S // P
C = E // P
H1, D1 = 16, 16
W1H = 32
G1 = H1 // 4
RANK = 8
LORA = 16 / 8
H2, D2 = 8, 64
IN2 = H2 * D2
M2 = IN2 // P
W2H = D2 + 1
WIN = 64
NQ, NKV = 128, 256
NSEL = NQ + NKV
ITERS = 50
EPS_LN = 1e-5
DEEP = 96
SHIFT = 3
Q_PARTS = (0, 0, 0, 1, 1, 2)
K_PARTS = (0, 1, 2, 0, 1, 0)
LOWEST = -87.33654
NEG = -3.0e38


def block_kernel(nc, x, xT, wq, wk, wv, wo, aq, ak, av, ao, bq_, bk_, bv_, bo_,
                 vec_q, vec_k, vec_v, vec_o, ln_w, ln_b, l_qk, l_v, l_out, rt_q, rt_kv,
                 gamma, h_q, h_k, h_v, h_out_w, null_k, null_v, null_q, out):
    ctx = ExitStack()
    with ctx:
        def sb(name, shape, dt=F32):
            return ctx.enter_context(nc.sbuf_tensor(name, shape, dt))

        def sem(name):
            return ctx.enter_context(nc.semaphore(name))

        def dram(name, shape, dt=F32):
            return nc.dram_tensor(name, shape, dt, kind="Internal").ap()

        parts_d = dram("parts_d", (2, 3, C * P, S), BF16)
        norm_d = dram("norm_d", (NB, P, T * E))
        light_d = dram("light_d", (NB, P, T * E))
        route_d = dram("route_d", (NB, 2 * T, P))
        slot_d = dram("slot_d", (2 * NB, S))

        ident = sb("ident", [P, P])
        PS = ctx.enter_context(nc.psum_tensor("PS", [P, 8, 512], F32))

        w_q = sb("w_q", [P, C, E]); w_k = sb("w_k", [P, C, E])
        w_v = sb("w_v", [P, C, E]); w_o = sb("w_o", [P, C, E])
        b_q = sb("b_q", [P, C]); b_k = sb("b_k", [P, C])
        b_v = sb("b_v", [P, E]); b_o = sb("b_o", [P, E])
        lnw = sb("lnw", [P, C]); lnb = sb("lnb", [P, C]); gam = sb("gam", [P, C])
        rt = sb("rt", [P, 2, E])
        half = sb("half", [P, 4 * T])

        weights = [(w_q, wq, aq, vec_q), (w_k, wk, ak, vec_k), (w_v, wv, av, vec_v), (w_o, wo, ao, vec_o)]

        s_w = sem("s_w"); s_init = sem("s_init"); s_ident = sem("s_ident")
        s_lora = sem("s_lora"); s_lora_used = sem("s_lora_used"); s_ready = sem("s_ready")
        step_sems = []

        def step_sem(name):
            step_sems.append(sem(name))
            return step_sems[-1]

        s_xT = step_sem("s_xT"); s_x = step_sem("s_x")
        s_qk = step_sem("s_qk"); s_v1 = step_sem("s_v1"); s_qk32 = step_sem("s_qk32")
        s_split = step_sem("s_split"); s_pool = step_sem("s_pool"); s_parts = [step_sem("s_q_parts"), step_sem("s_k_parts")]; s_stack = step_sem("s_stack")
        s_vx = step_sem("s_vx"); s_s1 = step_sem("s_s1"); s_max = step_sem("s_max"); s_maxT = step_sem("s_maxT")
        s_shift = step_sem("s_shift"); s_shift_in = step_sem("s_shift_in"); s_s2 = step_sem("s_s2"); s_p = step_sem("s_p")
        s_pv = step_sem("s_pv"); s_ot = step_sem("s_ot"); s_tok = step_sem("s_tok"); s_an = step_sem("s_an")
        s_aT = step_sem("s_aT"); s_aTs = step_sem("s_aTs"); s_y = step_sem("s_y"); s_xb = step_sem("s_xb")
        s_dve = step_sem("s_dve"); s_var = step_sem("s_var"); s_rstd = step_sem("s_rstd"); s_x1 = step_sem("s_x1")
        s_xn = step_sem("s_xn"); s_norm_out = step_sem("s_norm_out"); s_rt = step_sem("s_rt"); s_rtT = step_sem("s_rtT")
        s_rts = step_sem("s_rts"); s_route_out = step_sem("s_route_out")
        s_xlT = step_sem("s_xlT"); s_xl = step_sem("s_xl"); s_lp = step_sem("s_lp"); s_lpa = step_sem("s_lpa"); s_lpd = step_sem("s_lpd")
        s_vodd = step_sem("s_vodd"); s_ls = step_sem("s_ls"); s_lmax = step_sem("s_lmax"); s_lp_e = step_sem("s_lp_e")
        s_lpT = step_sem("s_lpT"); s_lpTs = step_sem("s_lpTs"); s_lo = step_sem("s_lo"); s_lon = step_sem("s_lon")
        s_loT = step_sem("s_loT"); s_loTs = step_sem("s_loTs"); s_lz = step_sem("s_lz"); s_z = step_sem("s_z"); s_z_out = step_sem("s_z_out")

        def pool_pow(out_ap, in_ap):
            return nc.gpsimd.tensor_tensor(out_ap, in_ap, half[:, 0:in_ap.shape[-1]], ALU.pow)

        with ExitStack() as c1:
            def sb1(name, shape, dt=F32):
                return c1.enter_context(nc.sbuf_tensor(name, shape, dt))
            lora_a = sb1("lora_a", [RANK, 4, E]); lora_b = sb1("lora_b", [RANK, 4, E])
            with nc.Block() as block:
                @block.sync
                def _(sp):
                    for n, (w, wt, a, bT) in enumerate(weights):
                        sp.dma_start(w[:, :, :], wt.rearrange("(c p) e -> p c e", p=P)).then_inc(s_w, 16)
                        sp.dma_start(lora_a[:, n, :], a).then_inc(s_w, 16)
                        sp.dma_start(lora_b[:, n, :], bT).then_inc(s_w, 16)
                    for dst, src in ((b_q, bq_), (b_k, bk_), (lnw, ln_w), (lnb, ln_b), (gam, gamma)):
                        sp.dma_start(dst[:, :], src.rearrange("(c p) -> p c", p=P),
                                     allow_slow_non_contiguous=True).then_inc(s_w, 16)
                    for dst, src in ((b_v, bv_), (b_o, bo_)):
                        sp.dma_start(dst[:, :], src.rearrange("(a e) -> a e", a=1).broadcast_to([P, E])).then_inc(s_w, 16)
                    sp.dma_start(rt[:, 0, :], rt_q.broadcast_to([P, E])).then_inc(s_w, 16)
                    sp.dma_start(rt[:, 1, :], rt_kv.broadcast_to([P, E])).then_inc(s_w, 16)

                @block.gpsimd
                def _(pool):
                    nc.gpsimd.memset(half[:, :], -0.5).then_inc(s_init, 1)
                    nc.gpsimd.memset(ident[:, :], 0.0).then_inc(s_ident, 1)
                    pool.wait_ge(s_ident, 1)
                    nc.gpsimd.affine_select(out=ident[:, :], in_=ident[:, :], compare_op=ALU.not_equal, fill=1.0,
                                            base=0, pattern=[[-1, P]], channel_multiplier=1).then_inc(s_ident, 1)

                @block.tensor
                def _(pe):
                    pe.wait_ge(s_w, 16 * 21)
                    for n in range(4):
                        for c in range(C):
                            nc.tensor.matmul(PS[:, n, c * E:(c + 1) * E], lora_a[:, n, c * P:(c + 1) * P],
                                             lora_b[:, n, :], start=True, stop=True).then_inc(s_lora, 1)

                @block.vector
                def _(dve):
                    for n, (w, _, _, _) in enumerate(weights):
                        dve.wait_ge(s_lora, C * (n + 1))
                        nc.vector.scalar_tensor_tensor(
                            out=w[:, :, :], in0=PS[:, n, :].rearrange("p (c e) -> p c e", c=C), scalar=LORA,
                            in1=w[:, :, :], op0=ALU.mult, op1=ALU.add).then_inc(s_lora_used, 1)
                    dve.wait_ge(s_lora_used, 4)
                    nc.vector.tensor_scalar(b_q[:, :], b_q[:, :], D1 ** -0.5, None, ALU.mult).then_inc(s_ready, 1)
                    dve.wait_ge(s_ready, 1)

        with ExitStack() as c1:
            def sb1(name, shape, dt=F32):
                return c1.enter_context(nc.sbuf_tensor(name, shape, dt))
            xT_s = sb1("xT_s", [P, C, S])
            x_s = sb1("x_s", [P, T, E])
            qk32 = sb1("qk32", [P, 2 * C, S])
            rest = sb1("rest", [P, 2 * C, S])
            parts = sb1("parts", [P, 2, 3, C, S], BF16)
            qs = sb1("qs", [DEEP + SHIFT, H1, S], BF16)
            ks = sb1("ks", [DEEP + SHIFT, H1, S], BF16)
            vx = sb1("vx", [P, T, H1, W1H])
            nmax = sb1("nmax", [P, H1, T])
            shift = sb1("shift", [H1 * T, SHIFT, P], BF16)
            shift_r = sb1("shift_r", [H1 * T, P])
            probs = sb1("probs", [P, 4, 2, S])
            oT = sb1("oT", [P, G1, S])
            rec = sb1("rec", [P, T, H1])
            an = sb1("an", [P, T, E])
            aT = sb1("aT", [P, C, S])
            y = sb1("y", [P, T, E])
            stats = sb1("stats", [P, T, 6]); mv = sb1("mv", [P, T, 2])
            sc = sb1("sc", [P, 8, T])
            x1 = sb1("x1", [P, T, E])
            xn = sb1("xn", [P, T, E])
            junk = sb1("junk", [P, 2, E])
            rs = sb1("rs", [P, 2, T]); rsT = sb1("rsT", [2 * T, P])
            xlT = sb1("xlT", [P, C, S])
            wl = sb1("wl", [P, C, 3 * IN2]); wlo = sb1("wlo", [P, M2, E])
            qkl = sb1("qkl", [P, 2 * M2, S])
            vl = sb1("vl", [P, T, H2, W2H]); vodd = sb1("vodd", [WIN, T, H2, W2H])
            nml = sb1("nml", [P, H2, T])
            pl = sb1("pl", [P, 2, T, 3 * WIN])
            pTl = sb1("pTl", [P, 2, T, 2 * P])
            recl = sb1("recl", [P, H2, T])
            al, alT = qk32, rest
            z = sb1("z", [P, T, E])

            with nc.Block() as block:
                @block.sync
                def _(sp):
                    sp.dma_start(wl[:, :, 0:2 * IN2], l_qk.rearrange("(c p) e -> p c e", p=P)).then_inc(s_w, 16)
                    sp.dma_start(wl[:, :, 2 * IN2:], l_v.rearrange("(c p) e -> p c e", p=P)).then_inc(s_w, 16)
                    sp.dma_start(wlo[:, :, :], l_out.rearrange("(c p) e -> p c e", p=P)).then_inc(s_w, 16)
                    sp.wait_ge(s_w, 16 * 24)

                @block.vector
                def _(dve):
                    nc.vector.memset(vx[:, :, :, :], 0.0).then_inc(s_init, 1)
                    dve.wait_ge(s_init, 2)
                    nc.vector.memset(vx[:, :, :, D1:D1 + 1], 1.0).then_inc(s_init, 1)
                    nc.vector.memset(vl[:, :, :, D2:W2H], 1.0).then_inc(s_init, 1)
                    nc.vector.memset(ks[DEEP:DEEP + SHIFT, :, :], 1.0).then_inc(s_init, 1)
                    dve.wait_ge(s_init, 5)

            with nc.Fori(0, NB) as i:
                with nc.Block() as block:
                    @block.sync
                    def _(sp):
                        sp.dma_start(xT_s[:, :, :], xT[bass.ds(i, 1), :, :].rearrange("a (c p) s -> p (a c) s", p=P)).then_inc(s_xT, 16)
                        sp.dma_start(x_s[:, :, :], x[bass.ds(i, 1), :, :].rearrange("a (t p) e -> p (a t) e", p=P)).then_inc(s_x, 16)
                        for n in range(2):
                            sp.wait_ge(s_split, n + 1)
                            for m in range(3):
                                sp.dma_start(parts_d[n, m, :, :].rearrange("(c p) s -> p c s", p=P),
                                             parts[:, n, m, :, :]).then_inc(s_parts[n], 16)
                        for n, (dst, which) in enumerate(((qs, Q_PARTS), (ks, K_PARTS))):
                            sp.wait_ge(s_parts[n], 48)
                            for j, m in enumerate(which):
                                sp.dma_start(dst[16 * j:16 * j + 16, :, :],
                                             parts_d[n, m, :, :].rearrange("(h d) s -> d h s", d=D1)).then_inc(s_stack, 16)
                        for m in range(SHIFT):
                            sp.wait_ge(s_shift, m + 1)
                            sp.dma_start(qs[DEEP + m:DEEP + m + 1, :, :].rearrange("a h (t s) -> a (h t) s", t=T),
                                         shift[:, m, :]).then_inc(s_shift_in, 16)
                        sp.wait_ge(s_xn, 2 * T)
                        sp.dma_start(norm_d[bass.ds(i, 1), :, :].rearrange("a p e -> (a p) e"),
                                     an[:, :, :].rearrange("p t e -> p (t e)")).then_inc(s_norm_out, 16)
                        sp.wait_ge(s_rts, 1)
                        sp.dma_start(route_d[bass.ds(i, 1), :, :].rearrange("a r s -> (a r) s"), rsT[:, :]).then_inc(s_route_out, 16)
                        sp.wait_ge(s_lpd, 6)
                        sp.dma_start(vodd[:, :, :, :], vl[WIN:P, :, :, :]).then_inc(s_vodd, 16)
                        sp.wait_ge(s_z, 1)
                        sp.dma_start(light_d[bass.ds(i, 1), :, :].rearrange("a p e -> (a p) e"),
                                     z[:, :, :].rearrange("p t e -> p (t e)")).then_inc(s_z_out, 16)
                        sp.wait_ge(s_norm_out, 16)
                        sp.wait_ge(s_route_out, 16)
                        sp.wait_ge(s_z_out, 16)

                    @block.gpsimd
                    def _(pool):
                        chain = [0]

                        def link(ins):
                            chain[0] += 1
                            ins.then_inc(s_pool, 1)
                            pool.wait_ge(s_pool, chain[0])

                        for n in range(2):
                            pool.wait_ge(s_qk32, 2 * n + 2)
                            f = qk32[:, C * n:C * n + C, :]
                            r = rest[:, C * n:C * n + C, :]
                            link(nc.gpsimd.tensor_copy(parts[:, n, 0, :, :], f))
                            link(nc.gpsimd.tensor_tensor(r, f, parts[:, n, 0, :, :], ALU.subtract))
                            link(nc.gpsimd.tensor_copy(parts[:, n, 1, :, :], r))
                            nc.gpsimd.tensor_tensor(parts[:, n, 2, :, :], r, parts[:, n, 1, :, :],
                                                    ALU.subtract).then_inc(s_split, 1)
                        pool.wait_ge(s_x, 16)
                        nc.gpsimd.tensor_tensor(x_s[:, :, :], x_s[:, :, :],
                                                b_o[:, :].rearrange("p (a e) -> p a e", a=1).broadcast_to([P, T, E]),
                                                ALU.add).then_inc(s_xb, 1)
                        pool.wait_ge(s_var, 1)
                        v = mv[:, :, 1]
                        link(nc.gpsimd.tensor_scalar(sc[:, 0, :], v, EPS_LN, None, ALU.add))
                        link(pool_pow(sc[:, 1, :], sc[:, 0, :]))
                        pool.sem_inc(s_rstd, 1)
                        link(nc.gpsimd.tensor_tensor(sc[:, 2, :], sc[:, 1, :], sc[:, 1, :], ALU.mult))
                        link(nc.gpsimd.tensor_tensor(sc[:, 3, :], sc[:, 2, :], v, ALU.mult))
                        link(nc.gpsimd.tensor_scalar(sc[:, 4, :], sc[:, 3, :], EPS_LN, None, ALU.add))
                        link(pool_pow(sc[:, 5, :], sc[:, 4, :]))
                        link(nc.gpsimd.tensor_scalar(sc[:, 6, :], sc[:, 3, :], 1e-24 / E, None, ALU.max))
                        link(pool_pow(sc[:, 7, :], sc[:, 6, :]))
                        pool.wait_ge(s_x1, T)
                        for t in range(T):
                            nc.gpsimd.tensor_scalar(xn[:, t, :], x1[:, t, :], sc[:, 5, t:t + 1], None, ALU.mult).then_inc(s_xn, 1)
                        for t in range(T):
                            nc.gpsimd.tensor_scalar(an[:, t, :], x1[:, t, :], sc[:, 7, t:t + 1], None, ALU.mult).then_inc(s_xn, 1)

                    @block.scalar
                    def _(act):
                        for n in range(4):
                            act.wait_ge(s_qk, n + 1)
                            c = n % C
                            nc.scalar.activation(qk32[:, n, :], PS[:, n, :], ACT.Identity,
                                                 bias=(b_q, b_k)[n // C][:, c:c + 1],
                                                 scale=D1 ** -0.5 if n < C else 1.0).then_inc(s_qk32, 1)
                        for g in range(2 * H1):
                            act.wait_ge(s_s2, 2 * g + 2)
                            if g >= 4:
                                act.wait_ge(s_pv, (g - 4) // 2 + 1)
                            b0 = 2 * (g % 3)
                            nc.scalar.activation(probs[:, g % 4, :, :], PS[:, b0:b0 + 2, :], ACT.Exp).then_inc(s_p, 1)
                            if g % 8 == 7:
                                gg = g // 8
                                act.wait_ge(s_pv, 4 * gg + 4)
                                nc.scalar.activation(oT[:, gg, :], PS[:, 6 + gg % 2, :], ACT.Copy).then_inc(s_ot, 1)
                        for c in range(C):
                            act.wait_ge(s_aT, T * (c + 1))
                            nc.scalar.activation(aT[:, c, :], PS[:, 4 + c, :], ACT.Copy).then_inc(s_aTs, 1)
                        act.wait_ge(s_rtT, 1)
                        nc.scalar.activation(rsT[:, :], PS[0:2 * T, 0, 0:P], ACT.Copy).then_inc(s_rts, 1)
                        for c in range(C):
                            act.wait_ge(s_xlT, T * (c + 1))
                            nc.scalar.activation(xlT[:, c, :], PS[:, 4 + c, :], ACT.Identity,
                                                 bias=lnb[:, c:c + 1], scale=lnw[:, c:c + 1]).then_inc(s_xl, 1)
                        for n in range(0, 2 * M2, 2):
                            act.wait_ge(s_lp, n + 1)
                            nc.scalar.activation(qkl[:, n, :], PS[:, n % 8, :], ACT.Copy,
                                                 scale=D2 ** -0.5 if n < M2 else 1.0).then_inc(s_lpa, 1)
                        for t in range(0, T, 2):
                            act.wait_ge(s_lp, 8 + t + 1)
                            nc.scalar.activation(vl[:, t, :, 0:D2], PS[:, t, :].rearrange("p (h d) -> p h d", d=D2),
                                                 ACT.Copy).then_inc(s_lpa, 1)
                        for h in range(H2):
                            act.wait_ge(s_lmax, h + 1)
                            if h >= 2:
                                act.wait_ge(s_lpT, h - 1)
                            b0 = 2 * (h % 2)
                            for j in range(T):
                                nc.scalar.activation(pl[:, h % 2, j, :], PS[:, b0 + j // 2, 256 * (j % 2):256 * (j % 2) + 3 * WIN],
                                                     ACT.Exp, bias=nml[:, h, j:j + 1]).then_inc(s_lp_e, 1)
                        for m in range(M2):
                            act.wait_ge(s_loT, T * (m + 1))
                            nc.scalar.activation(alT[:, m, :], PS[:, m, :], ACT.Copy).then_inc(s_loTs, 1)

                    @block.vector
                    def _(dve):
                        chain = [0]

                        def link(ins):
                            chain[0] += 1
                            ins.then_inc(s_dve, 1)
                            dve.wait_ge(s_dve, chain[0])

                        dve.wait_ge(s_v1, T)
                        for t in range(T):
                            nc.vector.tensor_tensor(
                                vx[:, t, :, 0:D1],
                                PS[:, 4 + t // 2, E * (t % 2):E * (t % 2) + E].rearrange("p (h d) -> p h d", d=D1),
                                b_v[:, :].rearrange("p (h d) -> p h d", d=D1), ALU.add).then_inc(s_vx, 1)
                        for g in range(2 * H1):
                            dve.wait_ge(s_s1, 2 * g + 2)
                            b0 = 2 * (g % 3)
                            nc.vector.reduce_max(nmax[:, g // 2, 2 * (g % 2):2 * (g % 2) + 2], PS[:, b0:b0 + 2, :],
                                                 AX.X, negate=True).then_inc(s_max, 1)
                        dve.wait_ge(s_maxT, 1)
                        mT = PS[0:H1 * T, 6, 0:P]
                        nc.vector.tensor_copy(shift[:, 0, :], mT).then_inc(s_shift, 1)
                        dve.wait_ge(s_shift, 1)
                        link(nc.vector.tensor_tensor(shift_r[:, :], mT, shift[:, 0, :], ALU.subtract))
                        nc.vector.tensor_copy(shift[:, 1, :], shift_r[:, :]).then_inc(s_shift, 1)
                        dve.wait_ge(s_shift, 2)
                        nc.vector.tensor_tensor(shift[:, 2, :], shift_r[:, :], shift[:, 1, :], ALU.subtract).then_inc(s_shift, 1)
                        for t in range(T):
                            dve.wait_ge(s_tok, G1 * (t + 1))
                            o = PS[:, t, :].rearrange("p (h d) -> p h d", d=W1H)
                            link(nc.vector.reciprocal(rec[:, t, :], o[:, :, D1]))
                            nc.vector.tensor_tensor(
                                an[:, t, :].rearrange("p (h d) -> p h d", d=D1), o[:, :, 0:D1],
                                rec[:, t, :].rearrange("p (h a) -> p h a", a=1).broadcast_to([P, H1, D1]),
                                ALU.mult).then_inc(s_an, 1)
                        dve.wait_ge(s_y, T)
                        dve.wait_ge(s_xb, 1)
                        link(nc.vector.tensor_tensor(y[:, :, :], PS[:, 6:8, :].rearrange("p b (t e) -> p (b t) e", e=E),
                                                     x_s[:, :, :], ALU.add))
                        for t in range(T):
                            ins = nc.vector.bn_stats(stats[:, t, :], y[:, t, :])
                        link(ins)
                        for t in range(T):
                            ins = nc.vector.bn_aggr(mv[:, t, :], stats[:, t, :])
                        ins.then_inc(s_var, 1)
                        dve.wait_ge(s_rstd, 1)
                        for t in range(T):
                            if t == 0:
                                dve.wait_ge(s_var, 1)
                            nc.vector.tensor_scalar(x1[:, t, :], y[:, t, :], mv[:, t, 0:1], sc[:, 1, t:t + 1],
                                                    ALU.subtract, ALU.mult).then_inc(s_x1, 1)
                        dve.wait_ge(s_x1, T)
                        for r in range(2):
                            for t in range(T):
                                link(nc.vector.tensor_tensor_reduce(
                                    out=junk[:, t % 2, :], in0=x1[:, t, :], in1=rt[:, r, :], scale=1.0, scalar=0.0,
                                    op0=ALU.mult, op1=ALU.add, accum_out=rs[:, r, t:t + 1]))
                        dve.sem_inc(s_rt, 1)
                        for n in range(1, 2 * M2, 2):
                            dve.wait_ge(s_lp, n + 1)
                            nc.vector.tensor_scalar(qkl[:, n, :], PS[:, n % 8, :], D2 ** -0.5 if n < M2 else 1.0, None,
                                                    ALU.mult).then_inc(s_lpd, 1)
                        for t in range(1, T, 2):
                            dve.wait_ge(s_lp, 8 + t + 1)
                            if t == 1:
                                dve.wait_ge(s_lpa, 6)
                            nc.vector.tensor_copy(vl[:, t, :, 0:D2],
                                                  PS[:, t, :].rearrange("p (h d) -> p h d", d=D2)).then_inc(s_lpd, 1)

                        def local_max(h):
                            dve.wait_ge(s_ls, h + 1)
                            b0 = 2 * (h % 2)
                            nc.vector.reduce_max(nml[:, h, :],
                                                 PS[:, b0:b0 + 2, :].rearrange("p b (j c) -> p (b j) c", j=2)[:, :, 0:3 * WIN],
                                                 AX.X, negate=True).then_inc(s_lmax, 1)

                        def local_out(h):
                            dve.wait_ge(s_lo, h + 1)
                            o = PS[:, 6 + h % 2, 0:T * W2H].rearrange("p (t d) -> p t d", d=W2H)
                            link(nc.vector.reciprocal(recl[:, h, :], o[:, :, D2]))
                            nc.vector.tensor_tensor(
                                al[:, :, h * D2:(h + 1) * D2], o[:, :, 0:D2],
                                recl[:, h, :].rearrange("p (t a) -> p t a", a=1).broadcast_to([P, T, D2]),
                                ALU.mult).then_inc(s_lon, 1)

                        local_max(0)
                        for h in range(H2):
                            if h + 1 < H2:
                                local_max(h + 1)
                            dve.wait_ge(s_lpT, h + 1)
                            if h >= 2:
                                dve.wait_ge(s_lo, h - 1)
                            nc.vector.tensor_copy(pTl[:, h % 2, :, :].rearrange("p t c -> p (t c)"),
                                                  PS[:, 4:6, :].rearrange("p b c -> p (b c)")).then_inc(s_lpTs, 1)
                            if h >= 1:
                                local_out(h - 1)
                        local_out(H2 - 1)
                        dve.wait_ge(s_lz, T)
                        nc.vector.tensor_tensor(z[:, :, :], PS[:, 4:6, :].rearrange("p b (t e) -> p (b t) e", e=E),
                                                x1[:, :, :], ALU.add).then_inc(s_z, 1)

                    @block.tensor
                    def _(pe):
                        pe.wait_ge(s_xT, 16)
                        for n in range(4):
                            w = (w_q, w_k)[n // C]
                            m = n % C
                            for c in range(C):
                                ins = nc.tensor.matmul(PS[:, n, :], w[:, c, m * P:(m + 1) * P], xT_s[:, c, :],
                                                       start=c == 0, stop=c == C - 1)
                            ins.then_inc(s_qk, 1)
                        for t in range(T):
                            for c in range(C):
                                ins = nc.tensor.matmul(PS[:, 4 + t // 2, E * (t % 2):E * (t % 2) + E],
                                                       xT_s[:, c, t * P:(t + 1) * P], w_v[:, c, :],
                                                       start=c == 0, stop=c == C - 1)
                            ins.then_inc(s_v1, 1)
                        pe.wait_ge(s_stack, 192)
                        pe.wait_ge(s_vx, T)
                        for n in range(H1 * T):
                            g = n // 2
                            h, t = n // T, n % T
                            if n % 2 == 0 and g >= 3:
                                pe.wait_ge(s_max, g - 2)
                            nc.tensor.matmul(PS[:, 2 * (g % 3) + n % 2, :], qs[0:DEEP, h, t * P:(t + 1) * P],
                                             ks[0:DEEP, h, :], start=True, stop=True).then_inc(s_s1, 1)
                        pe.wait_ge(s_max, 32)
                        nc.tensor.transpose(PS[0:H1 * T, 6, 0:P], nmax[:, :, :].rearrange("p h t -> p (h t)"),
                                            ident[:, :]).then_inc(s_maxT, 1)
                        pe.wait_ge(s_shift_in, 48)

                        def scores(g):
                            h = g // 2
                            if g >= 3:
                                pe.wait_ge(s_p, g - 2)
                            for k in range(2):
                                t = 2 * (g % 2) + k
                                nc.tensor.matmul(PS[:, 2 * (g % 3) + k, :], ks[:, h, t * P:(t + 1) * P], qs[:, h, :],
                                                 start=True, stop=True).then_inc(s_s2, 1)

                        def values(g):
                            h = g // 2
                            hg, r = h // 4, 32 * (h % 4)
                            pe.wait_ge(s_p, g + 1)
                            if g % 8 == 0 and hg >= 2:
                                pe.wait_ge(s_ot, hg - 1)
                            for k in range(2):
                                t = 2 * (g % 2) + k
                                ins = nc.tensor.matmul(PS[r:r + 32, 6 + hg % 2, :], vx[:, t, h, :], probs[:, g % 4, k, :],
                                                       start=t == 0, stop=t == T - 1)
                            if g % 2 == 1:
                                ins.then_inc(s_pv, 1)

                        scores(0)
                        scores(1)
                        for g in range(2 * H1):
                            if g + 2 < 2 * H1:
                                scores(g + 2)
                            values(g)
                        pe.wait_ge(s_ot, G1)
                        for t in range(T):
                            for g in range(G1):
                                nc.tensor.transpose(PS[:, t, g * P:(g + 1) * P], oT[:, g, t * P:(t + 1) * P],
                                                    ident[:, :]).then_inc(s_tok, 1)
                        for c in range(C):
                            for t in range(T):
                                if c == 0:
                                    pe.wait_ge(s_an, t + 1)
                                nc.tensor.transpose(PS[:, 4 + c, t * P:(t + 1) * P], an[:, t, c * P:(c + 1) * P],
                                                    ident[:, :]).then_inc(s_aT, 1)
                        pe.wait_ge(s_aTs, C)
                        for t in range(T):
                            for c in range(C):
                                ins = nc.tensor.matmul(PS[:, 6 + t // 2, E * (t % 2):E * (t % 2) + E],
                                                       aT[:, c, t * P:(t + 1) * P], w_o[:, c, :],
                                                       start=c == 0, stop=c == C - 1)
                            ins.then_inc(s_y, 1)
                        pe.wait_ge(s_rt, 1)
                        nc.tensor.transpose(PS[0:2 * T, 0, 0:P], rs[:, :, :].rearrange("p r t -> p (r t)"),
                                            ident[:, :]).then_inc(s_rtT, 1)
                        for c in range(C):
                            for t in range(T):
                                if c == 0:
                                    pe.wait_ge(s_xn, t + 1)
                                nc.tensor.transpose(PS[:, 4 + c, t * P:(t + 1) * P], xn[:, t, c * P:(c + 1) * P],
                                                    ident[:, :]).then_inc(s_xlT, 1)
                        pe.wait_ge(s_xl, C)
                        pe.wait_ge(s_rts, 1)
                        for n in range(2 * M2):
                            for c in range(C):
                                ins = nc.tensor.matmul(PS[:, n, :], wl[:, c, n * P:(n + 1) * P], xlT[:, c, :],
                                                       start=c == 0, stop=c == C - 1)
                            ins.then_inc(s_lp, 1)
                        for t in range(T):
                            if t % 2 == 0:
                                pe.wait_ge(s_lpa, t // 2 + 1)
                            else:
                                pe.wait_ge(s_lpd, t // 2 + 1)
                            for c in range(C):
                                ins = nc.tensor.matmul(PS[:, t, :], xlT[:, c, t * P:(t + 1) * P], wl[:, c, 2 * IN2:],
                                                       start=c == 0, stop=c == C - 1)
                            ins.then_inc(s_lp, 1)
                        pe.wait_ge(s_lpa, 6)
                        pe.wait_ge(s_lpd, 6)

                        def window_scores(h):
                            r, m = D2 * (h % 2), h // 2
                            q, k = qkl[r:r + D2, m, :], qkl[r:r + D2, M2 + m, :]
                            if h >= 2:
                                pe.wait_ge(s_lp_e, T * (h - 1))
                            for j in range(T):
                                o = PS[:, 2 * (h % 2) + j // 2, 256 * (j % 2):256 * (j % 2) + 3 * WIN]
                                before, after = max(2 * j - 1, 0), min(2 * j + 2, 2 * T - 1)
                                nc.tensor.matmul(o[0:WIN, 0:WIN], q[:, 2 * j * WIN:(2 * j + 1) * WIN],
                                                 k[:, before * WIN:(before + 1) * WIN], start=True, stop=True)
                                nc.tensor.matmul(o[WIN:P, 0:WIN], q[:, (2 * j + 1) * WIN:(2 * j + 2) * WIN],
                                                 k[:, after * WIN:(after + 1) * WIN], start=True, stop=True)
                                ins = nc.tensor.matmul(o[:, WIN:3 * WIN], q[:, j * P:(j + 1) * P], k[:, j * P:(j + 1) * P],
                                                       start=True, stop=True)
                            ins.then_inc(s_ls, 1)

                        def window_transposes(h):
                            pe.wait_ge(s_lp_e, T * (h + 1))
                            if h >= 1:
                                pe.wait_ge(s_lpTs, h)
                            for j in range(T):
                                o = PS[:, 4 + j // 2, 256 * (j % 2):256 * (j % 2) + 256]
                                nc.tensor.transpose(o[:, 0:P], pl[:, h % 2, j, WIN:3 * WIN], ident[:, :])
                                ins = nc.tensor.transpose(o[0:WIN, P:2 * P], pl[:, h % 2, j, 0:WIN], ident[:, :])
                            ins.then_inc(s_lpT, 1)

                        def window_values(h):
                            pe.wait_ge(s_lpTs, h + 1)
                            if h == 0:
                                pe.wait_ge(s_vodd, 16)
                            if h >= 2:
                                pe.wait_ge(s_lon, h - 1)
                            for j in range(T):
                                o = PS[:, 6 + h % 2, j * W2H:(j + 1) * W2H]
                                pT = pTl[:, h % 2, j, :]
                                ins = nc.tensor.matmul(o, pT[:, 0:P], vl[:, j, h, :], start=True, stop=False,
                                                       skip_group_check=True)
                                if j > 0:
                                    ins = nc.tensor.matmul(o[0:WIN, :], pT[0:WIN, P:P + WIN], vodd[:, j - 1, h, :],
                                                           start=False, stop=True, skip_group_check=True)
                                if j < T - 1:
                                    ins = nc.tensor.matmul(o[WIN:P, :], pT[0:WIN, P + WIN:2 * P], vl[0:WIN, j + 1, h, :],
                                                           start=False, stop=True, skip_group_check=True)
                            ins.then_inc(s_lo, 1)

                        window_scores(0)
                        for h in range(H2):
                            if h + 1 < H2:
                                window_scores(h + 1)
                            window_transposes(h)
                            window_values(h)
                        for m in range(M2):
                            for t in range(T):
                                if m == 0 and t == 0:
                                    pe.wait_ge(s_lon, H2)
                                nc.tensor.transpose(PS[:, m, t * P:(t + 1) * P], al[:, t, m * P:(m + 1) * P],
                                                    ident[:, :]).then_inc(s_loT, 1)
                        pe.wait_ge(s_loTs, M2)
                        for t in range(T):
                            for m in range(M2):
                                ins = nc.tensor.matmul(PS[:, 4 + t // 2, E * (t % 2):E * (t % 2) + E],
                                                       alT[:, m, t * P:(t + 1) * P], wlo[:, m, :],
                                                       start=m == 0, stop=m == M2 - 1)
                            ins.then_inc(s_lz, 1)

                nc.all_engine_barrier(sems_to_clear=range(step_sems[0].num, step_sems[-1].num + 1))

        slotT = sb("slotT", [P, T, 2 * NB]); scoreT = sb("scoreT", [P, T, 2 * NB])
        r_in = sem("r_in"); r_init = sem("r_init"); r_t = sem("r_t"); r_e = sem("r_e"); r_l = sem("r_l"); r_a = sem("r_a")
        r_dve = sem("r_dve"); r_score = sem("r_score"); r_T = sem("r_T"); r_end = sem("r_end"); r_slot = sem("r_slot")
        r_top = sem("r_top"); r_key = sem("r_key")
        R = 2 * NB
        with ExitStack() as c2:
            def sb2(name, shape, dt=F32):
                return c2.enter_context(nc.sbuf_tensor(name, shape, dt))
            s_r = sb2("s_r", [R, S]); low = sb2("low", [R, S]); e_r = sb2("e_r", [R, S])
            one = sb2("one", [R, S]); key = sb2("key", [R, S]); work = sb2("work", [R, 2, S])
            gt = sb2("gt", [R, S]); eq = sb2("eq", [R, S]); cum = sb2("cum", [R, S]); mask = sb2("mask", [R, S])
            slot = sb2("slot", [R, S]); score = sb2("score", [R, S]); inv = sb2("inv", [R, S])
            top = sb2("top", [R, 2, 8])
            logk = sb2("logk", [R, 1]); room = sb2("room", [R, 1]); kk = sb2("kk", [R, 1]); thr = sb2("thr", [R, 1])
            smax = sb2("smax", [R, 1]); na = sb2("na", [R, 1]); nm = sb2("nm", [R, 1]); se = sb2("se", [R, 1])
            ln = sb2("ln", [R, 1]); cnt = sb2("cnt", [R, 1])
            with nc.Block() as block:
                @block.sync
                def _(sp):
                    for r in range(2):
                        sp.dma_start(s_r[r * NB:(r + 1) * NB, :],
                                     route_d[:, r * T:(r + 1) * T, :].rearrange("b t s -> b (t s)")).then_inc(r_in, 16)
                    sp.wait_ge(r_slot, 1)
                    sp.dma_start(slot_d, slot[:, :]).then_inc(r_end, 16)
                    sp.wait_ge(r_end, 16)

                @block.scalar
                def _(act):
                    with act.Fori(0, ITERS - 1) as i:
                        act.wait_ge(r_t, i * 2 + 2)
                        nc.scalar.activation(e_r[:, :], low[:, :], ACT.Exp, bias=nm[:, 0:1], accum_out=se[:, 0:1]).then_inc(r_e, 1)
                        act.wait_ge(r_e, i + 1)
                        nc.scalar.activation(ln[:, :], se[:, :], ACT.Ln).then_inc(r_l, 1)
                    act.wait_ge(r_key, 1)
                    nc.scalar.activation(score[:, :], low[:, :], ACT.Exp).then_inc(r_score, 1)

                @block.vector
                def _(dve):
                    n_dve = [0]

                    def link(ins):
                        n_dve[0] += 1
                        ins.then_inc(r_dve, 1)
                        dve.wait_ge(r_dve, n_dve[0])

                    for r, k in ((0, NQ), (NB, NKV)):
                        nc.vector.memset(logk[r:r + NB, :], math.log(min(k * 9.0 / 8.0, S))).then_inc(r_init, 1)
                        nc.vector.memset(kk[r:r + NB, :], float(k)).then_inc(r_init, 1)
                        nc.vector.memset(na[r:r + NB, :], math.log(S) - math.log(min(k * 9.0 / 8.0, S))).then_inc(r_init, 1)
                    nc.vector.memset(one[:, :], 1.0).then_inc(r_init, 1)
                    dve.wait_ge(r_init, 7)
                    dve.wait_ge(r_in, 32)
                    link(nc.vector.reduce_max(smax[:, :], s_r[:, :], AX.X))
                    with dve.Fori(0, ITERS - 1) as i:
                        nc.vector.tensor_scalar(low[:, :], s_r[:, :], na[:, 0:1], None, ALU.min).then_inc(r_t, 1)
                        nc.vector.tensor_scalar(nm[:, :], smax[:, :], na[:, 0:1], -1.0, ALU.min, ALU.mult).then_inc(r_t, 1)
                        dve.wait_ge(r_l, i + 1)
                        nc.vector.tensor_scalar(na[:, :], ln[:, :], nm[:, 0:1], logk[:, 0:1], ALU.subtract,
                                                ALU.subtract).then_inc(r_a, 1)
                        dve.wait_ge(r_a, i + 1)
                    link(nc.vector.tensor_scalar(low[:, :], s_r[:, :], na[:, 0:1], 0.0, ALU.subtract, ALU.min))
                    dve.sem_inc(r_key, 1)
                    link(nc.vector.scalar_tensor_tensor(out=key[:, :], in0=low[:, :], scalar=-2.98e-8, in1=low[:, :],
                                                        op0=ALU.is_lt, op1=ALU.mult))
                    link(nc.vector.tensor_scalar(work[:, 0, :], key[:, :], LOWEST, None, ALU.max))
                    link(nc.vector.tensor_copy(key[:, :], work[:, 0, :]))
                    for half_, rows in enumerate((slice(0, NB), slice(NB, R))):
                        for i in range(NQ // 16):
                            for n in range(2):
                                done = (half_ * (NQ // 16) + i) * 4 + 2 * n
                                nc.vector.max(top[:, n, :], work[:, n, :]).then_inc(r_top, 1)
                                dve.wait_ge(r_top, done + 1)
                                nc.vector.match_replace(work[:, 1 - n, :], top[:, n, :], work[:, n, :], NEG).then_inc(r_top, 1)
                                dve.wait_ge(r_top, done + 2)
                        link(nc.vector.tensor_copy(thr[rows, :], top[rows, 1, 7:8]))
                    nc.vector.tensor_scalar(gt[:, :], key[:, :], thr[:, 0:1], None, ALU.is_gt)
                    link(nc.vector.tensor_scalar(eq[:, :], key[:, :], thr[:, 0:1], None, ALU.is_equal))
                    link(nc.vector.reduce_sum(cnt[:, :], gt[:, :], AX.X))
                    link(nc.vector.tensor_tensor_scan(cum[:, :], one[:, :], eq[:, :], 0.0, ALU.mult, ALU.add))
                    link(nc.vector.tensor_tensor(room[:, :], kk[:, :], cnt[:, :], ALU.subtract))
                    link(nc.vector.scalar_tensor_tensor(out=mask[:, :], in0=cum[:, :], scalar=room[:, 0:1], in1=eq[:, :],
                                                        op0=ALU.is_le, op1=ALU.mult))
                    link(nc.vector.tensor_tensor(eq[:, :], mask[:, :], gt[:, :], ALU.add))
                    link(nc.vector.tensor_tensor_scan(cum[:, :], one[:, :], eq[:, :], 0.0, ALU.mult, ALU.add))
                    link(nc.vector.tensor_tensor(gt[:, :], cum[:, :], eq[:, :], ALU.mult))
                    nc.vector.tensor_scalar(slot[:, :], gt[:, :], -1.0, None, ALU.add).then_inc(r_slot, 1)
                    dve.wait_ge(r_score, 1)
                    link(nc.vector.tensor_scalar(inv[:, :], score[:, :], -1.0, 1.0, ALU.mult, ALU.add))
                    nc.vector.tensor_tensor(work[:, 0, :], inv[:, :], score[:, :], ALU.add).then_inc(r_slot, 1)
                    dve.wait_ge(r_T, 2 * T)
                    nc.vector.tensor_copy(slotT[:, :, :].rearrange("p t r -> p (t r)"), PS[:, 0, 0:T * R])
                    link(nc.vector.tensor_copy(scoreT[:, :, :].rearrange("p t r -> p (t r)"), PS[:, 1, 0:T * R]))

                @block.tensor
                def _(pe):
                    pe.wait_ge(r_slot, 2)
                    for n, src in enumerate((slot[:, :], work[:, 0, :])):
                        for t in range(T):
                            nc.tensor.transpose(PS[:, n, t * R:(t + 1) * R], src[:, t * P:(t + 1) * P],
                                                ident[0:R, 0:R]).then_inc(r_T, 1)

        with ExitStack() as c3:
            def sb3(name, shape, dt=F32):
                return c3.enter_context(nc.sbuf_tensor(name, shape, dt))

            step_sems2 = []

            def sem3(name):
                step_sems2.append(c3.enter_context(nc.semaphore(name)))
                return step_sems2[-1]
            whq = sb3("whq", [P, C, IN2]); whk = sb3("whk", [P, C, IN2]); whv = sb3("whv", [P, C, IN2]); who = sb3("who", [P, M2, E])
            nq_b = sb3("nq_b", [P, E]); nv_b = sb3("nv_b", [P, H2, W2H])
            iota_r = sb3("iota_r", [P, NKV]); iota_c = sb3("iota_c", [P, 1])
            norm = sb3("norm", [P, 2, T, E]); light = sb3("light", [P, 2, T, E]); row = sb3("row", [P, 2, S])
            cols = sb3("cols", [P, T, 2]); scol = sb3("scol", [P, T, 2]); unch = sb3("unch", [P, T])
            oh = sb3("oh", [P, T, NSEL]); ohT = sb3("ohT", [P, S])
            xsT = sb3("xsT", [P, C, NSEL]); skv = sb3("skv", [P, 2])
            qh = sb3("qh", [P, M2, NQ]); kh = sb3("kh", [P, M2, NKV + 1]); vh = sb3("vh", [P, 2, H2, W2H])
            nmh = sb3("nmh", [P, H2]); ph = sb3("ph", [P, 2, NKV + 1]); pTh = sb3("pTh", [P, 2, NKV])
            ou = sb3("ou", [P, H2, W2H]); rech = sb3("rech", [P, H2]); oa = sb3("oa", [P, IN2]); oaT = sb3("oaT", [P, M2, NQ])
            hv = sb3("hv", [P, E]); f1 = sb3("f1", [P, T, E]); f2 = sb3("f2", [P, T, E])
            st2 = sb3("st2", [P, T, 6]); mv2 = sb3("mv2", [P, T, 2]); sc2 = sb3("sc2", [P, 2, T])
            outb = sb3("outb", [P, 2, T, E])
            h_w, h_init = (c3.enter_context(nc.semaphore(n)) for n in ("h_w", "h_init"))
            h_norm, h_light, h_row, h_dve, h_oh = (sem3(n) for n in ("h_norm", "h_light", "h_row", "h_dve", "h_oh"))
            h_ga, h_xs, h_q_, h_qs, h_k_, h_kc, h_v_, h_vs, h_skv, h_skvs = (sem3(n) for n in ("h_ga", "h_xs", "h_q_", "h_qs", "h_k_", "h_kc", "h_v_", "h_vs", "h_skv", "h_skvs"))
            h_s, h_max, h_p, h_pT, h_pTs, h_o, h_ou, h_oa, h_oT, h_oTs, h_hv, h_hvs, h_sc, h_f, h_var, h_rstd, h_y, h_out, h_pool, h_done = (
                sem3(n) for n in ("h_s", "h_max", "h_p", "h_pT", "h_pTs", "h_o", "h_ou", "h_oa", "h_oT", "h_oTs", "h_hv", "h_hvs", "h_sc", "h_f", "h_var", "h_rstd", "h_y", "h_out", "h_pool", "h_done"))
            with nc.Block() as block:
                @block.sync
                def _(sp):
                    for dst, src in ((whq, h_q), (whk, h_k), (whv, h_v), (who, h_out_w)):
                        sp.dma_start(dst[:, :, :], src.rearrange("(c p) e -> p c e", p=P)).then_inc(h_w, 16)
                    sp.dma_start(kh[:, :, NKV:NKV + 1], null_k.rearrange("(m h) (d a) -> (h d) m a", h=2, a=1),
                                 allow_slow_non_contiguous=True).then_inc(h_w, 16)
                    sp.dma_start(nv_b[:, :, 0:D2], null_v.rearrange("(a h) d -> a h d", a=1).broadcast_to([P, H2, D2])).then_inc(h_w, 16)
                    sp.dma_start(nq_b[:, :], null_q.rearrange("(a e) -> a e", a=1).broadcast_to([P, E])).then_inc(h_w, 16)
                    sp.wait_ge(h_w, 16 * 7)

                @block.gpsimd
                def _(pool):
                    nc.gpsimd.iota(iota_r[:, :], [[1, NKV]], base=0, channel_multiplier=0,
                                   allow_small_or_imprecise_dtypes=True).then_inc(h_init, 1)
                    nc.gpsimd.iota(iota_c[:, :], [[1, 1]], base=0, channel_multiplier=1,
                                   allow_small_or_imprecise_dtypes=True).then_inc(h_init, 1)
                    nc.gpsimd.memset(vh[:, :, :, D2:W2H], 1.0).then_inc(h_init, 1)
                    nc.gpsimd.memset(nv_b[:, :, D2:W2H], 1.0).then_inc(h_init, 1)

            with nc.Fori(0, NB) as i:
                with nc.Block() as block:
                    @block.sync
                    def _(sp):
                        sp.dma_start(norm[:, 0, :, :].rearrange("p t e -> p (t e)"), norm_d[bass.ds(i, 1), :, :].rearrange("a p e -> (a p) e")).then_inc(h_norm, 16)
                        sp.dma_start(row[:, 0, :], slot_d[bass.ds(i, 1), :].broadcast_to([P, S])).then_inc(h_row, 16)
                        sp.dma_start(light[:, 0, :, :].rearrange("p t e -> p (t e)"), light_d[bass.ds(i, 1), :, :].rearrange("a p e -> (a p) e")).then_inc(h_light, 16)
                        sp.wait_ge(h_y, T)
                        sp.dma_start(out[bass.ds(i, 1), :, :].rearrange("a (t p) e -> p (a t) e", p=P), outb[:, 0, :, :]).then_inc(h_done, 16)
                        sp.wait_ge(h_done, 16)

                    @block.gpsimd
                    def _(pool):
                        pool.wait_ge(h_var, 1)
                        nc.gpsimd.tensor_scalar(sc2[:, 0, :], mv2[:, :, 1], EPS_LN, None, ALU.add).then_inc(h_pool, 1)
                        pool.wait_ge(h_pool, 1)
                        pool_pow(sc2[:, 1, :], sc2[:, 0, :]).then_inc(h_rstd, 1)

                    @block.scalar
                    def _(act):
                        for c in range(C):
                            act.wait_ge(h_ga, c + 1)
                            nc.scalar.activation(xsT[:, c, :], PS[:, c, 0:NSEL], ACT.Copy, scale=gam[:, c:c + 1]).then_inc(h_xs, 1)
                        act.wait_ge(h_q_, 1)
                        nc.scalar.activation(qh[:, :, :].rearrange("p m s -> p (m s)"), PS[:, 3, :], ACT.Copy, scale=D2 ** -0.5).then_inc(h_qs, 1)
                        act.wait_ge(h_skvs, 1)
                        for s in range(2):
                            act.wait_ge(h_v_, s + 1)
                            nc.scalar.activation(vh[:, s, :, 0:D2], PS[:, 6 + s, :].rearrange("p (h d) -> p h d", d=D2), ACT.Copy,
                                                 scale=skv[:, s:s + 1]).then_inc(h_vs, 1)
                        for h in range(H2):
                            act.wait_ge(h_max, h + 1)
                            if h >= 2:
                                act.wait_ge(h_ou, h - 1)
                            nc.scalar.activation(ph[:, h % 2, :], PS[:, h % 2, 0:NKV + 1], ACT.Exp, bias=nmh[:, h:h + 1]).then_inc(h_p, 1)
                            act.wait_ge(h_pT, h + 1)
                            nc.scalar.activation(pTh[:, h % 2, :], PS[:, 2 + h % 2, 0:NKV], ACT.Copy).then_inc(h_pTs, 1)
                        act.wait_ge(h_oT, 1)
                        nc.scalar.activation(oaT[:, :, :].rearrange("p m s -> p (m s)"), PS[:, 6, :], ACT.Copy).then_inc(h_oTs, 1)
                        act.wait_ge(h_hv, 1)
                        nc.scalar.activation(hv[:, :], PS[:, 7, 0:E], ACT.Copy).then_inc(h_hvs, 1)

                    @block.vector
                    def _(dve):
                        chain = [0]

                        def link(ins):
                            chain[0] += 1
                            ins.then_inc(h_dve, 1)
                            dve.wait_ge(h_dve, chain[0])

                        nc.vector.tensor_copy(cols[:, :, :], slotT[:, :, :].rearrange("p t (r b) -> p t r b", r=2)[:, :, :, bass.ds(i, 1)].rearrange("p t r b -> p t (r b)"))
                        link(nc.vector.tensor_copy(scol[:, :, :], scoreT[:, :, :].rearrange("p t (r b) -> p t r b", r=2)[:, :, :, bass.ds(i, 1)].rearrange("p t r b -> p t (r b)")))
                        for t in range(T):
                            nc.vector.tensor_scalar(oh[:, t, 0:NQ], iota_r[:, 0:NQ], cols[:, t, 0:1], None, ALU.is_equal).then_inc(h_oh, 1)
                            nc.vector.tensor_scalar(oh[:, t, NQ:NSEL], iota_r[:, :], cols[:, t, 1:2], None, ALU.is_equal).then_inc(h_oh, 1)
                        dve.wait_ge(h_row, 16)
                        nc.vector.tensor_scalar(ohT[:, :], row[:, 0, :], iota_c[:, 0:1], None, ALU.is_equal).then_inc(h_oh, 1)
                        link(nc.vector.tensor_scalar(unch[:, :], cols[:, :, 0], 0.0, None, ALU.is_lt))
                        dve.wait_ge(h_skv, 1)
                        nc.vector.tensor_copy(skv[:, :], PS[:, 2, 0:2]).then_inc(h_skvs, 1)
                        dve.wait_ge(h_k_, 1)
                        nc.vector.tensor_copy(kh[:, :, 0:NKV], PS[:, 4:6, :].rearrange("p b (m s) -> p (b m) s", s=NKV)).then_inc(h_kc, 1)

                        def head_max(h):
                            dve.wait_ge(h_s, h + 1)
                            nc.vector.reduce_max(nmh[:, h:h + 1], PS[:, h % 2, 0:NKV + 1], AX.X, negate=True).then_inc(h_max, 1)

                        head_max(0)
                        for h in range(H2):
                            if h + 1 < H2:
                                head_max(h + 1)
                            dve.wait_ge(h_o, h + 1)
                            nc.vector.scalar_tensor_tensor(out=ou[:, h, :], in0=nv_b[:, h, :], scalar=ph[:, h % 2, NKV:NKV + 1],
                                                           in1=PS[:, 4 + h % 2, 0:W2H], op0=ALU.mult, op1=ALU.add).then_inc(h_ou, 1)
                        dve.wait_ge(h_ou, H2)
                        link(nc.vector.reciprocal(rech[:, :], ou[:, :, D2]))
                        nc.vector.tensor_tensor(oa[:, :].rearrange("p (h d) -> p h d", d=D2), ou[:, :, 0:D2],
                                                rech[:, :].rearrange("p (h a) -> p h a", a=1).broadcast_to([P, H2, D2]), ALU.mult).then_inc(h_oa, 1)
                        dve.wait_ge(h_light, 16)
                        for t in range(T):
                            dve.wait_ge(h_sc, 2 * (t // 2) + 2)
                            ins = nc.vector.scalar_tensor_tensor(out=f1[:, t, :], in0=PS[:, 4 + t // 2, E * (t % 2):E * (t % 2) + E],
                                                                 scalar=scol[:, t, 0:1], in1=light[:, 0, t, :], op0=ALU.mult, op1=ALU.add)
                            ins.then_inc(h_f, 1)
                        dve.wait_ge(h_f, T)
                        for t in range(T):
                            ins = nc.vector.scalar_tensor_tensor(out=f2[:, t, :], in0=nq_b[:, :], scalar=unch[:, t:t + 1],
                                                                 in1=f1[:, t, :], op0=ALU.mult, op1=ALU.add)
                        link(ins)
                        for t in range(T):
                            ins = nc.vector.bn_stats(st2[:, t, :], f2[:, t, :])
                        link(ins)
                        for t in range(T):
                            ins = nc.vector.bn_aggr(mv2[:, t, :], st2[:, t, :])
                        link(ins)
                        dve.sem_inc(h_var, 1)
                        dve.wait_ge(h_rstd, 1)
                        for t in range(T):
                            nc.vector.tensor_scalar(outb[:, 0, t, :], f2[:, t, :], mv2[:, t, 0:1], sc2[:, 1, t:t + 1],
                                                    ALU.subtract, ALU.mult).then_inc(h_y, 1)

                    @block.tensor
                    def _(pe):
                        pe.wait_ge(h_norm, 16)
                        pe.wait_ge(h_oh, 9)
                        for s in range(2):
                            for t in range(T):
                                ins = nc.tensor.matmul(PS[:, 2, s:s + 1], oh[:, t, NQ + s * P:NQ + (s + 1) * P], scol[:, t, 1:2],
                                                       start=t == 0, stop=t == T - 1)
                        ins.then_inc(h_skv, 1)
                        for c in range(C):
                            for t in range(T):
                                ins = nc.tensor.matmul(PS[:, c, 0:NSEL], norm[:, 0, t, c * P:(c + 1) * P], oh[:, t, :],
                                                       start=t == 0, stop=t == T - 1)
                            ins.then_inc(h_ga, 1)
                        pe.wait_ge(h_xs, C)
                        for m in range(M2):
                            for c in range(C):
                                ins = nc.tensor.matmul(PS[:, 3, m * NQ:(m + 1) * NQ], whq[:, c, m * P:(m + 1) * P], xsT[:, c, 0:NQ],
                                                       start=c == 0, stop=c == C - 1)
                        ins.then_inc(h_q_, 1)
                        for m in range(M2):
                            for c in range(C):
                                ins = nc.tensor.matmul(PS[:, 4 + m // 2, NKV * (m % 2):NKV * (m % 2) + NKV], whk[:, c, m * P:(m + 1) * P],
                                                       xsT[:, c, NQ:NSEL], start=c == 0, stop=c == C - 1)
                        ins.then_inc(h_k_, 1)
                        for s in range(2):
                            for c in range(C):
                                ins = nc.tensor.matmul(PS[:, 6 + s, :], xsT[:, c, NQ + s * P:NQ + (s + 1) * P], whv[:, c, :],
                                                       start=c == 0, stop=c == C - 1)
                            ins.then_inc(h_v_, 1)
                        pe.wait_ge(h_qs, 1)
                        pe.wait_ge(h_kc, 1)

                        def heavy_scores(h):
                            r, m = D2 * (h % 2), h // 2
                            if h >= 2:
                                pe.wait_ge(h_p, h - 1)
                            nc.tensor.matmul(PS[:, h % 2, 0:NKV + 1], qh[r:r + D2, m, :], kh[r:r + D2, m, :],
                                             start=True, stop=True).then_inc(h_s, 1)

                        heavy_scores(0)
                        for h in range(H2):
                            if h + 1 < H2:
                                heavy_scores(h + 1)
                            pe.wait_ge(h_p, h + 1)
                            if h == 0:
                                pe.wait_ge(h_skvs, 1)
                            for s in range(2):
                                ins = nc.tensor.transpose(PS[:, 2 + h % 2, s * P:(s + 1) * P], ph[:, h % 2, s * P:(s + 1) * P], ident[:, :])
                            ins.then_inc(h_pT, 1)
                            pe.wait_ge(h_pTs, h + 1)
                            if h == 0:
                                pe.wait_ge(h_vs, 2)
                            if h >= 2:
                                pe.wait_ge(h_ou, h - 1)
                            for s in range(2):
                                ins = nc.tensor.matmul(PS[:, 4 + h % 2, 0:W2H], pTh[:, h % 2, s * P:(s + 1) * P], vh[:, s, h, :],
                                                       start=s == 0, stop=s == 1)
                            ins.then_inc(h_o, 1)
                        pe.wait_ge(h_oa, 1)
                        for m in range(M2):
                            ins = nc.tensor.transpose(PS[:, 6, m * P:(m + 1) * P], oa[:, m * P:(m + 1) * P], ident[:, :])
                        ins.then_inc(h_oT, 1)
                        pe.wait_ge(h_oTs, 1)
                        for m in range(M2):
                            ins = nc.tensor.matmul(PS[:, 7, 0:E], oaT[:, m, :], who[:, m, :], start=m == 0, stop=m == M2 - 1)
                        ins.then_inc(h_hv, 1)
                        pe.wait_ge(h_hvs, 1)
                        for t in range(T):
                            nc.tensor.matmul(PS[:, 4 + t // 2, E * (t % 2):E * (t % 2) + E], ohT[:, t * P:(t + 1) * P], hv[:, :],
                                             start=True, stop=True).then_inc(h_sc, 1)
                nc.all_engine_barrier(sems_to_clear=range(step_sems2[0].num, step_sems2[-1].num + 1))


_INS = ["x", "xT", "wq", "wk", "wv", "wo", "aq", "ak", "av", "ao", "bq_", "bk_", "bv_", "bo_",
        "vec_q", "vec_k", "vec_v", "vec_o", "ln_w", "ln_b", "l_qk", "l_v", "l_out", "rt_q", "rt_kv",
        "gamma", "h_q", "h_k", "h_v", "h_out_w", "null_k", "null_v", "null_q"]


def kernel(**inputs):
    import numpy as _np
    import concourse.bacc as _bacc
    from concourse import mybir as _mybir
    from concourse.bass_utils import run_bass_kernel_spmd as _run

    def of(name):
        return _np.asarray(inputs["L0_" + name])

    x = of("attn_x")
    wqkv = of("ffn_Wqkv")
    wkv = of("ffn_Wkv").reshape(H2, 2, D2, E)
    laid = {
        "x": x, "xT": x.transpose(0, 2, 1),
        "ln_w": of("ffn_ln_w"), "ln_b": of("ffn_ln_b"), "gamma": of("ffn_gamma"),
        "l_qk": wqkv[:2 * IN2].T, "l_v": wqkv[2 * IN2:].T, "l_out": of("ffn_Wout_l").T,
        "rt_q": of("ffn_rt_q"), "rt_kv": of("ffn_rt_kv"),
        "h_q": of("ffn_Wq").T, "h_k": wkv[:, 0].reshape(IN2, E).T, "h_v": wkv[:, 1].reshape(IN2, E).T,
        "h_out_w": of("ffn_Wout_h").T, "null_k": of("ffn_null_kv")[0], "null_v": of("ffn_null_kv")[1],
        "null_q": of("ffn_null_q"),
    }
    for n in "qkvo":
        laid["w" + n] = of("attn_W" + n).T
        laid["b" + n + "_"] = of("attn_b" + n)
        laid["a" + n] = of("attn_A" + n)
        laid["vec_" + n] = of("attn_B" + n).T

    nc = _bacc.Bacc("TRN2", target_bir_lowering=False, num_devices=1)
    arrays, args = {}, []
    for name in _INS:
        a = _np.ascontiguousarray(laid[name])
        arrays[f"in_{name}_dram"] = a
        args.append(nc.dram_tensor(f"in_{name}_dram", a.shape, _mybir.dt.from_np(a.dtype), kind="ExternalInput").ap())
    out = nc.dram_tensor("out_0_dram", x.shape, _mybir.dt.float32, kind="ExternalOutput").ap()
    block_kernel(nc, *args, out)
    r = _run(nc, [arrays], core_ids=[0])
    return r.results[0]["out_0_dram"]
```

```python
import math
from contextlib import ExitStack

import concourse.bass as bass
from concourse import mybir

F32 = mybir.dt.float32
BF16 = mybir.dt.bfloat16
ALU = mybir.AluOpType
ACT = mybir.ActivationFunctionType
AX = mybir.AxisListType

P = 128
NB = 32
S = 512
E = 256
T = S // P
C = E // P
H1, D1 = 16, 16
W1 = D1 + 1
W1H = 32
PV_BANK = 4
G1 = H1 // 4
RANK = 8
LORA = 16 / 8
H2, D2 = 8, 64
IN2 = H2 * D2
M2 = IN2 // P
W2H = D2 + 1
WIN = 64
NQ, NKV = 128, 256
NSEL = NQ + NKV
ITERS = 50
EPS_LN = 1e-5
DEEP = 96
SHIFT = 3
Q_PARTS = (0, 0, 0, 1, 1, 2)
K_PARTS = (0, 1, 2, 0, 1, 0)
LOWEST = -87.33654
NEG = -3.0e38


BY_ACT, BY_DVE = 0, 1

TAKEN_BY = {
    "tok": lambda name: BY_DVE, "aT": lambda name: BY_ACT, "y": lambda name: BY_DVE,
    "qk": lambda name: BY_ACT, "v": lambda name: BY_DVE, "rt": lambda name: BY_ACT, "xl": lambda name: BY_ACT,
    "lp": lambda name: int(name.split()[1]) % 2, "S": lambda name: BY_ACT, "T": lambda name: int(name.split()[1]) % 2,
    "O": lambda name: BY_DVE, "lo": lambda name: BY_ACT, "lz": lambda name: BY_DVE,
}


def tiles_of(m, k, has):
    names = []
    if "prev" in has:
        if m == 0:
            names.append(f"tok {k}")
        if m == 1 and k in (1, 2):
            names.append(f"aT {k - 1}")
        if (m, k) == (2, 0):
            names += ["y 0", "y 1"]
        if (m, k) == (3, 1):
            names.append("rt")
        if m == 3 and k >= 2:
            names.append(f"xl {k - 2}")
        if 4 <= m < 7:
            names.append(f"lp {4 * (m - 4) + k}")
        if m >= 8 and k == 0:
            names.append(f"O {m - 8}")
        if 7 <= m < 15:
            names.append(f"{'SSTT'[k]} {2 * (m - 7) + k % 2}")
        if m == 15 and k in (1, 2):
            names += [f"lo {2 * k - 2}", f"lo {2 * k - 1}"]
        if (m, k) == (15, 3):
            names += ["lz 0", "lz 1"]
    if "load" in has:
        for n, place in enumerate(((1, 0), (1, 3), (2, 1), (2, 2))):
            if (m, k) == place:
                names.append(f"qk {n}")
    if "next" in has:
        for n, place in enumerate(((2, 3), (3, 0))):
            if (m, k) == place:
                names.append(f"v {n}")
    return names


def seq(tensor, n):
    return tensor[n:n + 1, :, :] if isinstance(n, int) else tensor[bass.ds(n, 1), :, :]


def block_kernel(nc, x, xT, wq, wk, wv, wo, aq, ak, av, ao, bq_, bk_, bv_, bo_,
                 vec_q, vec_k, vec_v, vec_o, ln_w, ln_b, l_qk, l_v, l_out, rt_q, rt_kv,
                 gamma, h_q, h_k, h_v, h_out_w, null_k, null_v, null_q, out):
    ctx = ExitStack()
    with ctx:
        def sb(name, shape, dt=F32):
            return ctx.enter_context(nc.sbuf_tensor(name, shape, dt))

        def sem(name):
            return ctx.enter_context(nc.semaphore(name))

        def dram(name, shape, dt=F32):
            return nc.dram_tensor(name, shape, dt, kind="Internal").ap()

        parts_d = dram("parts_d", (2, 2, 3, C * P, S), BF16)
        norm_d = dram("norm_d", (NB, P, T * E))
        light_d = dram("light_d", (NB, P, T * E))
        route_d = dram("route_d", (NB, 2 * T, P))
        slot_d = dram("slot_d", (2 * NB, S))

        ident = sb("ident", [P, P])
        PS = ctx.enter_context(nc.psum_tensor("PS", [P, 8, 512], F32))

        w_q = sb("w_q", [P, C, E]); w_k = sb("w_k", [P, C, E])
        w_v = sb("w_v", [P, C, E]); w_o = sb("w_o", [P, C, E])
        b_q = sb("b_q", [P, C]); b_k = sb("b_k", [P, C])
        b_v = sb("b_v", [P, E]); b_o = sb("b_o", [P, E])
        lnw = sb("lnw", [P, C]); lnb = sb("lnb", [P, C]); gam = sb("gam", [P, C])
        rt = sb("rt", [P, 2, E])
        half = sb("half", [P, 4 * T])

        weights = [(w_q, wq, aq, vec_q), (w_k, wk, ak, vec_k), (w_v, wv, av, vec_v), (w_o, wo, ao, vec_o)]

        s_w = sem("s_w"); s_init = sem("s_init"); s_ident = sem("s_ident")
        s_lora = sem("s_lora"); s_lora_used = sem("s_lora_used"); s_ready = sem("s_ready")
        step_sems = []

        def step_sem(name):
            step_sems.append(sem(name))
            return step_sems[-1]

        s_xT = step_sem("s_xT"); s_x = step_sem("s_x"); s_xb = step_sem("s_xb")
        s_split = step_sem("s_split")
        s_parts = [step_sem("s_q_parts"), step_sem("s_k_parts")]
        s_stack = [step_sem(f"s_stack{g}") for g in range(G1)]
        s_s1 = step_sem("s_s1"); s_max = step_sem("s_max")
        s_shift = step_sem("s_shift")
        s_shift_in = [step_sem(f"s_shift_in{g}") for g in range(G1)]
        s_s2 = step_sem("s_s2"); s_p = step_sem("s_p")
        s_pv = step_sem("s_pv"); s_ot = step_sem("s_ot")
        c_full = step_sem("c_full")
        c_act = step_sem("c_act"); c_dve = step_sem("c_dve")
        s_var = step_sem("s_var"); s_rstd = step_sem("s_rstd"); s_x1 = step_sem("s_x1"); s_xn = step_sem("s_xn")
        s_rt = step_sem("s_rt"); s_lmax = step_sem("s_lmax"); s_vodd = step_sem("s_vodd")
        s_norm_out = step_sem("s_norm_out"); s_route_out = step_sem("s_route_out"); s_z_out = step_sem("s_z_out")
        s_pool = step_sem("s_pool"); s_dve = step_sem("s_dve")

        def pool_pow(out_ap, in_ap):
            return nc.gpsimd.tensor_tensor(out_ap, in_ap, half[:, 0:in_ap.shape[-1]], ALU.pow)

        with ExitStack() as c1:
            def sb1(name, shape, dt=F32):
                return c1.enter_context(nc.sbuf_tensor(name, shape, dt))
            lora_a = sb1("lora_a", [RANK, 4, E]); lora_b = sb1("lora_b", [RANK, 4, E])
            with nc.Block() as block:
                @block.sync
                def _(sp):
                    for n, (w, wt, a, bT) in enumerate(weights):
                        sp.dma_start(w[:, :, :], wt.rearrange("(c p) e -> p c e", p=P)).then_inc(s_w, 16)
                        sp.dma_start(lora_a[:, n, :], a).then_inc(s_w, 16)
                        sp.dma_start(lora_b[:, n, :], bT).then_inc(s_w, 16)
                    for dst, src in ((b_q, bq_), (b_k, bk_), (lnw, ln_w), (lnb, ln_b), (gam, gamma)):
                        sp.dma_start(dst[:, :], src.rearrange("(c p) -> p c", p=P),
                                     allow_slow_non_contiguous=True).then_inc(s_w, 16)
                    for dst, src in ((b_v, bv_), (b_o, bo_)):
                        sp.dma_start(dst[:, :], src.rearrange("(a e) -> a e", a=1).broadcast_to([P, E])).then_inc(s_w, 16)
                    sp.dma_start(rt[:, 0, :], rt_q.broadcast_to([P, E])).then_inc(s_w, 16)
                    sp.dma_start(rt[:, 1, :], rt_kv.broadcast_to([P, E])).then_inc(s_w, 16)

                @block.gpsimd
                def _(pool):
                    nc.gpsimd.memset(half[:, :], -0.5).then_inc(s_init, 1)
                    nc.gpsimd.memset(ident[:, :], 0.0).then_inc(s_ident, 1)
                    pool.wait_ge(s_ident, 1)
                    nc.gpsimd.affine_select(out=ident[:, :], in_=ident[:, :], compare_op=ALU.not_equal, fill=1.0,
                                            base=0, pattern=[[-1, P]], channel_multiplier=1).then_inc(s_ident, 1)

                @block.tensor
                def _(pe):
                    pe.wait_ge(s_w, 16 * 21)
                    for n in range(4):
                        for c in range(C):
                            nc.tensor.matmul(PS[:, n, c * E:(c + 1) * E], lora_a[:, n, c * P:(c + 1) * P],
                                             lora_b[:, n, :], start=True, stop=True).then_inc(s_lora, 1)

                @block.vector
                def _(dve):
                    for n, (w, _, _, _) in enumerate(weights):
                        dve.wait_ge(s_lora, C * (n + 1))
                        nc.vector.scalar_tensor_tensor(
                            out=w[:, :, :], in0=PS[:, n, :].rearrange("p (c e) -> p c e", c=C), scalar=LORA,
                            in1=w[:, :, :], op0=ALU.mult, op1=ALU.add).then_inc(s_lora_used, 1)
                    dve.wait_ge(s_lora_used, 4)
                    nc.vector.tensor_scalar(b_q[:, :], b_q[:, :], D1 ** -0.5, None, ALU.mult).then_inc(s_ready, 1)
                    dve.wait_ge(s_ready, 1)

        with ExitStack() as c1:
            def sb1(name, shape, dt=F32):
                return c1.enter_context(nc.sbuf_tensor(name, shape, dt))
            xT_s = [sb1(f"xT_s{n}", [P, C, S]) for n in range(2)]
            qk32 = sb1("qk32", [P, 2 * C, S])
            rest = sb1("rest", [P, C, S])
            parts = sb1("parts", [P, 3, C, S], BF16)
            qs = [sb1(f"qs{n}", [DEEP + SHIFT, H1, S], BF16) for n in range(2)]
            ks = [sb1(f"ks{n}", [DEEP + SHIFT, H1, S], BF16) for n in range(2)]
            vx = [sb1(f"vx{n}", [P, T, H1, W1]) for n in range(2)]
            nmax = sb1("nmax", [P, H1 * T])
            shift = sb1("shift", [4 * T, 2, SHIFT, P], BF16)
            shift_r = sb1("shift_r", [4 * T, P])
            probs = sb1("probs", [P, 8, S])
            oT = sb1("oT", [P, G1, S])
            rec = sb1("rec", [P, T, H1])
            an = sb1("an", [P, T, E])
            aT = sb1("aT", [P, C, S])
            y = sb1("y", [P, T, E])
            stats = sb1("stats", [P, T, 6]); mv = sb1("mv", [P, T, 2])
            sc = sb1("sc", [P, 8, T])
            x1 = sb1("x1", [P, T, E])
            xn = sb1("xn", [P, T, E])
            rs = sb1("rs", [P, 2, T]); rsT = sb1("rsT", [2 * T, P])
            wl = sb1("wl", [P, C, 3 * IN2]); wlo = sb1("wlo", [P, M2, E])
            qkl = sb1("qkl", [P, 2 * M2, S])
            vl = sb1("vl", [P, T, H2, W2H]); vodd = sb1("vodd", [WIN, T, H2, W2H])
            nml = sb1("nml", [P, H2, T])
            recl = sb1("recl", [P, H2, T])
            al = qk32
            alT = qkl[:, 0:M2, :]
            x_s = xn
            xlT = aT
            z = y
            pl = y[:, :, :].rearrange("p t e -> p (t e)")[:, 0:T * 3 * WIN].rearrange("p (t c) -> p t c", t=T)
            pTl = xn
            junk = qkl[:, 0:M2, :].rearrange("p m (a e) -> p (m a) e", e=E)

            with nc.Block() as block:
                @block.sync
                def _(sp):
                    sp.dma_start(wl[:, :, 0:2 * IN2], l_qk.rearrange("(c p) e -> p c e", p=P)).then_inc(s_w, 16)
                    sp.dma_start(wl[:, :, 2 * IN2:], l_v.rearrange("(c p) e -> p c e", p=P)).then_inc(s_w, 16)
                    sp.dma_start(wlo[:, :, :], l_out.rearrange("(c p) e -> p c e", p=P)).then_inc(s_w, 16)
                    sp.dma_start(xT_s[0][:, :, :], xT[0, :, :].rearrange("(c p) s -> p c s", p=P)).then_inc(s_w, 16)
                    sp.wait_ge(s_w, 16 * 25)

                @block.vector
                def _(dve):
                    for n in range(2):
                        nc.vector.memset(vx[n][:, :, :, D1:W1], 1.0).then_inc(s_init, 1)
                        nc.vector.memset(ks[n][DEEP:DEEP + SHIFT, :, :], 1.0).then_inc(s_init, 1)
                    nc.vector.memset(vl[:, :, :, D2:W2H], 1.0).then_inc(s_init, 1)
                    nc.vector.memset(PS[:, PV_BANK, :], 0.0).then_inc(s_init, 1)
                    dve.wait_ge(s_init, 7)

            def run(phases):
                tiles, at = [], {}
                for f, (_, _, has) in enumerate(phases):
                    for m in range(16):
                        for k in range(4):
                            for name in tiles_of(m, k, has):
                                at[f, name] = len(tiles)
                                tiles.append(TAKEN_BY[name.split()[0]](name))

                def full(f, name):
                    return at[f, name] + 1

                def taken(f, name):
                    return at_place(at[f, name])

                def at_place(n):
                    return (c_act, c_dve)[tiles[n]], sum(t == tiles[n] for t in tiles[:n + 1])

                def bank(f, name):
                    return PS[:, 5 + at[f, name] % 3, :]

                with nc.Block() as block:
                    @block.sync
                    def _(sp):
                        for f, (p, par, has) in enumerate(phases):
                            def stack(group, to, f=f):
                                for n, (dst, which) in enumerate(((qs[to], Q_PARTS), (ks[to], K_PARTS))):
                                    for j, m in enumerate(which):
                                        sp.dma_start(dst[D1 * j:D1 * (j + 1), 4 * group:4 * group + 4, :],
                                                     parts_d[to, n, m, 4 * D1 * group:4 * D1 * (group + 1), :]
                                                     .rearrange("(h d) s -> d h s", d=D1)).then_inc(s_stack[group], 16)

                            def shifts(group, f=f):
                                sp.wait_ge(s_shift, 4 * f + group + 1)
                                for m in range(SHIFT):
                                    sp.dma_start(qs[1 - par][DEEP + m:DEEP + m + 1, 4 * group:4 * group + 4, :]
                                                 .rearrange("a h (t s) -> a (h t) s", t=T),
                                                 shift[:, group % 2, m, :]).then_inc(s_shift_in[group], 16)

                            def write_parts(n, f=f):
                                sp.wait_ge(s_split, 2 * f + n + 1)
                                for m in range(3):
                                    sp.dma_start(parts_d[par, n, m, :, :].rearrange("(c p) s -> p c s", p=P),
                                                 parts[:, m, :, :]).then_inc(s_parts[n], 16)

                            if "next" in has:
                                if f and "cur" in has:
                                    sp.wait_ge(s_s2, 64 * f)
                                stack(3, 1 - par)
                            if "prev" in has:
                                if f:
                                    sp.wait_ge(*taken(f - 1, "O 7"))
                                sp.dma_start(x_s[:, :, :], seq(x, p - 1).rearrange("a (t p) e -> p (a t) e", p=P)).then_inc(s_x, 16)
                            if "xT" in has:
                                if "next" in has:
                                    sp.wait_ge(c_full, full(f, "v 1"))
                                sp.dma_start(xT_s[1 - par][:, :, :], seq(xT, p + 3).rearrange("a (c p) s -> p (a c) s", p=P)).then_inc(s_xT, 16)
                            if "prev" in has:
                                sp.wait_ge(*taken(f, "rt"))
                                sp.dma_start(seq(route_d, p - 1).rearrange("a r s -> (a r) s"), rsT[:, :]).then_inc(s_route_out, 16)
                            if "next" in has:
                                shifts(0)
                            if "load" in has:
                                write_parts(0)
                            if "prev" in has:
                                for name in ("lp 10", "lp 11"):
                                    sp.wait_ge(*taken(f, name))
                                sp.dma_start(vodd[:, :, :, :], vl[WIN:P, :, :, :]).then_inc(s_vodd, 16)
                            if "load" in has:
                                write_parts(1)
                            if "next" in has:
                                shifts(1)
                            for group in range(3):
                                if "load" in has:
                                    if group == 0:
                                        sp.wait_ge(s_parts[0], 48 * (f + 1))
                                        sp.wait_ge(s_parts[1], 48 * (f + 1))
                                    if "cur" in has:
                                        sp.wait_ge(s_s2, 64 * f + 16 * (group + 1))
                                    stack(group, par)
                                if group == 0 and "prev" in has:
                                    sp.wait_ge(s_xn, 2 * T * (f + 1))
                                    sp.dma_start(seq(norm_d, p - 1).rearrange("a p e -> (a p) e"),
                                                 an[:, :, :].rearrange("p t e -> p (t e)")).then_inc(s_norm_out, 16)
                            if "next" in has:
                                shifts(2)
                                shifts(3)
                            if "prev" in has:
                                sp.wait_ge(*taken(f, "lz 1"))
                                sp.dma_start(seq(light_d, p - 1).rearrange("a p e -> (a p) e"),
                                             z[:, :, :].rearrange("p t e -> p (t e)")).then_inc(s_z_out, 16)
                        n = len(phases)
                        if "prev" in has:
                            for s in (s_x, s_route_out, s_vodd, s_norm_out, s_z_out):
                                sp.wait_ge(s, 16 * n)
                        if "xT" in has:
                            sp.wait_ge(s_xT, 16 * n)
                        if "next" in has:
                            sp.wait_ge(s_stack[3], 192 * n)
                            for group in range(G1):
                                sp.wait_ge(s_shift_in[group], 48 * n)
                        if "load" in has:
                            for group in range(3):
                                sp.wait_ge(s_stack[group], 192 * n)

                    @block.gpsimd
                    def _(pool):
                        chain = [0]

                        def link(ins):
                            chain[0] += 1
                            ins.then_inc(s_pool, 1)
                            pool.wait_ge(s_pool, chain[0])

                        for f, (p, par, has) in enumerate(phases):
                            if "prev" in has:
                                pool.wait_ge(s_x, 16 * (f + 1))
                                nc.gpsimd.tensor_tensor(x_s[:, :, :], x_s[:, :, :],
                                                        b_o[:, :].rearrange("p (a e) -> p a e", a=1).broadcast_to([P, T, E]),
                                                        ALU.add).then_inc(s_xb, 1)
                                pool.wait_ge(s_var, f + 1)
                                v = mv[:, :, 1]
                                link(nc.gpsimd.tensor_scalar(sc[:, 0, :], v, EPS_LN, None, ALU.add))
                                link(pool_pow(sc[:, 1, :], sc[:, 0, :]))
                                pool.sem_inc(s_rstd, 1)
                                link(nc.gpsimd.tensor_tensor(sc[:, 2, :], sc[:, 1, :], sc[:, 1, :], ALU.mult))
                                link(nc.gpsimd.tensor_tensor(sc[:, 3, :], sc[:, 2, :], v, ALU.mult))
                                link(nc.gpsimd.tensor_scalar(sc[:, 4, :], sc[:, 3, :], EPS_LN, None, ALU.add))
                                link(pool_pow(sc[:, 5, :], sc[:, 4, :]))
                                pool.wait_ge(s_x1, T * (f + 1))
                                for t in range(T):
                                    nc.gpsimd.tensor_scalar(xn[:, t, :], x1[:, t, :], sc[:, 5, t:t + 1], None, ALU.mult).then_inc(s_xn, 1)
                                link(nc.gpsimd.tensor_scalar(sc[:, 6, :], sc[:, 3, :], 1e-24 / E, None, ALU.max))
                                link(pool_pow(sc[:, 7, :], sc[:, 6, :]))
                            if "load" in has:
                                for n in range(2):
                                    pool.wait_ge(*taken(f, f"qk {2 * n + 1}"))
                                    if f or n:
                                        pool.wait_ge(s_parts[1 - n], 48 * (f + n))
                                    q = qk32[:, C * n:C * n + C, :]
                                    r = rest[:, :, :]
                                    link(nc.gpsimd.tensor_copy(parts[:, 0, :, :], q))
                                    link(nc.gpsimd.tensor_tensor(r, q, parts[:, 0, :, :], ALU.subtract))
                                    link(nc.gpsimd.tensor_copy(parts[:, 1, :, :], r))
                                    nc.gpsimd.tensor_tensor(parts[:, 2, :, :], r, parts[:, 1, :, :],
                                                            ALU.subtract).then_inc(s_split, 1)
                            if "prev" in has:
                                for t in range(T):
                                    nc.gpsimd.tensor_scalar(an[:, t, :], x1[:, t, :], sc[:, 7, t:t + 1], None, ALU.mult).then_inc(s_xn, 1)

                    @block.scalar
                    def _(act):
                        for f, (p, par, has) in enumerate(phases):
                            def heads_out(hg, f=f, has=has):
                                act.wait_ge(s_pv, 16 * f + 4 * hg + 4)
                                if hg == 0 and "prev" in has:
                                    act.wait_ge(c_full, full(f, "tok 3"))
                                nc.scalar.activation(oT[:, hg, :], PS[:, PV_BANK, :], ACT.Copy).then_inc(s_ot, 1)

                            for m in range(16):
                                for k in range(4):
                                    if "cur" in has:
                                        n = 64 * f + 4 * m + k
                                        act.wait_ge(s_s2, n + 1)
                                        if n >= 8:
                                            act.wait_ge(s_pv, (n - 8) // 4 + 1)
                                        nc.scalar.activation(probs[:, n % 8, :], PS[:, 2 + n % 2, :], ACT.Exp).then_inc(s_p, 1)
                                        if k == 2 and m and m % 4 == 0:
                                            heads_out(m // 4 - 1)
                                    for name in tiles_of(m, k, has):
                                        kind, n = name.split()[0], int((name + " 0").split()[1])
                                        b = bank(f, name)
                                        if kind == "S":
                                            h, j = n // 2, 2 * (n % 2)
                                            act.wait_ge(s_lmax, 16 * f + n + 1)
                                            nc.scalar.activation(pl[:, j, :], b[:, 0:3 * WIN], ACT.Exp, bias=nml[:, h, j:j + 1])
                                            nc.scalar.activation(pl[:, j + 1, :], b[:, 256:256 + 3 * WIN], ACT.Exp,
                                                                 bias=nml[:, h, j + 1:j + 2]).then_inc(c_act, 1)
                                            continue
                                        if TAKEN_BY[kind](name) != BY_ACT:
                                            continue
                                        act.wait_ge(c_full, full(f, name))
                                        if kind == "aT":
                                            ins = nc.scalar.activation(aT[:, n, :], b, ACT.Copy)
                                        elif kind == "qk":
                                            ins = nc.scalar.activation(qk32[:, n, :], b, ACT.Identity,
                                                                       bias=(b_q, b_k)[n // C][:, n % C:n % C + 1],
                                                                       scale=D1 ** -0.5 if n < C else 1.0)
                                        elif kind == "rt":
                                            if f:
                                                act.wait_ge(s_route_out, 16 * f)
                                            ins = nc.scalar.activation(rsT[:, :], b[0:2 * T, 0:P], ACT.Copy)
                                        elif kind == "xl":
                                            ins = nc.scalar.activation(xlT[:, n, :], b, ACT.Identity,
                                                                       bias=lnb[:, n:n + 1], scale=lnw[:, n:n + 1])
                                        elif kind == "lp" and n < 2 * M2:
                                            ins = nc.scalar.activation(qkl[:, n, :], b, ACT.Copy,
                                                                       scale=D2 ** -0.5 if n < M2 else 1.0)
                                        elif kind == "lp":
                                            if f:
                                                act.wait_ge(s_vodd, 16 * f)
                                            ins = nc.scalar.activation(vl[:, n - 2 * M2, :, 0:D2],
                                                                       b.rearrange("p (h d) -> p h d", d=D2), ACT.Copy)
                                        elif kind == "T":
                                            j = 2 * (n % 2)
                                            ins = nc.scalar.activation(pTl[:, j:j + 2, :].rearrange("p j c -> p (j c)"), b, ACT.Copy)
                                        elif kind == "lo":
                                            ins = nc.scalar.activation(alT[:, n, :], b, ACT.Copy)
                                        ins.then_inc(c_act, 1)
                            if "cur" in has:
                                heads_out(3)

                    @block.vector
                    def _(dve):
                        chain = [0]

                        def link(ins):
                            chain[0] += 1
                            ins.then_inc(s_dve, 1)
                            dve.wait_ge(s_dve, chain[0])

                        for f, (p, par, has) in enumerate(phases):
                            def parts_of_max(hg, f=f):
                                n = 68 * f + 17 * hg + 16
                                dve.wait_ge(s_s1, n + 1)
                                if hg >= 2:
                                    dve.wait_ge(s_shift_in[hg - 2], 48 * (f + 1))
                                elif f:
                                    dve.wait_ge(s_shift_in[hg + 2], 48 * f)
                                rows = PS[0:4 * T, n % 2, 0:P]
                                link(nc.vector.tensor_copy(shift[:, hg % 2, 0, :], rows))
                                nc.vector.tensor_tensor(shift_r[:, :], rows, shift[:, hg % 2, 0, :], ALU.subtract).then_inc(s_max, 1)
                                dve.wait_ge(s_max, n + 1)
                                link(nc.vector.tensor_copy(shift[:, hg % 2, 1, :], shift_r[:, :]))
                                nc.vector.tensor_tensor(shift[:, hg % 2, 2, :], shift_r[:, :], shift[:, hg % 2, 1, :],
                                                        ALU.subtract).then_inc(s_shift, 1)

                            for m in range(16):
                                for k in range(4):
                                    if "next" in has:
                                        u = 4 * m + k
                                        if u % 16 == 0 and u:
                                            parts_of_max(u // 16 - 1)
                                        n = 68 * f + u + u // 16
                                        dve.wait_ge(s_s1, n + 1)
                                        nc.vector.reduce_max(nmax[:, u:u + 1], PS[:, n % 2, :], AX.X, negate=True).then_inc(s_max, 1)
                                    for name in tiles_of(m, k, has):
                                        kind, n = name.split()[0], int((name + " 0").split()[1])
                                        b = bank(f, name)
                                        if kind == "S":
                                            h, j = n // 2, 2 * (n % 2)
                                            dve.wait_ge(c_full, full(f, name))
                                            nc.vector.reduce_max(nml[:, h, j:j + 2],
                                                                 b.rearrange("p (j c) -> p j c", j=2)[:, :, 0:3 * WIN],
                                                                 AX.X, negate=True).then_inc(s_lmax, 1)
                                            continue
                                        if TAKEN_BY[kind](name) != BY_DVE:
                                            continue
                                        dve.wait_ge(c_full, full(f, name))
                                        if kind == "tok":
                                            if n == 0 and f:
                                                dve.wait_ge(s_norm_out, 16 * f)
                                            o = b.rearrange("p (h d) -> p h d", d=W1H)
                                            link(nc.vector.reciprocal(rec[:, n, :], o[:, :, D1]))
                                            ins = nc.vector.tensor_tensor(
                                                an[:, n, :].rearrange("p (h d) -> p h d", d=D1), o[:, :, 0:D1],
                                                rec[:, n, :].rearrange("p (h a) -> p h a", a=1).broadcast_to([P, H1, D1]), ALU.mult)
                                        elif kind == "y":
                                            if n == 0:
                                                dve.wait_ge(s_xb, f + 1)
                                                if f:
                                                    dve.wait_ge(s_z_out, 16 * f)
                                            ins = nc.vector.tensor_tensor(y[:, 2 * n:2 * n + 2, :], b.rearrange("p (t e) -> p t e", e=E),
                                                                          x_s[:, 2 * n:2 * n + 2, :], ALU.add)
                                        elif kind == "v":
                                            ins = nc.vector.tensor_tensor(
                                                vx[1 - par][:, 2 * n:2 * n + 2, :, 0:D1],
                                                b.rearrange("p (t h d) -> p t h d", t=2, d=D1),
                                                b_v[:, :].rearrange("p (a h d) -> p a h d", a=1, d=D1).broadcast_to([P, 2, H1, D1]),
                                                ALU.add)
                                        elif kind == "lp" and n < 2 * M2:
                                            ins = nc.vector.tensor_scalar(qkl[:, n, :], b, D2 ** -0.5 if n < M2 else 1.0, None, ALU.mult)
                                        elif kind == "lp":
                                            if f:
                                                dve.wait_ge(s_vodd, 16 * f)
                                            ins = nc.vector.tensor_copy(vl[:, n - 2 * M2, :, 0:D2], b.rearrange("p (h d) -> p h d", d=D2))
                                        elif kind == "T":
                                            j = 2 * (n % 2)
                                            ins = nc.vector.tensor_copy(pTl[:, j:j + 2, :].rearrange("p j c -> p (j c)"), b)
                                        elif kind == "O":
                                            if n == 0 and "load" in has:
                                                dve.wait_ge(s_split, 2 * f + 2)
                                            o = b[:, 0:T * W2H].rearrange("p (t d) -> p t d", d=W2H)
                                            link(nc.vector.reciprocal(recl[:, n, :], o[:, :, D2]))
                                            ins = nc.vector.tensor_tensor(
                                                al[:, :, n * D2:(n + 1) * D2], o[:, :, 0:D2],
                                                recl[:, n, :].rearrange("p (t a) -> p t a", a=1).broadcast_to([P, T, D2]), ALU.mult)
                                        elif kind == "lz":
                                            ins = nc.vector.tensor_tensor(z[:, 2 * n:2 * n + 2, :], b.rearrange("p (t e) -> p t e", e=E),
                                                                          x1[:, 2 * n:2 * n + 2, :], ALU.add)
                                        ins.then_inc(c_dve, 1)
                                    if "prev" in has and (m, k) == (2, 0):
                                        dve.wait_ge(*taken(f, "y 1"))
                                        for t in range(T):
                                            ins = nc.vector.bn_stats(stats[:, t, :], y[:, t, :])
                                        link(ins)
                                        for t in range(T):
                                            ins = nc.vector.bn_aggr(mv[:, t, :], stats[:, t, :])
                                        ins.then_inc(s_var, 1)
                                    if "prev" in has and (m, k) == (2, 2):
                                        dve.wait_ge(s_rstd, f + 1)
                                        dve.wait_ge(s_var, f + 1)
                                        if f:
                                            dve.wait_ge(s_xn, 2 * T * f)
                                        for t in range(T):
                                            nc.vector.tensor_scalar(x1[:, t, :], y[:, t, :], mv[:, t, 0:1], sc[:, 1, t:t + 1],
                                                                    ALU.subtract, ALU.mult).then_inc(s_x1, 1)
                                    if "prev" in has and (m, k) == (2, 3):
                                        dve.wait_ge(s_x1, T * (f + 1))
                                        for r in range(2):
                                            for t in range(T):
                                                ins = nc.vector.tensor_tensor_reduce(
                                                    out=junk[:, T * r + t, :], in0=x1[:, t, :], in1=rt[:, r, :], scale=1.0, scalar=0.0,
                                                    op0=ALU.mult, op1=ALU.add, accum_out=rs[:, r, t:t + 1])
                                        ins.then_inc(s_rt, 1)
                            if "next" in has:
                                parts_of_max(3)

                    @block.tensor
                    def _(pe):
                        for f, (p, par, has) in enumerate(phases):
                            def max_rows(hg, f=f):
                                n = 68 * f + 17 * hg + 16
                                pe.wait_ge(s_max, n)
                                nc.tensor.transpose(PS[0:4 * T, n % 2, 0:P], nmax[:, 4 * T * hg:4 * T * (hg + 1)],
                                                    ident[:, :]).then_inc(s_s1, 1)

                            def values(m, f=f, par=par):
                                hg, t = m // 4, m % 4
                                pe.wait_ge(s_p, 64 * f + 4 * m + 4)
                                if t == 0 and (f or hg):
                                    pe.wait_ge(s_ot, 4 * f + hg)
                                if m == 0 and f:
                                    pe.wait_ge(*taken(f - 1, "v 1"))
                                for r in range(4):
                                    ins = nc.tensor.matmul(PS[32 * r:32 * r + W1, PV_BANK, :], vx[par][:, t, 4 * hg + r, :],
                                                           probs[:, (4 * m + r) % 8, :], start=t == 0, stop=t == T - 1)
                                ins.then_inc(s_pv, 1)

                            def tile(name, f=f, par=par):
                                kind, n = name.split()[0], int((name + " 0").split()[1])
                                b, place = bank(f, name), at[f, name]
                                if place >= 3:
                                    pe.wait_ge(*at_place(place - 3))
                                if kind == "tok":
                                    if f:
                                        pe.wait_ge(s_ot, 4 * f)
                                    for g in range(G1):
                                        ins = nc.tensor.transpose(b[:, g * P:(g + 1) * P], oT[:, g, n * P:(n + 1) * P], ident[:, :])
                                elif kind == "aT":
                                    pe.wait_ge(*taken(f, "tok 3"))
                                    for t in range(T):
                                        ins = nc.tensor.transpose(b[:, t * P:(t + 1) * P], an[:, t, n * P:(n + 1) * P], ident[:, :])
                                elif kind == "y":
                                    pe.wait_ge(*taken(f, "aT 1"))
                                    for t in (2 * n, 2 * n + 1):
                                        for c in range(C):
                                            ins = nc.tensor.matmul(b[:, E * (t % 2):E * (t % 2) + E], aT[:, c, t * P:(t + 1) * P],
                                                                   w_o[:, c, :], start=c == 0, stop=c == C - 1)
                                elif kind == "qk":
                                    if f:
                                        pe.wait_ge(s_xT, 16 * f)
                                    for c in range(C):
                                        ins = nc.tensor.matmul(b, (w_q, w_k)[n // C][:, c, (n % C) * P:(n % C + 1) * P],
                                                               xT_s[par][:, c, :], start=c == 0, stop=c == C - 1)
                                elif kind == "v":
                                    for t in (2 * n, 2 * n + 1):
                                        for c in range(C):
                                            ins = nc.tensor.matmul(b[:, E * (t % 2):E * (t % 2) + E],
                                                                   xT_s[1 - par][:, c, t * P:(t + 1) * P], w_v[:, c, :],
                                                                   start=c == 0, stop=c == C - 1)
                                elif kind == "rt":
                                    pe.wait_ge(s_rt, f + 1)
                                    ins = nc.tensor.transpose(b[0:2 * T, 0:P], rs[:, :, :].rearrange("p r t -> p (r t)"), ident[:, :])
                                elif kind == "xl":
                                    pe.wait_ge(s_xn, 2 * T * f + T)
                                    for t in range(T):
                                        ins = nc.tensor.transpose(b[:, t * P:(t + 1) * P], xn[:, t, n * P:(n + 1) * P], ident[:, :])
                                elif kind == "lp" and n < 2 * M2:
                                    pe.wait_ge(*taken(f, "xl 1"))
                                    for c in range(C):
                                        ins = nc.tensor.matmul(b, wl[:, c, n * P:(n + 1) * P], xlT[:, c, :],
                                                               start=c == 0, stop=c == C - 1)
                                elif kind == "lp":
                                    t = n - 2 * M2
                                    for c in range(C):
                                        ins = nc.tensor.matmul(b, xlT[:, c, t * P:(t + 1) * P], wl[:, c, 2 * IN2:],
                                                               start=c == 0, stop=c == C - 1)
                                elif kind == "S":
                                    h, half_ = n // 2, n % 2
                                    if n == 0:
                                        pe.wait_ge(*taken(f, "lp 10"))
                                        pe.wait_ge(*taken(f, "lp 11"))
                                    r, m = D2 * (h % 2), h // 2
                                    q, k = qkl[r:r + D2, m, :], qkl[r:r + D2, M2 + m, :]
                                    for j in (2 * half_, 2 * half_ + 1):
                                        o = b[:, 256 * (j % 2):256 * (j % 2) + 3 * WIN]
                                        before, after = max(2 * j - 1, 0), min(2 * j + 2, 2 * T - 1)
                                        nc.tensor.matmul(o[0:WIN, 0:WIN], q[:, 2 * j * WIN:(2 * j + 1) * WIN],
                                                         k[:, before * WIN:(before + 1) * WIN], start=True, stop=True)
                                        nc.tensor.matmul(o[WIN:P, 0:WIN], q[:, (2 * j + 1) * WIN:(2 * j + 2) * WIN],
                                                         k[:, after * WIN:(after + 1) * WIN], start=True, stop=True)
                                        ins = nc.tensor.matmul(o[:, WIN:3 * WIN], q[:, j * P:(j + 1) * P], k[:, j * P:(j + 1) * P],
                                                               start=True, stop=True)
                                elif kind == "T":
                                    pe.wait_ge(*taken(f, f"S {n}"))
                                    for j in range(2):
                                        src = pl[:, 2 * (n % 2) + j, :]
                                        nc.tensor.transpose(b[:, 256 * j:256 * j + P], src[:, WIN:3 * WIN], ident[:, :])
                                        ins = nc.tensor.transpose(b[0:WIN, 256 * j + P:256 * j + 2 * P], src[:, 0:WIN], ident[:, :])
                                elif kind == "O":
                                    pe.wait_ge(*taken(f, f"T {2 * n}"))
                                    pe.wait_ge(*taken(f, f"T {2 * n + 1}"))
                                    if n == 0:
                                        pe.wait_ge(s_vodd, 16 * (f + 1))
                                    for j in range(T):
                                        o = b[:, j * W2H:(j + 1) * W2H]
                                        pT = pTl[:, j, :]
                                        ins = nc.tensor.matmul(o, pT[:, 0:P], vl[:, j, n, :], start=True, stop=False, skip_group_check=True)
                                        if j > 0:
                                            ins = nc.tensor.matmul(o[0:WIN, :], pT[0:WIN, P:P + WIN], vodd[:, j - 1, n, :],
                                                                   start=False, stop=True, skip_group_check=True)
                                        if j < T - 1:
                                            ins = nc.tensor.matmul(o[WIN:P, :], pT[0:WIN, P + WIN:2 * P], vl[0:WIN, j + 1, n, :],
                                                                   start=False, stop=True, skip_group_check=True)
                                elif kind == "lo":
                                    pe.wait_ge(*taken(f, "O 7"))
                                    for t in range(T):
                                        ins = nc.tensor.transpose(b[:, t * P:(t + 1) * P], al[:, t, n * P:(n + 1) * P], ident[:, :])
                                elif kind == "lz":
                                    pe.wait_ge(*taken(f, "lo 3"))
                                    for t in (2 * n, 2 * n + 1):
                                        for m in range(M2):
                                            ins = nc.tensor.matmul(b[:, E * (t % 2):E * (t % 2) + E], alT[:, m, t * P:(t + 1) * P],
                                                                   wlo[:, m, :], start=m == 0, stop=m == M2 - 1)
                                ins.then_inc(c_full, 1)

                            for m in range(16):
                                for k in range(4):
                                    u = 4 * m + k
                                    if "cur" in has:
                                        n = 64 * f + u
                                        h, t = 4 * (u // 16) + u % 4, (u // 4) % 4
                                        if u % 16 == 0 and f:
                                            pe.wait_ge(s_shift_in[u // 16], 48 * f)
                                        if n >= 2:
                                            pe.wait_ge(s_p, n - 1)
                                        nc.tensor.matmul(PS[:, 2 + n % 2, :], ks[par][:, h, t * P:(t + 1) * P], qs[par][:, h, :],
                                                         start=True, stop=True).then_inc(s_s2, 1)
                                    if "next" in has:
                                        if u % 16 == 0:
                                            if u:
                                                max_rows(u // 16 - 1)
                                            landed = f + (u == 48)
                                            if landed:
                                                pe.wait_ge(s_stack[u // 16], 192 * landed)
                                        n = 68 * f + u + u // 16
                                        h, t = u // T, u % T
                                        if n >= 2:
                                            pe.wait_ge(s_max, n - 1)
                                        nc.tensor.matmul(PS[:, n % 2, :], qs[1 - par][0:DEEP, h, t * P:(t + 1) * P],
                                                         ks[1 - par][0:DEEP, h, :], start=True, stop=True).then_inc(s_s1, 1)
                                    if "cur" in has and k == 1 and m:
                                        values(m - 1)
                                    for name in tiles_of(m, k, has):
                                        tile(name)
                            if "cur" in has:
                                values(15)
                            if "next" in has:
                                max_rows(3)
                nc.all_engine_barrier(sems_to_clear=range(step_sems[0].num, step_sems[-1].num + 1))

            full_phase = ("load", "next", "cur", "prev", "xT")
            run([(-2, 0, ("load", "xT"))])
            run([(-1, 1, ("load", "next", "xT"))])
            run([(0, 0, ("load", "next", "cur", "xT"))])
            run([(1, 1, full_phase)])
            with nc.Fori(2, NB - 4, 2) as i:
                run([(i, 0, full_phase), (i + 1, 1, full_phase)])
            run([(NB - 4, 0, full_phase)])
            run([(NB - 3, 1, full_phase[:-1])])
            run([(NB - 2, 0, ("next", "cur", "prev"))])
            run([(NB - 1, 1, ("cur", "prev"))])
            run([(NB, 0, ("prev",))])

        slotT = sb("slotT", [P, T, 2 * NB]); scoreT = sb("scoreT", [P, T, 2 * NB])
        r_in = sem("r_in"); r_init = sem("r_init"); r_t = sem("r_t"); r_e = sem("r_e"); r_l = sem("r_l"); r_a = sem("r_a")
        r_dve = sem("r_dve"); r_score = sem("r_score"); r_T = sem("r_T"); r_end = sem("r_end"); r_slot = sem("r_slot")
        r_top = sem("r_top"); r_key = sem("r_key")
        R = 2 * NB
        with ExitStack() as c2:
            def sb2(name, shape, dt=F32):
                return c2.enter_context(nc.sbuf_tensor(name, shape, dt))
            s_r = sb2("s_r", [R, S]); low = sb2("low", [R, S]); e_r = sb2("e_r", [R, S])
            one = sb2("one", [R, S]); key = sb2("key", [R, S]); work = sb2("work", [R, 2, S])
            gt = sb2("gt", [R, S]); eq = sb2("eq", [R, S]); cum = sb2("cum", [R, S]); mask = sb2("mask", [R, S])
            slot = sb2("slot", [R, S]); score = sb2("score", [R, S]); inv = sb2("inv", [R, S])
            top = sb2("top", [R, 2, 8])
            logk = sb2("logk", [R, 1]); room = sb2("room", [R, 1]); kk = sb2("kk", [R, 1]); thr = sb2("thr", [R, 1])
            smax = sb2("smax", [R, 1]); na = sb2("na", [R, 1]); nm = sb2("nm", [R, 1]); se = sb2("se", [R, 1])
            ln = sb2("ln", [R, 1]); cnt = sb2("cnt", [R, 1])
            with nc.Block() as block:
                @block.sync
                def _(sp):
                    for r in range(2):
                        sp.dma_start(s_r[r * NB:(r + 1) * NB, :],
                                     route_d[:, r * T:(r + 1) * T, :].rearrange("b t s -> b (t s)")).then_inc(r_in, 16)
                    sp.wait_ge(r_slot, 1)
                    sp.dma_start(slot_d, slot[:, :]).then_inc(r_end, 16)
                    sp.wait_ge(r_end, 16)

                @block.scalar
                def _(act):
                    with act.Fori(0, ITERS - 1) as i:
                        act.wait_ge(r_t, i * 2 + 2)
                        nc.scalar.activation(e_r[:, :], low[:, :], ACT.Exp, bias=nm[:, 0:1], accum_out=se[:, 0:1]).then_inc(r_e, 1)
                        act.wait_ge(r_e, i + 1)
                        nc.scalar.activation(ln[:, :], se[:, :], ACT.Ln).then_inc(r_l, 1)
                    act.wait_ge(r_key, 1)
                    nc.scalar.activation(score[:, :], low[:, :], ACT.Exp).then_inc(r_score, 1)

                @block.vector
                def _(dve):
                    n_dve = [0]

                    def link(ins):
                        n_dve[0] += 1
                        ins.then_inc(r_dve, 1)
                        dve.wait_ge(r_dve, n_dve[0])

                    for r, k in ((0, NQ), (NB, NKV)):
                        nc.vector.memset(logk[r:r + NB, :], math.log(min(k * 9.0 / 8.0, S))).then_inc(r_init, 1)
                        nc.vector.memset(kk[r:r + NB, :], float(k)).then_inc(r_init, 1)
                        nc.vector.memset(na[r:r + NB, :], math.log(S) - math.log(min(k * 9.0 / 8.0, S))).then_inc(r_init, 1)
                    nc.vector.memset(one[:, :], 1.0).then_inc(r_init, 1)
                    dve.wait_ge(r_init, 7)
                    dve.wait_ge(r_in, 32)
                    link(nc.vector.reduce_max(smax[:, :], s_r[:, :], AX.X))
                    with dve.Fori(0, ITERS - 1) as i:
                        nc.vector.tensor_scalar(low[:, :], s_r[:, :], na[:, 0:1], None, ALU.min).then_inc(r_t, 1)
                        nc.vector.tensor_scalar(nm[:, :], smax[:, :], na[:, 0:1], -1.0, ALU.min, ALU.mult).then_inc(r_t, 1)
                        dve.wait_ge(r_l, i + 1)
                        nc.vector.tensor_scalar(na[:, :], ln[:, :], nm[:, 0:1], logk[:, 0:1], ALU.subtract,
                                                ALU.subtract).then_inc(r_a, 1)
                        dve.wait_ge(r_a, i + 1)
                    link(nc.vector.tensor_scalar(low[:, :], s_r[:, :], na[:, 0:1], 0.0, ALU.subtract, ALU.min))
                    dve.sem_inc(r_key, 1)
                    link(nc.vector.scalar_tensor_tensor(out=key[:, :], in0=low[:, :], scalar=-2.98e-8, in1=low[:, :],
                                                        op0=ALU.is_lt, op1=ALU.mult))
                    link(nc.vector.tensor_scalar(work[:, 0, :], key[:, :], LOWEST, None, ALU.max))
                    link(nc.vector.tensor_copy(key[:, :], work[:, 0, :]))
                    for half_, rows in enumerate((slice(0, NB), slice(NB, R))):
                        for i in range(NQ // 16):
                            for n in range(2):
                                done = (half_ * (NQ // 16) + i) * 4 + 2 * n
                                nc.vector.max(top[:, n, :], work[:, n, :]).then_inc(r_top, 1)
                                dve.wait_ge(r_top, done + 1)
                                nc.vector.match_replace(work[:, 1 - n, :], top[:, n, :], work[:, n, :], NEG).then_inc(r_top, 1)
                                dve.wait_ge(r_top, done + 2)
                        link(nc.vector.tensor_copy(thr[rows, :], top[rows, 1, 7:8]))
                    nc.vector.tensor_scalar(gt[:, :], key[:, :], thr[:, 0:1], None, ALU.is_gt)
                    link(nc.vector.tensor_scalar(eq[:, :], key[:, :], thr[:, 0:1], None, ALU.is_equal))
                    link(nc.vector.reduce_sum(cnt[:, :], gt[:, :], AX.X))
                    link(nc.vector.tensor_tensor_scan(cum[:, :], one[:, :], eq[:, :], 0.0, ALU.mult, ALU.add))
                    link(nc.vector.tensor_tensor(room[:, :], kk[:, :], cnt[:, :], ALU.subtract))
                    link(nc.vector.scalar_tensor_tensor(out=mask[:, :], in0=cum[:, :], scalar=room[:, 0:1], in1=eq[:, :],
                                                        op0=ALU.is_le, op1=ALU.mult))
                    link(nc.vector.tensor_tensor(eq[:, :], mask[:, :], gt[:, :], ALU.add))
                    link(nc.vector.tensor_tensor_scan(cum[:, :], one[:, :], eq[:, :], 0.0, ALU.mult, ALU.add))
                    link(nc.vector.tensor_tensor(gt[:, :], cum[:, :], eq[:, :], ALU.mult))
                    nc.vector.tensor_scalar(slot[:, :], gt[:, :], -1.0, None, ALU.add).then_inc(r_slot, 1)
                    dve.wait_ge(r_score, 1)
                    link(nc.vector.tensor_scalar(inv[:, :], score[:, :], -1.0, 1.0, ALU.mult, ALU.add))
                    nc.vector.tensor_tensor(work[:, 0, :], inv[:, :], score[:, :], ALU.add).then_inc(r_slot, 1)
                    dve.wait_ge(r_T, 2 * T)
                    nc.vector.tensor_copy(slotT[:, :, :].rearrange("p t r -> p (t r)"), PS[:, 0, 0:T * R])
                    link(nc.vector.tensor_copy(scoreT[:, :, :].rearrange("p t r -> p (t r)"), PS[:, 1, 0:T * R]))

                @block.tensor
                def _(pe):
                    pe.wait_ge(r_slot, 2)
                    for n, src in enumerate((slot[:, :], work[:, 0, :])):
                        for t in range(T):
                            nc.tensor.transpose(PS[:, n, t * R:(t + 1) * R], src[:, t * P:(t + 1) * P],
                                                ident[0:R, 0:R]).then_inc(r_T, 1)

        with ExitStack() as c3:
            def sb3(name, shape, dt=F32):
                return c3.enter_context(nc.sbuf_tensor(name, shape, dt))

            step_sems2 = []

            def sem3(name):
                step_sems2.append(c3.enter_context(nc.semaphore(name)))
                return step_sems2[-1]
            whq = sb3("whq", [P, C, IN2]); whk = sb3("whk", [P, C, IN2]); whv = sb3("whv", [P, C, IN2]); who = sb3("who", [P, M2, E])
            nq_b = sb3("nq_b", [P, E]); nv_b = sb3("nv_b", [P, H2, W2H])
            iota_r = sb3("iota_r", [P, NKV]); iota_c = sb3("iota_c", [P, 1])
            norm = sb3("norm", [P, 2, T, E]); light = sb3("light", [P, 2, T, E]); row = sb3("row", [P, 2, S])
            cols = sb3("cols", [P, T, 2]); scol = sb3("scol", [P, T, 2]); unch = sb3("unch", [P, T])
            oh = sb3("oh", [P, T, NSEL]); ohT = sb3("ohT", [P, S])
            xsT = sb3("xsT", [P, C, NSEL]); skv = sb3("skv", [P, 2])
            qh = sb3("qh", [P, M2, NQ]); kh = sb3("kh", [P, M2, NKV + 1]); vh = sb3("vh", [P, 2, H2, W2H])
            nmh = sb3("nmh", [P, H2]); ph = sb3("ph", [P, 2, NKV + 1]); pTh = sb3("pTh", [P, 2, NKV])
            ou = sb3("ou", [P, H2, W2H]); rech = sb3("rech", [P, H2]); oa = sb3("oa", [P, IN2]); oaT = sb3("oaT", [P, M2, NQ])
            hv = sb3("hv", [P, E]); f1 = sb3("f1", [P, T, E]); f2 = sb3("f2", [P, T, E])
            st2 = sb3("st2", [P, T, 6]); mv2 = sb3("mv2", [P, T, 2]); sc2 = sb3("sc2", [P, 2, T])
            outb = sb3("outb", [P, 2, T, E])
            h_w, h_init = (c3.enter_context(nc.semaphore(n)) for n in ("h_w", "h_init"))
            h_norm, h_light, h_row, h_dve, h_oh = (sem3(n) for n in ("h_norm", "h_light", "h_row", "h_dve", "h_oh"))
            h_ga, h_xs, h_q_, h_qs, h_k_, h_kc, h_v_, h_vs, h_skv, h_skvs = (sem3(n) for n in ("h_ga", "h_xs", "h_q_", "h_qs", "h_k_", "h_kc", "h_v_", "h_vs", "h_skv", "h_skvs"))
            h_s, h_max, h_p, h_pT, h_pTs, h_o, h_ou, h_oa, h_oT, h_oTs, h_hv, h_hvs, h_sc, h_f, h_var, h_rstd, h_y, h_out, h_pool, h_done = (
                sem3(n) for n in ("h_s", "h_max", "h_p", "h_pT", "h_pTs", "h_o", "h_ou", "h_oa", "h_oT", "h_oTs", "h_hv", "h_hvs", "h_sc", "h_f", "h_var", "h_rstd", "h_y", "h_out", "h_pool", "h_done"))
            with nc.Block() as block:
                @block.sync
                def _(sp):
                    for dst, src in ((whq, h_q), (whk, h_k), (whv, h_v), (who, h_out_w)):
                        sp.dma_start(dst[:, :, :], src.rearrange("(c p) e -> p c e", p=P)).then_inc(h_w, 16)
                    sp.dma_start(kh[:, :, NKV:NKV + 1], null_k.rearrange("(m h) (d a) -> (h d) m a", h=2, a=1),
                                 allow_slow_non_contiguous=True).then_inc(h_w, 16)
                    sp.dma_start(nv_b[:, :, 0:D2], null_v.rearrange("(a h) d -> a h d", a=1).broadcast_to([P, H2, D2])).then_inc(h_w, 16)
                    sp.dma_start(nq_b[:, :], null_q.rearrange("(a e) -> a e", a=1).broadcast_to([P, E])).then_inc(h_w, 16)
                    sp.wait_ge(h_w, 16 * 7)

                @block.gpsimd
                def _(pool):
                    nc.gpsimd.iota(iota_r[:, :], [[1, NKV]], base=0, channel_multiplier=0,
                                   allow_small_or_imprecise_dtypes=True).then_inc(h_init, 1)
                    nc.gpsimd.iota(iota_c[:, :], [[1, 1]], base=0, channel_multiplier=1,
                                   allow_small_or_imprecise_dtypes=True).then_inc(h_init, 1)
                    nc.gpsimd.memset(vh[:, :, :, D2:W2H], 1.0).then_inc(h_init, 1)
                    nc.gpsimd.memset(nv_b[:, :, D2:W2H], 1.0).then_inc(h_init, 1)

            with nc.Fori(0, NB) as i:
                with nc.Block() as block:
                    @block.sync
                    def _(sp):
                        sp.dma_start(norm[:, 0, :, :].rearrange("p t e -> p (t e)"), norm_d[bass.ds(i, 1), :, :].rearrange("a p e -> (a p) e")).then_inc(h_norm, 16)
                        sp.dma_start(row[:, 0, :], slot_d[bass.ds(i, 1), :].broadcast_to([P, S])).then_inc(h_row, 16)
                        sp.dma_start(light[:, 0, :, :].rearrange("p t e -> p (t e)"), light_d[bass.ds(i, 1), :, :].rearrange("a p e -> (a p) e")).then_inc(h_light, 16)
                        sp.wait_ge(h_y, T)
                        sp.dma_start(out[bass.ds(i, 1), :, :].rearrange("a (t p) e -> p (a t) e", p=P), outb[:, 0, :, :]).then_inc(h_done, 16)
                        sp.wait_ge(h_done, 16)

                    @block.gpsimd
                    def _(pool):
                        pool.wait_ge(h_var, 1)
                        nc.gpsimd.tensor_scalar(sc2[:, 0, :], mv2[:, :, 1], EPS_LN, None, ALU.add).then_inc(h_pool, 1)
                        pool.wait_ge(h_pool, 1)
                        pool_pow(sc2[:, 1, :], sc2[:, 0, :]).then_inc(h_rstd, 1)

                    @block.scalar
                    def _(act):
                        for c in range(C):
                            act.wait_ge(h_ga, c + 1)
                            nc.scalar.activation(xsT[:, c, :], PS[:, c, 0:NSEL], ACT.Copy, scale=gam[:, c:c + 1]).then_inc(h_xs, 1)
                        act.wait_ge(h_q_, 1)
                        nc.scalar.activation(qh[:, :, :].rearrange("p m s -> p (m s)"), PS[:, 3, :], ACT.Copy, scale=D2 ** -0.5).then_inc(h_qs, 1)
                        act.wait_ge(h_skvs, 1)
                        for s in range(2):
                            act.wait_ge(h_v_, s + 1)
                            nc.scalar.activation(vh[:, s, :, 0:D2], PS[:, 6 + s, :].rearrange("p (h d) -> p h d", d=D2), ACT.Copy,
                                                 scale=skv[:, s:s + 1]).then_inc(h_vs, 1)
                        for h in range(H2):
                            act.wait_ge(h_max, h + 1)
                            if h >= 2:
                                act.wait_ge(h_ou, h - 1)
                            nc.scalar.activation(ph[:, h % 2, :], PS[:, h % 2, 0:NKV + 1], ACT.Exp, bias=nmh[:, h:h + 1]).then_inc(h_p, 1)
                            act.wait_ge(h_pT, h + 1)
                            nc.scalar.activation(pTh[:, h % 2, :], PS[:, 2 + h % 2, 0:NKV], ACT.Copy).then_inc(h_pTs, 1)
                        act.wait_ge(h_oT, 1)
                        nc.scalar.activation(oaT[:, :, :].rearrange("p m s -> p (m s)"), PS[:, 6, :], ACT.Copy).then_inc(h_oTs, 1)
                        act.wait_ge(h_hv, 1)
                        nc.scalar.activation(hv[:, :], PS[:, 7, 0:E], ACT.Copy).then_inc(h_hvs, 1)

                    @block.vector
                    def _(dve):
                        chain = [0]

                        def link(ins):
                            chain[0] += 1
                            ins.then_inc(h_dve, 1)
                            dve.wait_ge(h_dve, chain[0])

                        nc.vector.tensor_copy(cols[:, :, :], slotT[:, :, :].rearrange("p t (r b) -> p t r b", r=2)[:, :, :, bass.ds(i, 1)].rearrange("p t r b -> p t (r b)"))
                        link(nc.vector.tensor_copy(scol[:, :, :], scoreT[:, :, :].rearrange("p t (r b) -> p t r b", r=2)[:, :, :, bass.ds(i, 1)].rearrange("p t r b -> p t (r b)")))
                        for t in range(T):
                            nc.vector.tensor_scalar(oh[:, t, 0:NQ], iota_r[:, 0:NQ], cols[:, t, 0:1], None, ALU.is_equal).then_inc(h_oh, 1)
                            nc.vector.tensor_scalar(oh[:, t, NQ:NSEL], iota_r[:, :], cols[:, t, 1:2], None, ALU.is_equal).then_inc(h_oh, 1)
                        dve.wait_ge(h_row, 16)
                        nc.vector.tensor_scalar(ohT[:, :], row[:, 0, :], iota_c[:, 0:1], None, ALU.is_equal).then_inc(h_oh, 1)
                        link(nc.vector.tensor_scalar(unch[:, :], cols[:, :, 0], 0.0, None, ALU.is_lt))
                        dve.wait_ge(h_skv, 1)
                        nc.vector.tensor_copy(skv[:, :], PS[:, 2, 0:2]).then_inc(h_skvs, 1)
                        dve.wait_ge(h_k_, 1)
                        nc.vector.tensor_copy(kh[:, :, 0:NKV], PS[:, 4:6, :].rearrange("p b (m s) -> p (b m) s", s=NKV)).then_inc(h_kc, 1)

                        def head_max(h):
                            dve.wait_ge(h_s, h + 1)
                            nc.vector.reduce_max(nmh[:, h:h + 1], PS[:, h % 2, 0:NKV + 1], AX.X, negate=True).then_inc(h_max, 1)

                        head_max(0)
                        for h in range(H2):
                            if h + 1 < H2:
                                head_max(h + 1)
                            dve.wait_ge(h_o, h + 1)
                            nc.vector.scalar_tensor_tensor(out=ou[:, h, :], in0=nv_b[:, h, :], scalar=ph[:, h % 2, NKV:NKV + 1],
                                                           in1=PS[:, 4 + h % 2, 0:W2H], op0=ALU.mult, op1=ALU.add).then_inc(h_ou, 1)
                        dve.wait_ge(h_ou, H2)
                        link(nc.vector.reciprocal(rech[:, :], ou[:, :, D2]))
                        nc.vector.tensor_tensor(oa[:, :].rearrange("p (h d) -> p h d", d=D2), ou[:, :, 0:D2],
                                                rech[:, :].rearrange("p (h a) -> p h a", a=1).broadcast_to([P, H2, D2]), ALU.mult).then_inc(h_oa, 1)
                        dve.wait_ge(h_light, 16)
                        for t in range(T):
                            dve.wait_ge(h_sc, 2 * (t // 2) + 2)
                            ins = nc.vector.scalar_tensor_tensor(out=f1[:, t, :], in0=PS[:, 4 + t // 2, E * (t % 2):E * (t % 2) + E],
                                                                 scalar=scol[:, t, 0:1], in1=light[:, 0, t, :], op0=ALU.mult, op1=ALU.add)
                            ins.then_inc(h_f, 1)
                        dve.wait_ge(h_f, T)
                        for t in range(T):
                            ins = nc.vector.scalar_tensor_tensor(out=f2[:, t, :], in0=nq_b[:, :], scalar=unch[:, t:t + 1],
                                                                 in1=f1[:, t, :], op0=ALU.mult, op1=ALU.add)
                        link(ins)
                        for t in range(T):
                            ins = nc.vector.bn_stats(st2[:, t, :], f2[:, t, :])
                        link(ins)
                        for t in range(T):
                            ins = nc.vector.bn_aggr(mv2[:, t, :], st2[:, t, :])
                        link(ins)
                        dve.sem_inc(h_var, 1)
                        dve.wait_ge(h_rstd, 1)
                        for t in range(T):
                            nc.vector.tensor_scalar(outb[:, 0, t, :], f2[:, t, :], mv2[:, t, 0:1], sc2[:, 1, t:t + 1],
                                                    ALU.subtract, ALU.mult).then_inc(h_y, 1)

                    @block.tensor
                    def _(pe):
                        pe.wait_ge(h_norm, 16)
                        pe.wait_ge(h_oh, 9)
                        for s in range(2):
                            for t in range(T):
                                ins = nc.tensor.matmul(PS[:, 2, s:s + 1], oh[:, t, NQ + s * P:NQ + (s + 1) * P], scol[:, t, 1:2],
                                                       start=t == 0, stop=t == T - 1)
                        ins.then_inc(h_skv, 1)
                        for c in range(C):
                            for t in range(T):
                                ins = nc.tensor.matmul(PS[:, c, 0:NSEL], norm[:, 0, t, c * P:(c + 1) * P], oh[:, t, :],
                                                       start=t == 0, stop=t == T - 1)
                            ins.then_inc(h_ga, 1)
                        pe.wait_ge(h_xs, C)
                        for m in range(M2):
                            for c in range(C):
                                ins = nc.tensor.matmul(PS[:, 3, m * NQ:(m + 1) * NQ], whq[:, c, m * P:(m + 1) * P], xsT[:, c, 0:NQ],
                                                       start=c == 0, stop=c == C - 1)
                        ins.then_inc(h_q_, 1)
                        for m in range(M2):
                            for c in range(C):
                                ins = nc.tensor.matmul(PS[:, 4 + m // 2, NKV * (m % 2):NKV * (m % 2) + NKV], whk[:, c, m * P:(m + 1) * P],
                                                       xsT[:, c, NQ:NSEL], start=c == 0, stop=c == C - 1)
                        ins.then_inc(h_k_, 1)
                        for s in range(2):
                            for c in range(C):
                                ins = nc.tensor.matmul(PS[:, 6 + s, :], xsT[:, c, NQ + s * P:NQ + (s + 1) * P], whv[:, c, :],
                                                       start=c == 0, stop=c == C - 1)
                            ins.then_inc(h_v_, 1)
                        pe.wait_ge(h_qs, 1)
                        pe.wait_ge(h_kc, 1)

                        def heavy_scores(h):
                            r, m = D2 * (h % 2), h // 2
                            if h >= 2:
                                pe.wait_ge(h_p, h - 1)
                            nc.tensor.matmul(PS[:, h % 2, 0:NKV + 1], qh[r:r + D2, m, :], kh[r:r + D2, m, :],
                                             start=True, stop=True).then_inc(h_s, 1)

                        heavy_scores(0)
                        for h in range(H2):
                            if h + 1 < H2:
                                heavy_scores(h + 1)
                            pe.wait_ge(h_p, h + 1)
                            if h == 0:
                                pe.wait_ge(h_skvs, 1)
                            for s in range(2):
                                ins = nc.tensor.transpose(PS[:, 2 + h % 2, s * P:(s + 1) * P], ph[:, h % 2, s * P:(s + 1) * P], ident[:, :])
                            ins.then_inc(h_pT, 1)
                            pe.wait_ge(h_pTs, h + 1)
                            if h == 0:
                                pe.wait_ge(h_vs, 2)
                            if h >= 2:
                                pe.wait_ge(h_ou, h - 1)
                            for s in range(2):
                                ins = nc.tensor.matmul(PS[:, 4 + h % 2, 0:W2H], pTh[:, h % 2, s * P:(s + 1) * P], vh[:, s, h, :],
                                                       start=s == 0, stop=s == 1)
                            ins.then_inc(h_o, 1)
                        pe.wait_ge(h_oa, 1)
                        for m in range(M2):
                            ins = nc.tensor.transpose(PS[:, 6, m * P:(m + 1) * P], oa[:, m * P:(m + 1) * P], ident[:, :])
                        ins.then_inc(h_oT, 1)
                        pe.wait_ge(h_oTs, 1)
                        for m in range(M2):
                            ins = nc.tensor.matmul(PS[:, 7, 0:E], oaT[:, m, :], who[:, m, :], start=m == 0, stop=m == M2 - 1)
                        ins.then_inc(h_hv, 1)
                        pe.wait_ge(h_hvs, 1)
                        for t in range(T):
                            nc.tensor.matmul(PS[:, 4 + t // 2, E * (t % 2):E * (t % 2) + E], ohT[:, t * P:(t + 1) * P], hv[:, :],
                                             start=True, stop=True).then_inc(h_sc, 1)
                nc.all_engine_barrier(sems_to_clear=range(step_sems2[0].num, step_sems2[-1].num + 1))


_INS = ["x", "xT", "wq", "wk", "wv", "wo", "aq", "ak", "av", "ao", "bq_", "bk_", "bv_", "bo_",
        "vec_q", "vec_k", "vec_v", "vec_o", "ln_w", "ln_b", "l_qk", "l_v", "l_out", "rt_q", "rt_kv",
        "gamma", "h_q", "h_k", "h_v", "h_out_w", "null_k", "null_v", "null_q"]


def kernel(**inputs):
    import numpy as _np
    import concourse.bacc as _bacc
    from concourse import mybir as _mybir
    from concourse.bass_utils import run_bass_kernel_spmd as _run

    def of(name):
        return _np.asarray(inputs["L0_" + name])

    x = of("attn_x")
    wqkv = of("ffn_Wqkv")
    wkv = of("ffn_Wkv").reshape(H2, 2, D2, E)
    laid = {
        "x": x, "xT": x.transpose(0, 2, 1),
        "ln_w": of("ffn_ln_w"), "ln_b": of("ffn_ln_b"), "gamma": of("ffn_gamma"),
        "l_qk": wqkv[:2 * IN2].T, "l_v": wqkv[2 * IN2:].T, "l_out": of("ffn_Wout_l").T,
        "rt_q": of("ffn_rt_q"), "rt_kv": of("ffn_rt_kv"),
        "h_q": of("ffn_Wq").T, "h_k": wkv[:, 0].reshape(IN2, E).T, "h_v": wkv[:, 1].reshape(IN2, E).T,
        "h_out_w": of("ffn_Wout_h").T, "null_k": of("ffn_null_kv")[0], "null_v": of("ffn_null_kv")[1],
        "null_q": of("ffn_null_q"),
    }
    for n in "qkvo":
        laid["w" + n] = of("attn_W" + n).T
        laid["b" + n + "_"] = of("attn_b" + n)
        laid["a" + n] = of("attn_A" + n)
        laid["vec_" + n] = of("attn_B" + n).T

    nc = _bacc.Bacc("TRN2", target_bir_lowering=False, num_devices=1)
    arrays, args = {}, []
    for name in _INS:
        a = _np.ascontiguousarray(laid[name])
        arrays[f"in_{name}_dram"] = a
        args.append(nc.dram_tensor(f"in_{name}_dram", a.shape, _mybir.dt.from_np(a.dtype), kind="ExternalInput").ap())
    out = nc.dram_tensor("out_0_dram", x.shape, _mybir.dt.float32, kind="ExternalOutput").ap()
    block_kernel(nc, *args, out)
    r = _run(nc, [arrays], core_ids=[0])
    return r.results[0]["out_0_dram"]
```

```python
import math
from contextlib import ExitStack

import concourse.bass as bass
from concourse import mybir

F32 = mybir.dt.float32
BF16 = mybir.dt.bfloat16
F32R = mybir.dt.float32r
HI, LO = 0, 1
ALU = mybir.AluOpType
ACT = mybir.ActivationFunctionType
AX = mybir.AxisListType

P = 128
NB = 32
S = 512
E = 256
T = S // P
C = E // P
H1, D1 = 16, 16
W1 = D1 + 1
W1H = 32
PV_BANK = 4
G1 = H1 // 4
RANK = 8
LORA = 16 / 8
H2, D2 = 8, 64
IN2 = H2 * D2
M2 = IN2 // P
W2H = D2 + 1
WIN = 64
NQ, NKV = 128, 256
NSEL = NQ + NKV
ITERS = 50
EPS_LN = 1e-5
DEEP = 96
SHIFT = 3
Q_PARTS = (0, 0, 0, 1, 1, 2)
K_PARTS = (0, 1, 2, 0, 1, 0)
LOWEST = -87.33654
NEG = -3.0e38


BY_ACT, BY_DVE = 0, 1

TAKEN_BY = {
    "tok": lambda name: BY_DVE, "aT": lambda name: BY_ACT, "y": lambda name: BY_DVE,
    "qk": lambda name: BY_ACT, "v": lambda name: BY_DVE, "rt": lambda name: BY_ACT, "xl": lambda name: BY_ACT,
    "lp": lambda name: int(name.split()[1]) % 2, "S": lambda name: BY_ACT, "T": lambda name: int(name.split()[1]) % 2,
    "O": lambda name: BY_DVE, "lo": lambda name: BY_ACT, "lz": lambda name: BY_DVE,
}


def tiles_of(m, k, has):
    names = []
    if "prev" in has:
        if m == 0:
            names.append(f"tok {k}")
        if m == 1 and k in (1, 2):
            names.append(f"aT {k - 1}")
        if (m, k) == (2, 0):
            names += ["y 0", "y 1"]
        if (m, k) == (3, 1):
            names.append("rt")
        if m == 3 and k >= 2:
            names.append(f"xl {k - 2}")
        if 4 <= m < 7 and (m, k) != (4, 0):
            names.append(f"lp {4 * (m - 4) + k - 1}")
        if (m, k) == (6, 3):
            names.append("lp 11")
        if m >= 8 and k == (1 if m == 15 else 2):
            names.append(f"O {m - 8}")
        if 7 <= m < 15:
            names.append(f"{'SSTT'[k]} {2 * (m - 7) + k % 2}")
        if (m, k) in ((10, 3), (12, 3), (14, 3), (15, 2)):
            names.append(f"lo {(m - 9) // 2}")
        if (m, k) == (15, 3):
            names += ["lz 0", "lz 1"]
    if "load" in has:
        for n, place in enumerate(((1, 0), (1, 3), (2, 1), (2, 2))):
            if (m, k) == place:
                names.append(f"qk {n}")
    if "next" in has:
        for n, place in enumerate(((2, 3), (3, 0))):
            if (m, k) == place:
                names.append(f"v {n}")
    return names


HEAVY_TILES = (
    ("ga 0 gather", "S 0 heads", "S 1 heads", "skv 0 gather", "ga 1 gather", "T 0 heads", "S 2 heads"),
    ("T 1 heads", "S 3 heads", "O 0 heads", "oT 0 final"),
    ("T 2 heads", "S 4 heads", "q 0 gather", "O 1 heads", "hv 0 final"),
    ("T 3 heads", "S 5 heads", "k 0 gather", "O 2 heads"),
    ("T 4 heads", "S 6 heads", "sc 0 final", "O 3 heads", "sc 1 final"),
    ("T 5 heads", "S 7 heads", "k 1 gather", "O 4 heads"),
    ("T 6 heads", "v 0 gather", "O 5 heads"),
    ("T 7 heads", "O 6 heads", "v 1 gather", "O 7 heads"),
)
HEAVY_TAKEN_BY = {"S": BY_ACT, "T": BY_ACT, "O": BY_DVE, "ga": BY_DVE, "skv": BY_DVE, "q": BY_DVE, "k": BY_DVE,
                  "v": BY_ACT, "oT": BY_DVE, "hv": BY_DVE, "sc": BY_DVE}
HEAVY_SPLIT = ("ga", "q", "k", "oT", "hv")


def heavy_tiles(step, has):
    named = [entry.split() for entry in HEAVY_TILES[step]]
    return [(kind, int(n)) for kind, n, piece in named if piece in has]


def seq(tensor, n):
    return tensor[n:n + 1, :, :] if isinstance(n, int) else tensor[bass.ds(n, 1), :, :]


def block_kernel(nc, x, xT, wq, wk, wv, wo, aq, ak, av, ao, bq_, bk_, bv_, bo_,
                 vec_q, vec_k, vec_v, vec_o, ln_w, ln_b, l_qk, l_v, l_out, rt_q, rt_kv,
                 gamma, h_q, h_k, h_v, h_out_w, null_k, null_v, null_q, out):
    ctx = ExitStack()
    with ctx:
        def sb(name, shape, dt=F32):
            return ctx.enter_context(nc.sbuf_tensor(name, shape, dt))

        def sem(name):
            return ctx.enter_context(nc.semaphore(name))

        def dram(name, shape, dt=F32):
            return nc.dram_tensor(name, shape, dt, kind="Internal").ap()

        parts_d = dram("parts_d", (2, 2, 3, C * P, S), BF16)
        norm_d = dram("norm_d", (NB, P, T * E))
        light_d = dram("light_d", (NB, P, T * E))
        route_d = dram("route_d", (NB, 2 * T, P))
        slot_d = dram("slot_d", (2 * NB, S))

        ident = sb("ident", [P, P])
        PS = ctx.enter_context(nc.psum_tensor("PS", [P, 8, 512], F32))

        w_q = sb("w_q", [P, C, E]); w_k = sb("w_k", [P, C, E])
        w_v = sb("w_v", [P, C, E]); w_o = sb("w_o", [P, C, E])
        b_q = sb("b_q", [P, C]); b_k = sb("b_k", [P, C])
        b_v = sb("b_v", [P, E]); b_o = sb("b_o", [P, E])
        lnw = sb("lnw", [P, C]); lnb = sb("lnb", [P, C]); gam = sb("gam", [P, C])
        rt = sb("rt", [P, 2, E])
        half = sb("half", [P, 4 * T])

        weights = [(w_q, wq, aq, vec_q), (w_k, wk, ak, vec_k), (w_v, wv, av, vec_v), (w_o, wo, ao, vec_o)]

        s_w = sem("s_w"); s_init = sem("s_init"); s_ident = sem("s_ident")
        s_lora = sem("s_lora"); s_lora_used = sem("s_lora_used"); s_ready = sem("s_ready"); s_wl = sem("s_wl")
        step_sems = []

        def step_sem(name):
            step_sems.append(sem(name))
            return step_sems[-1]

        s_xT = step_sem("s_xT"); s_x = step_sem("s_x"); s_xb = step_sem("s_xb")
        s_split = step_sem("s_split")
        s_parts = [step_sem(f"s_part{m}") for m in range(3)]
        s_stack = [step_sem(f"s_stack{g}") for g in range(G1)]
        s_s1 = step_sem("s_s1"); s_max = step_sem("s_max")
        s_shift = step_sem("s_shift")
        s_shift_in = [step_sem(f"s_shift_in{g}") for g in range(G1)]
        s_s2 = step_sem("s_s2"); s_p = step_sem("s_p")
        s_pv = step_sem("s_pv"); s_ot = step_sem("s_ot")
        c_full = step_sem("c_full")
        c_act = step_sem("c_act"); c_dve = step_sem("c_dve")
        s_var = step_sem("s_var"); s_rstd = step_sem("s_rstd"); s_x1 = step_sem("s_x1"); s_xn = step_sem("s_xn")
        s_xhi = step_sem("s_xhi"); s_xlo = step_sem("s_xlo")
        s_factor = step_sem("s_factor")
        s_rt = step_sem("s_rt"); s_lmax = step_sem("s_lmax"); s_vodd = step_sem("s_vodd")
        s_norm_out = step_sem("s_norm_out"); s_route_out = step_sem("s_route_out"); s_z_out = step_sem("s_z_out")
        s_pool = step_sem("s_pool"); s_dve = step_sem("s_dve")

        def pool_pow(out_ap, in_ap):
            return nc.gpsimd.tensor_tensor(out_ap, in_ap, half[:, 0:in_ap.shape[-1]], ALU.pow)

        def product(out_, a, b, start, stop):
            nc.tensor.matmul(out_, a(LO), b(HI), start=start, stop=False)
            nc.tensor.matmul(out_, a(HI), b(LO), start=False, stop=False)
            return nc.tensor.matmul(out_, a(HI), b(HI), start=False, stop=stop)

        with ExitStack() as c1:
            def sb1(name, shape, dt=F32):
                return c1.enter_context(nc.sbuf_tensor(name, shape, dt))
            lora_a = sb1("lora_a", [RANK, 4, E]); lora_b = sb1("lora_b", [RANK, 4, E])
            with nc.Block() as block:
                @block.sync
                def _(sp):
                    for n, (w, wt, a, bT) in enumerate(weights):
                        sp.dma_start(w[:, :, :], wt.rearrange("(c p) e -> p c e", p=P)).then_inc(s_w, 16)
                        sp.dma_start(lora_a[:, n, :], a).then_inc(s_w, 16)
                        sp.dma_start(lora_b[:, n, :], bT).then_inc(s_w, 16)
                    for dst, src in ((b_q, bq_), (b_k, bk_), (lnw, ln_w), (lnb, ln_b), (gam, gamma)):
                        sp.dma_start(dst[:, :], src.rearrange("(c p) -> p c", p=P),
                                     allow_slow_non_contiguous=True).then_inc(s_w, 16)
                    for dst, src in ((b_v, bv_), (b_o, bo_)):
                        sp.dma_start(dst[:, :], src.rearrange("(a e) -> a e", a=1).broadcast_to([P, E])).then_inc(s_w, 16)
                    sp.dma_start(rt[:, 0, :], rt_q.broadcast_to([P, E])).then_inc(s_w, 16)
                    sp.dma_start(rt[:, 1, :], rt_kv.broadcast_to([P, E])).then_inc(s_w, 16)

                @block.gpsimd
                def _(pool):
                    nc.gpsimd.memset(half[:, :], -0.5).then_inc(s_init, 1)
                    nc.gpsimd.memset(ident[:, :], 0.0).then_inc(s_ident, 1)
                    pool.wait_ge(s_ident, 1)
                    nc.gpsimd.affine_select(out=ident[:, :], in_=ident[:, :], compare_op=ALU.not_equal, fill=1.0,
                                            base=0, pattern=[[-1, P]], channel_multiplier=1).then_inc(s_ident, 1)

                @block.tensor
                def _(pe):
                    pe.wait_ge(s_w, 16 * 21)
                    for n in range(4):
                        for c in range(C):
                            nc.tensor.matmul(PS[:, n, c * E:(c + 1) * E], lora_a[:, n, c * P:(c + 1) * P],
                                             lora_b[:, n, :], start=True, stop=True).then_inc(s_lora, 1)

                @block.vector
                def _(dve):
                    for n, (w, _, _, _) in enumerate(weights):
                        dve.wait_ge(s_lora, C * (n + 1))
                        nc.vector.scalar_tensor_tensor(
                            out=w[:, :, :], in0=PS[:, n, :].rearrange("p (c e) -> p c e", c=C), scalar=LORA,
                            in1=w[:, :, :], op0=ALU.mult, op1=ALU.add).then_inc(s_lora_used, 1)
                    dve.wait_ge(s_lora_used, 4)
                    nc.vector.tensor_scalar(b_q[:, :], b_q[:, :], D1 ** -0.5, None, ALU.mult).then_inc(s_ready, 1)
                    dve.wait_ge(s_ready, 1)

        with ExitStack() as c1:
            def sb1(name, shape, dt=F32):
                return c1.enter_context(nc.sbuf_tensor(name, shape, dt))
            xT_s = [sb1(f"xT_s{n}", [P, C, S]) for n in range(2)]
            qk32 = sb1("qk32", [P, 2 * C, S])
            qs = [sb1(f"qs{n}", [DEEP + SHIFT, H1, S], BF16) for n in range(2)]
            ks = [sb1(f"ks{n}", [DEEP + SHIFT, H1, S], BF16) for n in range(2)]
            vx = [sb1(f"vx{n}", [P, T, H1, W1]) for n in range(2)]
            nmax = sb1("nmax", [P, H1 * T])
            shift = sb1("shift", [4 * T, 2, SHIFT, P], BF16)
            shift_r = sb1("shift_r", [4 * T, P])
            probs = sb1("probs", [P, 8, S])
            oT = sb1("oT", [P, G1, S])
            rec = sb1("rec", [P, T, H1])
            stats = sb1("stats", [P, T, 6]); mv = sb1("mv", [P, T, 2])
            sc = sb1("sc", [P, 8, T])
            x1 = sb1("x1", [P, T, E])
            xn = sb1("xn", [P, T, E])
            rs = sb1("rs", [P, 2, T])
            wl = sb1("wl", [P, 2, C, 3 * IN2], F32R); wlo = sb1("wlo", [P, M2, E])
            qkl = sb1("qkl", [P, 2 * M2, S])
            xlT = sb1("xlT", [P, 2, C, S], F32R)
            pl = sb1("pl", [P, T, 3 * WIN])
            vl = sb1("vl", [P, T, H2, W2H]); vodd = sb1("vodd", [WIN, T, H2, W2H])
            nml = sb1("nml", [P, H2, T])
            recl = sb1("recl", [P, H2, T])
            al = qk32
            alT = qkl[:, 0:M2, :]
            x_s = xn
            an = qkl[:, M2:M2 + 2, :].rearrange("p m (a e) -> p (m a) e", e=E)
            xl32 = oT[:, 2:4, :]
            rsT = oT[0:2 * T, 1, 0:P]
            rms = xn
            wl_in = probs[:, 0:6, :].rearrange("p n s -> p (n s)").rearrange("p (c e) -> p c e", c=C)
            y = x1; z = x1
            parts = pl[:, :, :].rearrange("p t c -> p (t c)").bitcast(BF16).rearrange("p (m s) -> p m s", m=3)
            aT = qkl[:, 0:C, :]
            pTl = xn
            junk = qkl[:, 0:M2, :].rearrange("p m (a e) -> p (m a) e", e=E)

            with nc.Block() as block:
                @block.scalar
                def _(act):
                    act.wait_ge(s_w, 16 * 25)
                    nc.scalar.activation(wl[:, HI, :, :], wl_in, ACT.Copy).then_inc(s_wl, 1)

                @block.sync
                def _(sp):
                    sp.dma_start(wl_in[:, :, 0:2 * IN2], l_qk.rearrange("(c p) e -> p c e", p=P)).then_inc(s_w, 16)
                    sp.dma_start(wl_in[:, :, 2 * IN2:], l_v.rearrange("(c p) e -> p c e", p=P)).then_inc(s_w, 16)
                    sp.dma_start(wlo[:, :, :], l_out.rearrange("(c p) e -> p c e", p=P)).then_inc(s_w, 16)
                    sp.dma_start(xT_s[0][:, :, :], xT[0, :, :].rearrange("(c p) s -> p c s", p=P)).then_inc(s_w, 16)
                    sp.wait_ge(s_w, 16 * 25)

                @block.vector
                def _(dve):
                    for n in range(2):
                        nc.vector.memset(vx[n][:, :, :, D1:W1], 1.0).then_inc(s_init, 1)
                        nc.vector.memset(ks[n][DEEP:DEEP + SHIFT, :, :], 1.0).then_inc(s_init, 1)
                    nc.vector.memset(vl[:, :, :, D2:W2H], 1.0).then_inc(s_init, 1)
                    nc.vector.memset(PS[:, PV_BANK, :], 0.0).then_inc(s_init, 1)
                    dve.wait_ge(s_init, 7)
                    dve.wait_ge(s_wl, 1)
                    nc.vector.tensor_tensor(wl[:, LO, :, :], wl_in, wl[:, HI, :, :], ALU.subtract)

            def run(phases):
                tiles, at = [], {}
                for f, (_, _, has) in enumerate(phases):
                    for m in range(16):
                        for k in range(4):
                            for name in tiles_of(m, k, has):
                                at[f, name] = len(tiles)
                                tiles.append(TAKEN_BY[name.split()[0]](name))

                def full(f, name):
                    return at[f, name] + 1

                def taken(f, name):
                    return at_place(at[f, name])

                def at_place(n):
                    return (c_act, c_dve)[tiles[n]], sum(t == tiles[n] for t in tiles[:n + 1])

                def bank(f, name):
                    return PS[:, 5 + at[f, name] % 3, :]

                def before(f, piece):
                    return sum(piece in has for _, _, has in phases[:f])

                def had(f, piece):
                    return f > 0 and piece in phases[f - 1][2]

                with nc.Block() as block:
                    @block.sync
                    def _(sp):
                        for f, (p, par, has) in enumerate(phases):
                            loads, nexts, curs, prevs = (before(f, piece) for piece in ("load", "next", "cur", "prev"))

                            def stack(group, to):
                                for n, (dst, which) in enumerate(((qs[to], Q_PARTS), (ks[to], K_PARTS))):
                                    for j, m in enumerate(which):
                                        sp.dma_start(dst[D1 * j:D1 * (j + 1), 4 * group:4 * group + 4, :],
                                                     parts_d[to, n, m, 4 * D1 * group:4 * D1 * (group + 1), :]
                                                     .rearrange("(h d) s -> d h s", d=D1)).then_inc(s_stack[group], 16)

                            def shifts(group, nexts=nexts, par=par):
                                sp.wait_ge(s_shift, 4 * nexts + group + 1)
                                for m in range(SHIFT):
                                    sp.dma_start(qs[1 - par][DEEP + m:DEEP + m + 1, 4 * group:4 * group + 4, :]
                                                 .rearrange("a h (t s) -> a (h t) s", t=T),
                                                 shift[:, group % 2, m, :]).then_inc(s_shift_in[group], 16)

                            def write_parts(n, loads=loads, par=par):
                                for m in range(3):
                                    sp.wait_ge(s_split, 3 * (4 * loads + n) + m + 1)
                                    sp.dma_start(parts_d[par, n // C, m, (n % C) * P:(n % C + 1) * P, :],
                                                 parts[:, m, :]).then_inc(s_parts[m], 16)

                            if "next" in has:
                                if had(f, "cur"):
                                    sp.wait_ge(s_s2, 64 * curs)
                                stack(3, 1 - par)
                            if "prev" in has:
                                if had(f, "prev"):
                                    sp.wait_ge(*taken(f - 1, "O 7"))
                                sp.dma_start(x_s[:, :, :], seq(x, p - 1).rearrange("a (t p) e -> p (a t) e", p=P)).then_inc(s_x, 16)
                            if "xT" in has:
                                if "next" in has:
                                    sp.wait_ge(c_full, full(f, "v 1"))
                                sp.dma_start(xT_s[1 - par][:, :, :], seq(xT, p + 3).rearrange("a (c p) s -> p (a c) s", p=P)).then_inc(s_xT, 16)
                            if "load" in has:
                                write_parts(0)
                            if "prev" in has:
                                sp.wait_ge(*taken(f, "rt"))
                                sp.dma_start(seq(route_d, p - 1).rearrange("a r s -> (a r) s"), rsT).then_inc(s_route_out, 16)
                            if "load" in has:
                                write_parts(1)
                            if "next" in has:
                                shifts(0)
                            if "load" in has:
                                write_parts(2)
                                write_parts(3)
                            if "prev" in has:
                                sp.wait_ge(s_xn, 2 * T * (prevs + 1))
                                sp.dma_start(seq(norm_d, p - 1).rearrange("a p e -> (a p) e"),
                                             rms[:, :, :].rearrange("p t e -> p (t e)")).then_inc(s_norm_out, 16)
                                for name in ("lp 10", "lp 11"):
                                    sp.wait_ge(*taken(f, name))
                                sp.dma_start(vodd[:, :, :, :], vl[WIN:P, :, :, :]).then_inc(s_vodd, 16)
                            if "next" in has:
                                shifts(1)
                            for group in range(3):
                                if "load" in has:
                                    if group == 0:
                                        for m in range(3):
                                            sp.wait_ge(s_parts[m], 64 * (loads + 1))
                                    if "cur" in has:
                                        sp.wait_ge(s_s2, 64 * curs + 16 * (group + 1))
                                    stack(group, par)
                            if "next" in has:
                                shifts(2)
                                shifts(3)
                            if "prev" in has:
                                sp.wait_ge(*taken(f, "lz 1"))
                                sp.dma_start(seq(light_d, p - 1).rearrange("a p e -> (a p) e"),
                                             z[:, :, :].rearrange("p t e -> p (t e)")).then_inc(s_z_out, 16)
                        n = len(phases)
                        for piece, s, each in (("prev", s_x, 16), ("prev", s_route_out, 16), ("prev", s_vodd, 16),
                                               ("prev", s_norm_out, 16), ("prev", s_z_out, 16), ("xT", s_xT, 16),
                                               *(("next", s, 48) for s in s_shift_in),
                                               *(("load", s, 192) for s in s_stack[:3]), ("next", s_stack[3], 192)):
                            if before(n, piece):
                                sp.wait_ge(s, each * before(n, piece))

                    @block.gpsimd
                    def _(pool):
                        chain = [0]

                        def link(ins):
                            chain[0] += 1
                            ins.then_inc(s_pool, 1)
                            pool.wait_ge(s_pool, chain[0])

                        for f, (p, par, has) in enumerate(phases):
                            loads, nexts, curs, prevs = (before(f, piece) for piece in ("load", "next", "cur", "prev"))

                            def split(n, f=f, loads=loads, has=has):
                                if "load" not in has:
                                    return
                                pool.wait_ge(*taken(f, f"qk {n}"))
                                chunks = 4 * loads + n

                                def gone(m):
                                    if chunks:
                                        pool.wait_ge(s_parts[m], 16 * chunks)

                                q = qk32[:, n, :]
                                gone(0)
                                link(nc.gpsimd.tensor_copy(parts[:, 0, :], q))
                                pool.sem_inc(s_split, 1)
                                link(nc.gpsimd.tensor_tensor(q, q, parts[:, 0, :], ALU.subtract))
                                gone(1)
                                link(nc.gpsimd.tensor_copy(parts[:, 1, :], q))
                                pool.sem_inc(s_split, 1)
                                gone(2)
                                nc.gpsimd.tensor_tensor(parts[:, 2, :], q, parts[:, 1, :], ALU.subtract).then_inc(s_split, 1)

                            if "prev" in has:
                                pool.wait_ge(s_x, 16 * (prevs + 1))
                                nc.gpsimd.tensor_tensor(x_s[:, :, :], x_s[:, :, :],
                                                        b_o[:, :].rearrange("p (a e) -> p a e", a=1).broadcast_to([P, T, E]),
                                                        ALU.add).then_inc(s_xb, 1)
                                pool.wait_ge(s_var, prevs + 1)
                                v = mv[:, :, 1]
                                link(nc.gpsimd.tensor_scalar(sc[:, 0, :], v, EPS_LN, None, ALU.add))
                                link(pool_pow(sc[:, 1, :], sc[:, 0, :]))
                                pool.sem_inc(s_rstd, 1)
                                link(nc.gpsimd.tensor_tensor(sc[:, 2, :], sc[:, 1, :], sc[:, 1, :], ALU.mult))
                                link(nc.gpsimd.tensor_tensor(sc[:, 3, :], sc[:, 2, :], v, ALU.mult))
                                link(nc.gpsimd.tensor_scalar(sc[:, 4, :], sc[:, 3, :], EPS_LN, None, ALU.add))
                                link(pool_pow(sc[:, 5, :], sc[:, 4, :]))
                                pool.sem_inc(s_factor, 1)
                                link(nc.gpsimd.tensor_scalar(sc[:, 6, :], sc[:, 3, :], 1e-24 / E, None, ALU.max))
                                link(pool_pow(sc[:, 7, :], sc[:, 6, :]))
                                pool.sem_inc(s_factor, 1)
                            for n in range(2 * C):
                                split(n)

                    @block.scalar
                    def _(act):
                        for f, (p, par, has) in enumerate(phases):
                            loads, nexts, curs, prevs = (before(f, piece) for piece in ("load", "next", "cur", "prev"))

                            def heads_out(hg, f=f, has=has, curs=curs, prevs=prevs):
                                act.wait_ge(s_pv, 16 * curs + 4 * hg + 4)
                                if hg == 0 and "prev" in has:
                                    act.wait_ge(c_full, full(f, "tok 3"))
                                if hg == 1 and "prev" in has:
                                    act.wait_ge(s_route_out, 16 * (prevs + 1))
                                nc.scalar.activation(oT[:, hg, :], PS[:, PV_BANK, :], ACT.Copy).then_inc(s_ot, 1)

                            for m in range(16):
                                for k in range(4):
                                    if "cur" in has:
                                        n = 64 * curs + 4 * m + k
                                        act.wait_ge(s_s2, n + 1)
                                        if n >= 8:
                                            act.wait_ge(s_pv, (n - 8) // 4 + 1)
                                        nc.scalar.activation(probs[:, n % 8, :], PS[:, 2 + n % 2, :], ACT.Exp).then_inc(s_p, 1)
                                        if k == 2 and m and m % 4 == 0:
                                            heads_out(m // 4 - 1)
                                    for name in tiles_of(m, k, has):
                                        kind, n = name.split()[0], int((name + " 0").split()[1])
                                        b = bank(f, name)
                                        if kind == "S":
                                            h, j = n // 2, 2 * (n % 2)
                                            act.wait_ge(s_lmax, 16 * prevs + n + 1)
                                            if n == 0 and "load" in has:
                                                for part in s_parts:
                                                    act.wait_ge(part, 64 * (loads + 1))
                                            nc.scalar.activation(pl[:, j, :], b[:, 0:3 * WIN], ACT.Exp, bias=nml[:, h, j:j + 1])
                                            nc.scalar.activation(pl[:, j + 1, :], b[:, 256:256 + 3 * WIN], ACT.Exp,
                                                                 bias=nml[:, h, j + 1:j + 2]).then_inc(c_act, 1)
                                            continue
                                        if TAKEN_BY[kind](name) != BY_ACT:
                                            continue
                                        act.wait_ge(c_full, full(f, name))
                                        if kind == "aT":
                                            ins = nc.scalar.activation(aT[:, n, :], b, ACT.Copy)
                                        elif kind == "qk":
                                            ins = nc.scalar.activation(qk32[:, n, :], b, ACT.Identity,
                                                                       bias=(b_q, b_k)[n // C][:, n % C:n % C + 1],
                                                                       scale=D1 ** -0.5 if n < C else 1.0)
                                        elif kind == "rt":
                                            if prevs:
                                                act.wait_ge(s_route_out, 16 * prevs)
                                            ins = nc.scalar.activation(rsT, b[0:2 * T, 0:P], ACT.Copy)
                                        elif kind == "xl":
                                            nc.scalar.activation(xl32[:, n, :], b, ACT.Identity,
                                                                 bias=lnb[:, n:n + 1], scale=lnw[:, n:n + 1]).then_inc(c_act, 1)
                                            act.wait_ge(*taken(f, name))
                                            nc.scalar.activation(xlT[:, HI, n, :], xl32[:, n, :], ACT.Copy).then_inc(s_xhi, 1)
                                            continue
                                        elif kind == "lp" and n < 2 * M2:
                                            ins = nc.scalar.activation(qkl[:, n, :], b, ACT.Copy,
                                                                       scale=D2 ** -0.5 if n < M2 else 1.0)
                                        elif kind == "lp":
                                            if prevs:
                                                act.wait_ge(s_vodd, 16 * prevs)
                                            ins = nc.scalar.activation(vl[:, n - 2 * M2, :, 0:D2],
                                                                       b.rearrange("p (h d) -> p h d", d=D2), ACT.Copy)
                                        elif kind == "T":
                                            j = 2 * (n % 2)
                                            if n == 0:
                                                act.wait_ge(s_norm_out, 16 * (prevs + 1))
                                            ins = nc.scalar.activation(pTl[:, j:j + 2, :].rearrange("p j c -> p (j c)"), b, ACT.Copy)
                                        elif kind == "lo":
                                            ins = nc.scalar.activation(alT[:, n, :], b, ACT.Copy)
                                        ins.then_inc(c_act, 1)
                                    if "prev" in has and (m, k) == (3, 0):
                                        act.wait_ge(s_x1, T * (prevs + 1))
                                        act.wait_ge(s_factor, 2 * prevs + 1)
                                        for t in range(T):
                                            nc.scalar.activation(xn[:, t, :], x1[:, t, :], ACT.Copy,
                                                                 scale=sc[:, 5, t:t + 1]).then_inc(s_xn, 1)
                                    if "prev" in has and (m, k) in ((4, 2), (4, 3), (5, 0), (5, 1)):
                                        act.wait_ge(s_xn, 2 * T * prevs + T)
                                        act.wait_ge(c_full, full(f, "xl 1"))
                                        act.wait_ge(s_factor, 2 * prevs + 2)
                                        t = (k + 2) % 4
                                        nc.scalar.activation(rms[:, t, :], x1[:, t, :], ACT.Copy,
                                                             scale=sc[:, 7, t:t + 1]).then_inc(s_xn, 1)
                            if "cur" in has:
                                heads_out(3)

                    @block.vector
                    def _(dve):
                        chain = [0]

                        def link(ins):
                            chain[0] += 1
                            ins.then_inc(s_dve, 1)
                            dve.wait_ge(s_dve, chain[0])

                        for f, (p, par, has) in enumerate(phases):
                            loads, nexts, curs, prevs = (before(f, piece) for piece in ("load", "next", "cur", "prev"))

                            def parts_of_max(hg, nexts=nexts):
                                n = 68 * nexts + 17 * hg + 16
                                dve.wait_ge(s_s1, n + 1)
                                if hg >= 2:
                                    dve.wait_ge(s_shift_in[hg - 2], 48 * (nexts + 1))
                                elif nexts:
                                    dve.wait_ge(s_shift_in[hg + 2], 48 * nexts)
                                rows = PS[0:4 * T, n % 2, 0:P]
                                link(nc.vector.tensor_copy(shift[:, hg % 2, 0, :], rows))
                                nc.vector.tensor_tensor(shift_r[:, :], rows, shift[:, hg % 2, 0, :], ALU.subtract).then_inc(s_max, 1)
                                dve.wait_ge(s_max, n + 1)
                                link(nc.vector.tensor_copy(shift[:, hg % 2, 1, :], shift_r[:, :]))
                                nc.vector.tensor_tensor(shift[:, hg % 2, 2, :], shift_r[:, :], shift[:, hg % 2, 1, :],
                                                        ALU.subtract).then_inc(s_shift, 1)

                            for m in range(16):
                                for k in range(4):
                                    if "next" in has:
                                        u = 4 * m + k
                                        if u % 16 == 0 and u:
                                            parts_of_max(u // 16 - 1)
                                        n = 68 * nexts + u + u // 16
                                        dve.wait_ge(s_s1, n + 1)
                                        nc.vector.reduce_max(nmax[:, u:u + 1], PS[:, n % 2, :], AX.X, negate=True).then_inc(s_max, 1)
                                    for name in tiles_of(m, k, has):
                                        kind, n = name.split()[0], int((name + " 0").split()[1])
                                        b = bank(f, name)
                                        if kind == "S":
                                            h, j = n // 2, 2 * (n % 2)
                                            dve.wait_ge(c_full, full(f, name))
                                            nc.vector.reduce_max(nml[:, h, j:j + 2],
                                                                 b.rearrange("p (j c) -> p j c", j=2)[:, :, 0:3 * WIN],
                                                                 AX.X, negate=True).then_inc(s_lmax, 1)
                                            continue
                                        if TAKEN_BY[kind](name) != BY_DVE:
                                            continue
                                        dve.wait_ge(c_full, full(f, name))
                                        if kind == "tok":
                                            o = b.rearrange("p (h d) -> p h d", d=W1H)
                                            link(nc.vector.reciprocal(rec[:, n, :], o[:, :, D1]))
                                            ins = nc.vector.tensor_tensor(
                                                an[:, n, :].rearrange("p (h d) -> p h d", d=D1), o[:, :, 0:D1],
                                                rec[:, n, :].rearrange("p (h a) -> p h a", a=1).broadcast_to([P, H1, D1]), ALU.mult)
                                        elif kind == "y":
                                            if n == 0:
                                                dve.wait_ge(s_xb, prevs + 1)
                                                if prevs:
                                                    dve.wait_ge(s_xn, 2 * T * prevs)
                                                if prevs:
                                                    dve.wait_ge(s_z_out, 16 * prevs)
                                            ins = nc.vector.tensor_tensor(y[:, 2 * n:2 * n + 2, :], b.rearrange("p (t e) -> p t e", e=E),
                                                                          x_s[:, 2 * n:2 * n + 2, :], ALU.add)
                                        elif kind == "v":
                                            ins = nc.vector.tensor_tensor(
                                                vx[1 - par][:, 2 * n:2 * n + 2, :, 0:D1],
                                                b.rearrange("p (t h d) -> p t h d", t=2, d=D1),
                                                b_v[:, :].rearrange("p (a h d) -> p a h d", a=1, d=D1).broadcast_to([P, 2, H1, D1]),
                                                ALU.add)
                                        elif kind == "lp" and n < 2 * M2:
                                            ins = nc.vector.tensor_scalar(qkl[:, n, :], b, D2 ** -0.5 if n < M2 else 1.0, None, ALU.mult)
                                        elif kind == "lp":
                                            if prevs:
                                                dve.wait_ge(s_vodd, 16 * prevs)
                                            ins = nc.vector.tensor_copy(vl[:, n - 2 * M2, :, 0:D2], b.rearrange("p (h d) -> p h d", d=D2))
                                        elif kind == "T":
                                            j = 2 * (n % 2)
                                            if n == 1:
                                                dve.wait_ge(s_norm_out, 16 * (prevs + 1))
                                            ins = nc.vector.tensor_copy(pTl[:, j:j + 2, :].rearrange("p j c -> p (j c)"), b)
                                        elif kind == "O":
                                            if n == 0 and "load" in has:
                                                dve.wait_ge(s_split, 12 * (loads + 1))
                                            o = b[:, 0:T * W2H].rearrange("p (t d) -> p t d", d=W2H)
                                            link(nc.vector.reciprocal(recl[:, n, :], o[:, :, D2]))
                                            ins = nc.vector.tensor_tensor(
                                                al[:, :, n * D2:(n + 1) * D2], o[:, :, 0:D2],
                                                recl[:, n, :].rearrange("p (t a) -> p t a", a=1).broadcast_to([P, T, D2]), ALU.mult)
                                        elif kind == "lz":
                                            dve.wait_ge(s_xn, 2 * T * (prevs + 1))
                                            ins = nc.vector.tensor_tensor(z[:, 2 * n:2 * n + 2, :], b.rearrange("p (t e) -> p t e", e=E),
                                                                          x1[:, 2 * n:2 * n + 2, :], ALU.add)
                                        ins.then_inc(c_dve, 1)
                                    if "prev" in has and (m, k) in ((3, 3), (4, 0)):
                                        n = m - 3
                                        dve.wait_ge(s_xhi, 2 * prevs + n + 1)
                                        nc.vector.tensor_tensor(xlT[:, LO, n, :], xl32[:, n, :], xlT[:, HI, n, :],
                                                                ALU.subtract).then_inc(s_xlo, 1)
                                    if "prev" in has and (m, k) == (2, 0):
                                        dve.wait_ge(*taken(f, "y 1"))
                                        for t in range(T):
                                            ins = nc.vector.bn_stats(stats[:, t, :], y[:, t, :])
                                        link(ins)
                                        for t in range(T):
                                            ins = nc.vector.bn_aggr(mv[:, t, :], stats[:, t, :])
                                        ins.then_inc(s_var, 1)
                                    if "prev" in has and (m, k) == (2, 2):
                                        dve.wait_ge(s_rstd, prevs + 1)
                                        dve.wait_ge(s_var, prevs + 1)
                                        for t in range(T):
                                            nc.vector.tensor_scalar(x1[:, t, :], y[:, t, :], mv[:, t, 0:1], sc[:, 1, t:t + 1],
                                                                    ALU.subtract, ALU.mult).then_inc(s_x1, 1)
                                    if "prev" in has and (m, k) == (2, 3):
                                        dve.wait_ge(s_x1, T * (prevs + 1))
                                        for r in range(2):
                                            for t in range(T):
                                                ins = nc.vector.tensor_tensor_reduce(
                                                    out=junk[:, T * r + t, :], in0=x1[:, t, :], in1=rt[:, r, :], scale=1.0, scalar=0.0,
                                                    op0=ALU.mult, op1=ALU.add, accum_out=rs[:, r, t:t + 1])
                                        ins.then_inc(s_rt, 1)
                            if "next" in has:
                                parts_of_max(3)

                    @block.tensor
                    def _(pe):
                        for f, (p, par, has) in enumerate(phases):
                            loads, nexts, curs, prevs = (before(f, piece) for piece in ("load", "next", "cur", "prev"))

                            def max_rows(hg, nexts=nexts):
                                n = 68 * nexts + 17 * hg + 16
                                pe.wait_ge(s_max, n)
                                nc.tensor.transpose(PS[0:4 * T, n % 2, 0:P], nmax[:, 4 * T * hg:4 * T * (hg + 1)],
                                                    ident[:, :]).then_inc(s_s1, 1)

                            def values(m, f=f, par=par, curs=curs):
                                hg, t = m // 4, m % 4
                                pe.wait_ge(s_p, 64 * curs + 4 * m + 4)
                                if t == 0 and (curs or hg):
                                    pe.wait_ge(s_ot, 4 * curs + hg)
                                if m == 0 and had(f, "next"):
                                    pe.wait_ge(*taken(f - 1, "v 1"))
                                for r in range(4):
                                    ins = nc.tensor.matmul(PS[32 * r:32 * r + W1, PV_BANK, :], vx[par][:, t, 4 * hg + r, :],
                                                           probs[:, (4 * m + r) % 8, :], start=t == 0, stop=t == T - 1)
                                ins.then_inc(s_pv, 1)

                            def tile(name, f=f, par=par, curs=curs, prevs=prevs):
                                kind, n = name.split()[0], int((name + " 0").split()[1])
                                b, place = bank(f, name), at[f, name]
                                if place >= 3:
                                    pe.wait_ge(*at_place(place - 3))
                                if kind == "tok":
                                    if curs:
                                        pe.wait_ge(s_ot, 4 * curs)
                                    for g in range(G1):
                                        ins = nc.tensor.transpose(b[:, g * P:(g + 1) * P], oT[:, g, n * P:(n + 1) * P], ident[:, :])
                                elif kind == "aT":
                                    pe.wait_ge(*taken(f, "tok 3"))
                                    for t in range(T):
                                        ins = nc.tensor.transpose(b[:, t * P:(t + 1) * P], an[:, t, n * P:(n + 1) * P], ident[:, :])
                                elif kind == "y":
                                    pe.wait_ge(*taken(f, "aT 1"))
                                    for t in (2 * n, 2 * n + 1):
                                        for c in range(C):
                                            ins = nc.tensor.matmul(b[:, E * (t % 2):E * (t % 2) + E], aT[:, c, t * P:(t + 1) * P],
                                                                   w_o[:, c, :], start=c == 0, stop=c == C - 1)
                                elif kind == "qk":
                                    if before(f, "xT"):
                                        pe.wait_ge(s_xT, 16 * before(f, "xT"))
                                    for c in range(C):
                                        ins = nc.tensor.matmul(b, (w_q, w_k)[n // C][:, c, (n % C) * P:(n % C + 1) * P],
                                                               xT_s[par][:, c, :], start=c == 0, stop=c == C - 1)
                                elif kind == "v":
                                    for t in (2 * n, 2 * n + 1):
                                        for c in range(C):
                                            ins = nc.tensor.matmul(b[:, E * (t % 2):E * (t % 2) + E],
                                                                   xT_s[1 - par][:, c, t * P:(t + 1) * P], w_v[:, c, :],
                                                                   start=c == 0, stop=c == C - 1)
                                elif kind == "rt":
                                    pe.wait_ge(s_rt, prevs + 1)
                                    ins = nc.tensor.transpose(b[0:2 * T, 0:P], rs[:, :, :].rearrange("p r t -> p (r t)"), ident[:, :])
                                elif kind == "xl":
                                    pe.wait_ge(s_xn, 2 * T * prevs + T)
                                    for t in range(T):
                                        ins = nc.tensor.transpose(b[:, t * P:(t + 1) * P], xn[:, t, n * P:(n + 1) * P], ident[:, :])
                                elif kind == "lp" and n < 2 * M2:
                                    pe.wait_ge(s_xlo, 2 * (prevs + 1))
                                    for c in range(C):
                                        ins = product(b, lambda part: wl[:, part, c, n * P:(n + 1) * P],
                                                      lambda part: xlT[:, part, c, :], c == 0, c == C - 1)
                                elif kind == "lp":
                                    t = n - 2 * M2
                                    for c in range(C):
                                        ins = product(b, lambda part: xlT[:, part, c, t * P:(t + 1) * P],
                                                      lambda part: wl[:, part, c, 2 * IN2:], c == 0, c == C - 1)
                                elif kind == "S":
                                    h, half_ = n // 2, n % 2
                                    if n == 0:
                                        pe.wait_ge(*taken(f, "lp 10"))
                                        pe.wait_ge(*taken(f, "lp 11"))
                                    r, m = D2 * (h % 2), h // 2
                                    q, k = qkl[r:r + D2, m, :], qkl[r:r + D2, M2 + m, :]
                                    for j in (2 * half_, 2 * half_ + 1):
                                        o = b[:, 256 * (j % 2):256 * (j % 2) + 3 * WIN]
                                        left, right = max(2 * j - 1, 0), min(2 * j + 2, 2 * T - 1)
                                        nc.tensor.matmul(o[0:WIN, 0:WIN], q[:, 2 * j * WIN:(2 * j + 1) * WIN],
                                                         k[:, left * WIN:(left + 1) * WIN], start=True, stop=True)
                                        nc.tensor.matmul(o[WIN:P, 0:WIN], q[:, (2 * j + 1) * WIN:(2 * j + 2) * WIN],
                                                         k[:, right * WIN:(right + 1) * WIN], start=True, stop=True)
                                        ins = nc.tensor.matmul(o[:, WIN:3 * WIN], q[:, j * P:(j + 1) * P], k[:, j * P:(j + 1) * P],
                                                               start=True, stop=True)
                                elif kind == "T":
                                    pe.wait_ge(*taken(f, f"S {n}"))
                                    for j in range(2):
                                        src = pl[:, 2 * (n % 2) + j, :]
                                        nc.tensor.transpose(b[:, 256 * j:256 * j + P], src[:, WIN:3 * WIN], ident[:, :])
                                        ins = nc.tensor.transpose(b[0:WIN, 256 * j + P:256 * j + 2 * P], src[:, 0:WIN], ident[:, :])
                                elif kind == "O":
                                    pe.wait_ge(*taken(f, f"T {2 * n}"))
                                    pe.wait_ge(*taken(f, f"T {2 * n + 1}"))
                                    if n == 0:
                                        pe.wait_ge(s_vodd, 16 * (prevs + 1))
                                    for j in range(T):
                                        o = b[:, j * W2H:(j + 1) * W2H]
                                        pT = pTl[:, j, :]
                                        ins = nc.tensor.matmul(o, pT[:, 0:P], vl[:, j, n, :], start=True, stop=False, skip_group_check=True)
                                        if j > 0:
                                            ins = nc.tensor.matmul(o[0:WIN, :], pT[0:WIN, P:P + WIN], vodd[:, j - 1, n, :],
                                                                   start=False, stop=True, skip_group_check=True)
                                        if j < T - 1:
                                            ins = nc.tensor.matmul(o[WIN:P, :], pT[0:WIN, P + WIN:2 * P], vl[0:WIN, j + 1, n, :],
                                                                   start=False, stop=True, skip_group_check=True)
                                elif kind == "lo":
                                    pe.wait_ge(*taken(f, f"O {2 * n + 1}"))
                                    for t in range(T):
                                        ins = nc.tensor.transpose(b[:, t * P:(t + 1) * P], al[:, t, n * P:(n + 1) * P], ident[:, :])
                                elif kind == "lz":
                                    pe.wait_ge(*taken(f, "lo 3"))
                                    for t in (2 * n, 2 * n + 1):
                                        for m in range(M2):
                                            ins = nc.tensor.matmul(b[:, E * (t % 2):E * (t % 2) + E], alT[:, m, t * P:(t + 1) * P],
                                                                   wlo[:, m, :], start=m == 0, stop=m == M2 - 1)
                                ins.then_inc(c_full, 1)

                            for m in range(16):
                                for k in range(4):
                                    u = 4 * m + k
                                    if "cur" in has:
                                        n = 64 * curs + u
                                        h, t = 4 * (u // 16) + u % 4, (u // 4) % 4
                                        if u % 16 == 0 and nexts:
                                            pe.wait_ge(s_shift_in[u // 16], 48 * nexts)
                                        if n >= 2:
                                            pe.wait_ge(s_p, n - 1)
                                        nc.tensor.matmul(PS[:, 2 + n % 2, :], ks[par][:, h, t * P:(t + 1) * P], qs[par][:, h, :],
                                                         start=True, stop=True).then_inc(s_s2, 1)
                                    if "next" in has:
                                        if u % 16 == 0:
                                            if u:
                                                max_rows(u // 16 - 1)
                                            landed = nexts + 1 if u == 48 else loads
                                            if landed:
                                                pe.wait_ge(s_stack[u // 16], 192 * landed)
                                        n = 68 * nexts + u + u // 16
                                        h, t = u // T, u % T
                                        if n >= 2:
                                            pe.wait_ge(s_max, n - 1)
                                        nc.tensor.matmul(PS[:, n % 2, :], qs[1 - par][0:DEEP, h, t * P:(t + 1) * P],
                                                         ks[1 - par][0:DEEP, h, :], start=True, stop=True).then_inc(s_s1, 1)
                                    if "cur" in has and k == 1 and m:
                                        values(m - 1)
                                    for name in tiles_of(m, k, has):
                                        tile(name)
                            if "cur" in has:
                                values(15)
                            if "next" in has:
                                max_rows(3)
                nc.all_engine_barrier(sems_to_clear=range(step_sems[0].num, step_sems[-1].num + 1))

            full_phase = ("load", "next", "cur", "prev", "xT")
            run([(-2, 0, ("load", "xT")), (-1, 1, ("load", "next", "xT")),
                 (0, 0, ("load", "next", "cur", "xT")), (1, 1, full_phase)])
            with nc.Fori(2, NB - 11, 6) as i:
                run([(i + j, j % 2, full_phase) for j in range(6)])
            run([(NB - 6, 0, full_phase), (NB - 5, 1, full_phase), (NB - 4, 0, full_phase), (NB - 3, 1, full_phase[:-1]),
                 (NB - 2, 0, ("next", "cur", "prev")), (NB - 1, 1, ("cur", "prev")), (NB, 0, ("prev",))])

        slotT = sb("slotT", [P, T, 2 * NB]); scoreT = sb("scoreT", [P, T, 2 * NB])
        r_in = sem("r_in"); r_init = sem("r_init"); r_t = sem("r_t"); r_e = sem("r_e"); r_l = sem("r_l"); r_a = sem("r_a")
        r_dve = sem("r_dve"); r_score = sem("r_score"); r_T = sem("r_T"); r_end = sem("r_end"); r_slot = sem("r_slot")
        r_top = sem("r_top"); r_key = sem("r_key")
        R = 2 * NB
        with ExitStack() as c2:
            def sb2(name, shape, dt=F32):
                return c2.enter_context(nc.sbuf_tensor(name, shape, dt))
            s_r = sb2("s_r", [R, S]); low = sb2("low", [R, S]); e_r = sb2("e_r", [R, S])
            one = sb2("one", [R, S]); key = sb2("key", [R, S]); work = sb2("work", [R, 2, S])
            gt = sb2("gt", [R, S]); eq = sb2("eq", [R, S]); cum = sb2("cum", [R, S]); mask = sb2("mask", [R, S])
            slot = sb2("slot", [R, S]); score = sb2("score", [R, S]); inv = sb2("inv", [R, S])
            top = sb2("top", [R, 2, 8])
            logk = sb2("logk", [R, 1]); room = sb2("room", [R, 1]); kk = sb2("kk", [R, 1]); thr = sb2("thr", [R, 1])
            smax = sb2("smax", [R, 1]); na = sb2("na", [R, 1]); nm = sb2("nm", [R, 1]); se = sb2("se", [R, 1])
            ln = sb2("ln", [R, 1]); cnt = sb2("cnt", [R, 1])
            with nc.Block() as block:
                @block.sync
                def _(sp):
                    for r in range(2):
                        sp.dma_start(s_r[r * NB:(r + 1) * NB, :],
                                     route_d[:, r * T:(r + 1) * T, :].rearrange("b t s -> b (t s)")).then_inc(r_in, 16)
                    sp.wait_ge(r_slot, 1)
                    sp.dma_start(slot_d, slot[:, :]).then_inc(r_end, 16)
                    sp.wait_ge(r_end, 16)

                @block.scalar
                def _(act):
                    nc.scalar.preload_act_table_set("natural_log_exp_and_others")
                    with act.Fori(0, ITERS - 1) as i:
                        act.wait_ge(r_t, i * 2 + 2)
                        nc.scalar.activation(e_r[:, :], low[:, :], ACT.Exp, bias=nm[:, 0:1], accum_out=se[:, 0:1]).then_inc(r_e, 1)
                        act.wait_ge(r_e, i + 1)
                        nc.scalar.activation(ln[:, :], se[:, :], ACT.Ln).then_inc(r_l, 1)
                    act.wait_ge(r_key, 1)
                    nc.scalar.activation(score[:, :], low[:, :], ACT.Exp).then_inc(r_score, 1)

                @block.vector
                def _(dve):
                    n_dve = [0]

                    def link(ins):
                        n_dve[0] += 1
                        ins.then_inc(r_dve, 1)
                        dve.wait_ge(r_dve, n_dve[0])

                    for r, k in ((0, NQ), (NB, NKV)):
                        nc.vector.memset(logk[r:r + NB, :], math.log(min(k * 9.0 / 8.0, S))).then_inc(r_init, 1)
                        nc.vector.memset(kk[r:r + NB, :], float(k)).then_inc(r_init, 1)
                        nc.vector.memset(na[r:r + NB, :], math.log(S) - math.log(min(k * 9.0 / 8.0, S))).then_inc(r_init, 1)
                    nc.vector.memset(one[:, :], 1.0).then_inc(r_init, 1)
                    dve.wait_ge(r_init, 7)
                    dve.wait_ge(r_in, 32)
                    link(nc.vector.reduce_max(smax[:, :], s_r[:, :], AX.X))
                    with dve.Fori(0, ITERS - 1) as i:
                        nc.vector.tensor_scalar(low[:, :], s_r[:, :], na[:, 0:1], None, ALU.min).then_inc(r_t, 1)
                        nc.vector.tensor_scalar(nm[:, :], smax[:, :], na[:, 0:1], -1.0, ALU.min, ALU.mult).then_inc(r_t, 1)
                        dve.wait_ge(r_l, i + 1)
                        nc.vector.tensor_scalar(na[:, :], ln[:, :], nm[:, 0:1], logk[:, 0:1], ALU.subtract,
                                                ALU.subtract).then_inc(r_a, 1)
                        dve.wait_ge(r_a, i + 1)
                    link(nc.vector.tensor_scalar(low[:, :], s_r[:, :], na[:, 0:1], 0.0, ALU.subtract, ALU.min))
                    dve.sem_inc(r_key, 1)
                    link(nc.vector.scalar_tensor_tensor(out=key[:, :], in0=low[:, :], scalar=-2.98e-8, in1=low[:, :],
                                                        op0=ALU.is_lt, op1=ALU.mult))
                    link(nc.vector.tensor_scalar(work[:, 0, :], key[:, :], LOWEST, None, ALU.max))
                    link(nc.vector.tensor_copy(key[:, :], work[:, 0, :]))
                    for half_, rows in enumerate((slice(0, NB), slice(NB, R))):
                        for i in range(NQ // 16):
                            for n in range(2):
                                done = (half_ * (NQ // 16) + i) * 4 + 2 * n
                                nc.vector.max(top[:, n, :], work[:, n, :]).then_inc(r_top, 1)
                                dve.wait_ge(r_top, done + 1)
                                nc.vector.match_replace(work[:, 1 - n, :], top[:, n, :], work[:, n, :], NEG).then_inc(r_top, 1)
                                dve.wait_ge(r_top, done + 2)
                        link(nc.vector.tensor_copy(thr[rows, :], top[rows, 1, 7:8]))
                    nc.vector.tensor_scalar(gt[:, :], key[:, :], thr[:, 0:1], None, ALU.is_gt)
                    link(nc.vector.tensor_scalar(eq[:, :], key[:, :], thr[:, 0:1], None, ALU.is_equal))
                    link(nc.vector.reduce_sum(cnt[:, :], gt[:, :], AX.X))
                    link(nc.vector.tensor_tensor_scan(cum[:, :], one[:, :], eq[:, :], 0.0, ALU.mult, ALU.add))
                    link(nc.vector.tensor_tensor(room[:, :], kk[:, :], cnt[:, :], ALU.subtract))
                    link(nc.vector.scalar_tensor_tensor(out=mask[:, :], in0=cum[:, :], scalar=room[:, 0:1], in1=eq[:, :],
                                                        op0=ALU.is_le, op1=ALU.mult))
                    link(nc.vector.tensor_tensor(eq[:, :], mask[:, :], gt[:, :], ALU.add))
                    link(nc.vector.tensor_tensor_scan(cum[:, :], one[:, :], eq[:, :], 0.0, ALU.mult, ALU.add))
                    link(nc.vector.tensor_tensor(gt[:, :], cum[:, :], eq[:, :], ALU.mult))
                    nc.vector.tensor_scalar(slot[:, :], gt[:, :], -1.0, None, ALU.add).then_inc(r_slot, 1)
                    dve.wait_ge(r_score, 1)
                    link(nc.vector.tensor_scalar(inv[:, :], score[:, :], -1.0, 1.0, ALU.mult, ALU.add))
                    nc.vector.tensor_tensor(work[:, 0, :], inv[:, :], score[:, :], ALU.add).then_inc(r_slot, 1)
                    dve.wait_ge(r_T, 2 * T)
                    nc.vector.tensor_copy(slotT[:, :, :].rearrange("p t r -> p (t r)"), PS[:, 0, 0:T * R])
                    link(nc.vector.tensor_copy(scoreT[:, :, :].rearrange("p t r -> p (t r)"), PS[:, 1, 0:T * R]))

                @block.tensor
                def _(pe):
                    pe.wait_ge(r_slot, 2)
                    for n, src in enumerate((slot[:, :], work[:, 0, :])):
                        for t in range(T):
                            nc.tensor.transpose(PS[:, n, t * R:(t + 1) * R], src[:, t * P:(t + 1) * P],
                                                ident[0:R, 0:R]).then_inc(r_T, 1)

        with ExitStack() as c3:
            def sb3(name, shape, dt=F32):
                return c3.enter_context(nc.sbuf_tensor(name, shape, dt))

            step_sems2 = []

            def sem3(name):
                step_sems2.append(c3.enter_context(nc.semaphore(name)))
                return step_sems2[-1]
            whq = sb3("whq", [P, C, IN2])
            w_in = [sb3(n, [P, C, IN2]) for n in ("w_in_k", "w_in_v")] + [sb3("w_in_o", [P, M2, E])]
            whk, whv = (sb3(n, [P, 2, C, IN2], F32R) for n in ("whk", "whv")); who = sb3("who", [P, 2, M2, E], F32R)
            null_col = sb3("null_col", [P, M2, 2])
            nq_b = sb3("nq_b", [P, E]); nv_b = sb3("nv_b", [P, H2, W2H])
            iota_r = sb3("iota_r", [P, NKV]); iota_c = sb3("iota_c", [P, 1])
            norm = sb3("norm", [P, 2, T, E]); light = sb3("light", [P, 2, T, E]); row = sb3("row", [P, 2, S])
            cols = sb3("cols", [P, T, 2]); scol = sb3("scol", [P, T, 2], F32R); oh = sb3("oh", [P, T, NSEL], F32R)
            nsplit = sb3("nsplit", [P, 2, T, E], F32R)
            qcol = sb3("qcol", [P, T]); qscore = sb3("qscore", [P, T]); unch = sb3("unch", [P, T]); ohT = sb3("ohT", [P, S], F32R)
            xq = sb3("xq", [P, C, NQ]); xkv = sb3("xkv", [P, 2, C, NKV], F32R); skv = sb3("skv", [P, 2])
            qh = sb3("qh", [P, 2, 2, M2, NQ], F32R); kh = sb3("kh", [P, 2, 2, M2, NKV + 2], F32R); vh = sb3("vh", [P, 2, 2, H2, W2H])
            nmh = sb3("nmh", [P, H2]); ph = sb3("ph", [P, 4, NKV + 1]); pTh = sb3("pTh", [P, 4, NKV])
            ou = sb3("ou", [P, H2, W2H]); rech = sb3("rech", [P, H2]); oa = sb3("oa", [P, IN2]); oaT = sb3("oaT", [P, 2, M2, NQ], F32R)
            hv = sb3("hv", [P, 2, E], F32R); base = sb3("base", [P, T, E]); sums = sb3("sums", [P, T, E])
            st2 = sb3("st2", [P, T, 6]); mv2 = sb3("mv2", [P, T, 2]); sc2 = sb3("sc2", [P, 2, T])
            outb = sb3("outb", [P, 2, T, E])
            h_w, h_whi, h_zero, h_init = (c3.enter_context(nc.semaphore(n)) for n in ("h_w", "h_whi", "h_zero", "h_init"))
            h_norm = [sem3("h_norm0"), sem3("h_norm1")]
            h_light = [sem3("h_light0"), sem3("h_light1")]
            h_row = [sem3("h_row0"), sem3("h_row1")]
            h_out = [sem3("h_out0"), sem3("h_out1")]
            h_full = sem3("h_full")
            h_act = sem3("h_act"); h_dve = sem3("h_dve")
            h_hi = sem3("h_hi")
            h_nhi = sem3("h_nhi"); h_split = sem3("h_split")
            h_max = sem3("h_max")
            h_oh = sem3("h_oh"); h_ohT = sem3("h_ohT")
            h_oa = sem3("h_oa"); h_base = sem3("h_base")
            h_var = sem3("h_var"); h_rstd = sem3("h_rstd"); h_y = sem3("h_y")
            h_link = sem3("h_link"); h_pool = sem3("h_pool")
            with nc.Block() as block:
                @block.sync
                def _(sp):
                    for dst, src in zip([whq] + w_in, (h_q, h_k, h_v, h_out_w)):
                        sp.dma_start(dst[:, :, :], src.rearrange("(c p) e -> p c e", p=P)).then_inc(h_w, 16)
                    sp.dma_start(null_col[:, :, 0:1], null_k.rearrange("(m h) (d a) -> (h d) m a", h=2, a=1),
                                 allow_slow_non_contiguous=True).then_inc(h_w, 16)
                    sp.dma_start(nv_b[:, :, 0:D2], null_v.rearrange("(a h) d -> a h d", a=1).broadcast_to([P, H2, D2])).then_inc(h_w, 16)
                    sp.dma_start(nq_b[:, :], null_q.rearrange("(a e) -> a e", a=1).broadcast_to([P, E])).then_inc(h_w, 16)
                    sp.wait_ge(h_w, 16 * 7)

                @block.scalar
                def _(act):
                    act.wait_ge(h_w, 16 * 7)
                    act.wait_ge(h_zero, 1)
                    for src, dst in zip(w_in, (whk, whv, who)):
                        nc.scalar.activation(dst[:, HI, :, :], src[:, :, :], ACT.Copy).then_inc(h_whi, 1)
                    for par in range(2):
                        nc.scalar.activation(kh[:, par, HI, :, NKV:NKV + 2], null_col[:, :, :], ACT.Copy).then_inc(h_whi, 1)

                @block.vector
                def _(dve):
                    nc.vector.memset(null_col[:, :, 1:2], 0.0).then_inc(h_zero, 1)
                    dve.wait_ge(h_zero, 1)
                    dve.wait_ge(h_w, 16 * 7)
                    for n, (src, dst) in enumerate(zip(w_in, (whk, whv, who))):
                        dve.wait_ge(h_whi, n + 1)
                        nc.vector.tensor_tensor(dst[:, LO, :, :], src[:, :, :], dst[:, HI, :, :], ALU.subtract)
                    for par in range(2):
                        dve.wait_ge(h_whi, 4 + par)
                        nc.vector.tensor_tensor(kh[:, par, LO, :, NKV:NKV + 2], null_col[:, :, :],
                                                kh[:, par, HI, :, NKV:NKV + 2], ALU.subtract)

                @block.gpsimd
                def _(pool):
                    nc.gpsimd.iota(iota_r[:, :], [[1, NKV]], base=0, channel_multiplier=0,
                                   allow_small_or_imprecise_dtypes=True).then_inc(h_init, 1)
                    nc.gpsimd.iota(iota_c[:, :], [[1, 1]], base=0, channel_multiplier=1,
                                   allow_small_or_imprecise_dtypes=True).then_inc(h_init, 1)
                    nc.gpsimd.memset(vh[:, :, :, :, D2:W2H], 1.0).then_inc(h_init, 1)
                    nc.gpsimd.memset(nv_b[:, :, D2:W2H], 1.0).then_inc(h_init, 1)

            def run_heavy(phases):
                tiles, at = [], {}
                for f, (_, _, has) in enumerate(phases):
                    for m in range(H2):
                        for kind, n in heavy_tiles(m, has):
                            at[f, kind, n] = len(tiles)
                            tiles.append(HEAVY_TAKEN_BY[kind])

                def full(f, kind, n):
                    return at[f, kind, n] + 1

                def at_place(n):
                    return (h_act, h_dve)[tiles[n]], sum(t == tiles[n] for t in tiles[:n + 1])

                def taken(f, kind, n=0):
                    return at_place(at[f, kind, n])

                def bank(f, kind, n):
                    return PS[:, at[f, kind, n] % 8, :]

                def before(f, piece, par=None):
                    return sum(piece in has and par in (None, q) for _, q, has in phases[:f])

                def had(f, piece):
                    return f > 0 and piece in phases[f - 1][2]

                def high(f, kind, n):
                    order = [key for key in at if key[1] in HEAVY_SPLIT]
                    return order.index((f, kind, n)) + 1

                def batch(tensor, n):
                    return seq(tensor, n).rearrange("a p e -> (a p) e")

                with nc.Block() as block:
                    @block.sync
                    def _(sp):
                        for f, (p, par, has) in enumerate(phases):
                            if "onehot" in has:
                                if before(f - 1, "onehot") and f > 1:
                                    sp.wait_ge(h_split, before(f - 1, "onehot"))
                                sp.dma_start(norm[:, par, :, :].rearrange("p t e -> p (t e)"),
                                             batch(norm_d, p + 2)).then_inc(h_norm[par], 16)
                            if "heads" in has:
                                if before(f - 1, "heads") and f > 1:
                                    sp.wait_ge(h_ohT, before(f - 1, "heads"))
                                this = slot_d[p:p + 1, :] if isinstance(p, int) else slot_d[bass.ds(p, 1), :]
                                sp.dma_start(row[:, par, :], this.broadcast_to([P, S])).then_inc(h_row[par], 16)
                                if had(f, "final"):
                                    sp.wait_ge(h_base, before(f, "final"))
                                sp.dma_start(light[:, par, :, :].rearrange("p t e -> p (t e)"),
                                             batch(light_d, p)).then_inc(h_light[par], 16)
                            if "final" in has:
                                sp.wait_ge(h_y, T * (before(f, "final") + 1))
                                sp.dma_start(seq(out, p - 1).rearrange("a (t p) e -> p (a t) e", p=P),
                                             outb[:, par, :, :]).then_inc(h_out[par], 16)
                        n = len(phases)
                        for q in range(2):
                            for s, piece in ((h_norm, "onehot"), (h_row, "heads"), (h_light, "heads"), (h_out, "final")):
                                if before(n, piece, q):
                                    sp.wait_ge(s[q], 16 * before(n, piece, q))

                    @block.gpsimd
                    def _(pool):
                        for f, (p, par, has) in enumerate(phases):
                            done = before(f, "final")
                            if "final" in has:
                                if had(f, "heads"):
                                    pool.wait_ge(h_light[1 - par], 16 * before(f, "heads", 1 - par))
                                    pool.wait_ge(h_ohT, before(f, "heads"))
                                if had(f, "final"):
                                    pool.wait_ge(*taken(f - 1, "sc", 1))
                                for t in range(T):
                                    nc.gpsimd.tensor_scalar(base[:, t, :], nq_b[:, :], unch[:, t:t + 1], None, ALU.mult).then_inc(h_pool, 1)
                                pool.wait_ge(h_pool, (T + 1) * done + T)
                                nc.gpsimd.tensor_tensor(base[:, :, :], base[:, :, :], light[:, 1 - par, :, :], ALU.add).then_inc(h_base, 1)
                            if "onehot" in has:
                                if "gather" in has:
                                    pool.wait_ge(h_full, full(f, "ga", 1))
                                pool.wait_ge(h_norm[par], 16 * (before(f, "onehot", par) + 1))
                                nc.gpsimd.tensor_copy(nsplit[:, HI, :, :], norm[:, par, :, :]).then_inc(h_nhi, 1)
                                pool.wait_ge(h_nhi, before(f, "onehot") + 1)
                                nc.gpsimd.tensor_tensor(nsplit[:, LO, :, :], norm[:, par, :, :], nsplit[:, HI, :, :],
                                                        ALU.subtract).then_inc(h_split, 1)
                            if "final" not in has:
                                continue
                            pool.wait_ge(h_var, done + 1)
                            nc.gpsimd.tensor_scalar(sc2[:, 0, :], mv2[:, :, 1], EPS_LN, None, ALU.add).then_inc(h_pool, 1)
                            pool.wait_ge(h_pool, (T + 1) * (done + 1))
                            pool_pow(sc2[:, 1, :], sc2[:, 0, :]).then_inc(h_rstd, 1)

                    @block.scalar
                    def _(act):
                        for f, (p, par, has) in enumerate(phases):
                            for m in range(H2):
                                for kind, n in heavy_tiles(m, has):
                                    b = bank(f, kind, n)
                                    if kind in HEAVY_SPLIT:
                                        act.wait_ge(h_full, full(f, kind, n))
                                        if kind == "ga":
                                            nc.scalar.activation(xq[:, n, :], b[:, 0:NQ], ACT.Copy, scale=gam[:, n:n + 1])
                                            ins = nc.scalar.activation(xkv[:, HI, n, :], b[:, NQ:NSEL], ACT.Copy, scale=gam[:, n:n + 1])
                                        elif kind == "q":
                                            ins = nc.scalar.activation(qh[:, 1 - par, HI, :, :].rearrange("p m s -> p (m s)"), b,
                                                                       ACT.Copy, scale=D2 ** -0.5)
                                        elif kind == "k":
                                            ins = nc.scalar.activation(kh[:, 1 - par, HI, 2 * n:2 * n + 2, 0:NKV],
                                                                       b.rearrange("p (m s) -> p m s", s=NKV), ACT.Copy)
                                        elif kind == "oT":
                                            ins = nc.scalar.activation(oaT[:, HI, :, :].rearrange("p m s -> p (m s)"), b, ACT.Copy)
                                        elif kind == "hv":
                                            ins = nc.scalar.activation(hv[:, HI, :], b[:, 0:E], ACT.Copy)
                                        ins.then_inc(h_hi, 1)
                                        continue
                                    if HEAVY_TAKEN_BY[kind] != BY_ACT:
                                        continue
                                    if kind == "S":
                                        act.wait_ge(h_max, H2 * before(f, "heads") + n + 1)
                                        if n >= 4:
                                            act.wait_ge(*taken(f, "O", n - 4))
                                        elif had(f, "heads"):
                                            act.wait_ge(*taken(f - 1, "O", n + 4))
                                        ins = nc.scalar.activation(ph[:, n % 4, :], b[:, 0:NKV + 1], ACT.Exp, bias=nmh[:, n:n + 1])
                                    else:
                                        act.wait_ge(h_full, full(f, kind, n))
                                    if kind == "T":
                                        ins = nc.scalar.activation(pTh[:, n % 4, :], b[:, 0:NKV], ACT.Copy)
                                    elif kind == "v":
                                        act.wait_ge(*taken(f, "skv"))
                                        ins = nc.scalar.activation(vh[:, 1 - par, n, :, 0:D2], b.rearrange("p (h d) -> p h d", d=D2),
                                                                   ACT.Copy, scale=skv[:, n:n + 1])
                                    ins.then_inc(h_act, 1)

                    @block.vector
                    def _(dve):
                        chain = [0]

                        def link(ins):
                            chain[0] += 1
                            ins.then_inc(h_link, 1)
                            dve.wait_ge(h_link, chain[0])

                        def column(tensor, which, n):
                            at_ = slice(which * NB + n, which * NB + n + 1) if isinstance(n, int) else bass.ds(n + which * NB, 1)
                            return tensor[:, :, at_].rearrange("p t b -> p (t b)")

                        for f, (p, par, has) in enumerate(phases):
                            for m in range(H2):
                                for kind, n in heavy_tiles(m, has):
                                    b = bank(f, kind, n)
                                    if kind == "S":
                                        dve.wait_ge(h_full, full(f, kind, n))
                                        nc.vector.reduce_max(nmh[:, n:n + 1], b[:, 0:NKV + 1], AX.X, negate=True).then_inc(h_max, 1)
                                    if HEAVY_TAKEN_BY[kind] != BY_DVE:
                                        continue
                                    dve.wait_ge(h_full, full(f, kind, n))
                                    if kind == "O":
                                        ins = nc.vector.scalar_tensor_tensor(out=ou[:, n, :], in0=nv_b[:, n, :],
                                                                             scalar=ph[:, n % 4, NKV:NKV + 1], in1=b[:, 0:W2H],
                                                                             op0=ALU.mult, op1=ALU.add)
                                    elif kind == "skv":
                                        if had(f, "gather"):
                                            dve.wait_ge(*taken(f - 1, "v", 1))
                                        ins = nc.vector.reduce_sum(skv[:, :], b[:, 0:4].rearrange("p (s part) -> p s part", part=2), AX.X)
                                    elif kind in HEAVY_SPLIT:
                                        dve.wait_ge(h_hi, high(f, kind, n))
                                        if kind == "ga":
                                            ins = nc.vector.scalar_tensor_tensor(out=xkv[:, LO, n, :], in0=b[:, NQ:NSEL],
                                                                                 scalar=gam[:, n:n + 1], in1=xkv[:, HI, n, :],
                                                                                 op0=ALU.mult, op1=ALU.subtract)
                                        elif kind == "q":
                                            ins = nc.vector.scalar_tensor_tensor(out=qh[:, 1 - par, LO, :, :],
                                                                                 in0=b.rearrange("p (m s) -> p m s", s=NQ),
                                                                                 scalar=D2 ** -0.5, in1=qh[:, 1 - par, HI, :, :],
                                                                                 op0=ALU.mult, op1=ALU.subtract)
                                        elif kind == "k":
                                            ins = nc.vector.tensor_tensor(kh[:, 1 - par, LO, 2 * n:2 * n + 2, 0:NKV],
                                                                          b.rearrange("p (m s) -> p m s", s=NKV),
                                                                          kh[:, 1 - par, HI, 2 * n:2 * n + 2, 0:NKV], ALU.subtract)
                                        elif kind == "oT":
                                            ins = nc.vector.tensor_tensor(oaT[:, LO, :, :], b.rearrange("p (m s) -> p m s", s=NQ),
                                                                          oaT[:, HI, :, :], ALU.subtract)
                                        elif kind == "hv":
                                            ins = nc.vector.tensor_tensor(hv[:, LO, :], b[:, 0:E], hv[:, HI, :], ALU.subtract)
                                    elif kind == "sc":
                                        if n == 0:
                                            dve.wait_ge(h_base, before(f, "final") + 1)
                                        for t in (2 * n, 2 * n + 1):
                                            ins = nc.vector.scalar_tensor_tensor(out=sums[:, t, :], in0=b[:, E * (t % 2):E * (t % 2) + E],
                                                                                 scalar=qscore[:, t:t + 1], in1=base[:, t, :],
                                                                                 op0=ALU.mult, op1=ALU.add)
                                    ins.then_inc(h_dve, 1)
                                if "onehot" in has and m == 2:
                                    if "gather" in has:
                                        dve.wait_ge(h_full, full(f, "ga", 1))
                                    for which in range(2):
                                        nc.vector.tensor_copy(cols[:, :, which], column(slotT, which, p + 2))
                                    link(nc.vector.tensor_copy(scol[:, :, HI], column(scoreT, 1, p + 2)))
                                    link(nc.vector.tensor_tensor(scol[:, :, LO], column(scoreT, 1, p + 2), scol[:, :, HI], ALU.subtract))
                                if "onehot" in has and m in (2, 3):
                                    for t in (2 * m - 4, 2 * m - 3):
                                        nc.vector.tensor_scalar(oh[:, t, 0:NQ], iota_r[:, 0:NQ], cols[:, t, 0:1], None,
                                                                ALU.is_equal).then_inc(h_oh, 1)
                                        nc.vector.tensor_scalar(oh[:, t, NQ:NSEL], iota_r[:, :], cols[:, t, 1:2], None,
                                                                ALU.is_equal).then_inc(h_oh, 1)
                                if "final" in has and m == 4:
                                    dve.wait_ge(*taken(f, "sc", 1))
                                    for t in range(T):
                                        ins = nc.vector.bn_stats(st2[:, t, :], sums[:, t, :])
                                    link(ins)
                                    for t in range(T):
                                        ins = nc.vector.bn_aggr(mv2[:, t, :], st2[:, t, :])
                                    link(ins)
                                    dve.sem_inc(h_var, 1)
                                if "heads" in has and m == 5:
                                    if "final" in has:
                                        dve.wait_ge(h_base, before(f, "final") + 1)
                                        dve.wait_ge(h_full, full(f, "sc", 1))
                                    link(nc.vector.tensor_copy(qcol[:, :], column(slotT, 0, p)))
                                    nc.vector.tensor_copy(qscore[:, :], column(scoreT, 0, p))
                                    link(nc.vector.tensor_scalar(unch[:, :], qcol[:, :], 0.0, None, ALU.is_lt))
                                    dve.wait_ge(h_row[par], 16 * (before(f, "heads", par) + 1))
                                    nc.vector.tensor_scalar(ohT[:, :], row[:, par, :], iota_c[:, 0:1], None,
                                                            ALU.is_equal).then_inc(h_ohT, 1)
                                if "final" in has and m == 6:
                                    dve.wait_ge(h_rstd, before(f, "final") + 1)
                                    if before(f, "final", par):
                                        dve.wait_ge(h_out[par], 16 * before(f, "final", par))
                                    for t in range(T):
                                        nc.vector.tensor_scalar(outb[:, par, t, :], sums[:, t, :], mv2[:, t, 0:1], sc2[:, 1, t:t + 1],
                                                                ALU.subtract, ALU.mult).then_inc(h_y, 1)
                            if "heads" in has:
                                dve.wait_ge(*taken(f, "O", 7))
                                link(nc.vector.reciprocal(rech[:, :], ou[:, :, D2]))
                                nc.vector.tensor_tensor(oa[:, :].rearrange("p (h d) -> p h d", d=D2), ou[:, :, 0:D2],
                                                        rech[:, :].rearrange("p (h a) -> p h a", a=1).broadcast_to([P, H2, D2]),
                                                        ALU.mult).then_inc(h_oa, 1)

                    @block.tensor
                    def _(pe):
                        for f, (p, par, has) in enumerate(phases):
                            for m in range(H2):
                                for kind, n in heavy_tiles(m, has):
                                    b, place = bank(f, kind, n), at[f, kind, n]
                                    if place >= 8:
                                        pe.wait_ge(*at_place(place - 8))
                                    if kind == "S":
                                        if n == 0 and had(f, "gather"):
                                            pe.wait_ge(*taken(f - 1, "q"))
                                            pe.wait_ge(*taken(f - 1, "k", 1))
                                        r = D2 * (n % 2)
                                        ins = product(b[:, 0:NKV + 2], lambda part: qh[r:r + D2, par, part, n // 2, :],
                                                      lambda part: kh[r:r + D2, par, part, n // 2, :], True, True)
                                    elif kind == "T":
                                        pe.wait_ge(*taken(f, "S", n))
                                        for s in range(2):
                                            ins = nc.tensor.transpose(b[:, s * P:(s + 1) * P], ph[:, n % 4, s * P:(s + 1) * P], ident[:, :])
                                    elif kind == "O":
                                        pe.wait_ge(*taken(f, "T", n))
                                        if n == 0 and had(f, "gather"):
                                            pe.wait_ge(*taken(f - 1, "v", 1))
                                        for s in range(2):
                                            ins = nc.tensor.matmul(b[:, 0:W2H], pTh[:, n % 4, s * P:(s + 1) * P],
                                                                   vh[:, par, s, n, :], start=s == 0, stop=s == 1)
                                    elif kind == "ga":
                                        if n == 0 and had(f, "onehot"):
                                            pe.wait_ge(h_oh, 2 * T * before(f, "onehot"))
                                            pe.wait_ge(h_split, before(f, "onehot"))
                                        for part in (LO, HI):
                                            for t in range(T):
                                                ins = nc.tensor.matmul(b[:, 0:NSEL], nsplit[:, part, t, n * P:(n + 1) * P], oh[:, t, :],
                                                                       start=(part, t) == (LO, 0), stop=(part, t) == (HI, T - 1))
                                    elif kind == "skv":
                                        for s in range(2):
                                            for t in range(T):
                                                ins = nc.tensor.matmul(b[:, 2 * s:2 * s + 2], oh[:, t, NQ + s * P:NQ + (s + 1) * P],
                                                                       scol[:, t, :], start=t == 0, stop=t == T - 1)
                                    elif kind == "q":
                                        pe.wait_ge(*taken(f, "ga", 1))
                                        for j in range(M2):
                                            for c in range(C):
                                                ins = nc.tensor.matmul(b[:, j * NQ:(j + 1) * NQ], whq[:, c, j * P:(j + 1) * P],
                                                                       xq[:, c, :], start=c == 0, stop=c == C - 1)
                                    elif kind == "k":
                                        for j in (2 * n, 2 * n + 1):
                                            for c in range(C):
                                                ins = product(b[:, NKV * (j % 2):NKV * (j % 2) + NKV],
                                                              lambda part: whk[:, part, c, j * P:(j + 1) * P],
                                                              lambda part: xkv[:, part, c, :], c == 0, c == C - 1)
                                    elif kind == "v":
                                        for c in range(C):
                                            ins = product(b, lambda part: xkv[:, part, c, n * P:(n + 1) * P],
                                                          lambda part: whv[:, part, c, :], c == 0, c == C - 1)
                                    elif kind == "oT":
                                        if had(f, "heads"):
                                            pe.wait_ge(h_oa, before(f, "heads"))
                                        for j in range(M2):
                                            ins = nc.tensor.transpose(b[:, j * P:(j + 1) * P], oa[:, j * P:(j + 1) * P], ident[:, :])
                                    elif kind == "hv":
                                        pe.wait_ge(*taken(f, "oT"))
                                        for j in range(M2):
                                            ins = product(b[:, 0:E], lambda part: oaT[:, part, j, :], lambda part: who[:, part, j, :],
                                                          j == 0, j == M2 - 1)
                                    elif kind == "sc":
                                        if n == 0:
                                            pe.wait_ge(*taken(f, "hv"))
                                            if had(f, "heads"):
                                                pe.wait_ge(h_ohT, before(f, "heads"))
                                        for t in (2 * n, 2 * n + 1):
                                            for part in (LO, HI):
                                                ins = nc.tensor.matmul(b[:, E * (t % 2):E * (t % 2) + E], ohT[:, t * P:(t + 1) * P],
                                                                       hv[:, part, :], start=part == LO, stop=part == HI)
                                    ins.then_inc(h_full, 1)
                nc.all_engine_barrier(sems_to_clear=range(step_sems2[0].num, step_sems2[-1].num + 1))

            every = ("onehot", "gather", "heads", "final")
            run_heavy([(-2, 0, every[:1]), (-1, 1, every[:2]), (0, 0, every[:3]), (1, 1, every)])
            with nc.Fori(2, NB - 11, 6) as i:
                run_heavy([(i + j, j % 2, every) for j in range(6)])
            run_heavy([(NB - 6 + j, j % 2, every) for j in range(4)] +
                      [(NB - 2, 0, every[1:]), (NB - 1, 1, every[2:]), (NB, 0, every[3:])])


_INS = ["x", "xT", "wq", "wk", "wv", "wo", "aq", "ak", "av", "ao", "bq_", "bk_", "bv_", "bo_",
        "vec_q", "vec_k", "vec_v", "vec_o", "ln_w", "ln_b", "l_qk", "l_v", "l_out", "rt_q", "rt_kv",
        "gamma", "h_q", "h_k", "h_v", "h_out_w", "null_k", "null_v", "null_q"]


def kernel(**inputs):
    import numpy as _np
    import concourse.bacc as _bacc
    from concourse import mybir as _mybir
    from concourse.bass_utils import run_bass_kernel_spmd as _run

    def of(name):
        return _np.asarray(inputs["L0_" + name])

    x = of("attn_x")
    wqkv = of("ffn_Wqkv")
    wkv = of("ffn_Wkv").reshape(H2, 2, D2, E)
    laid = {
        "x": x, "xT": x.transpose(0, 2, 1),
        "ln_w": of("ffn_ln_w"), "ln_b": of("ffn_ln_b"), "gamma": of("ffn_gamma"),
        "l_qk": wqkv[:2 * IN2].T, "l_v": wqkv[2 * IN2:].T, "l_out": of("ffn_Wout_l").T,
        "rt_q": of("ffn_rt_q"), "rt_kv": of("ffn_rt_kv"),
        "h_q": of("ffn_Wq").T, "h_k": wkv[:, 0].reshape(IN2, E).T, "h_v": wkv[:, 1].reshape(IN2, E).T,
        "h_out_w": of("ffn_Wout_h").T, "null_k": of("ffn_null_kv")[0], "null_v": of("ffn_null_kv")[1],
        "null_q": of("ffn_null_q"),
    }
    for n in "qkvo":
        laid["w" + n] = of("attn_W" + n).T
        laid["b" + n + "_"] = of("attn_b" + n)
        laid["a" + n] = of("attn_A" + n)
        laid["vec_" + n] = of("attn_B" + n).T

    nc = _bacc.Bacc("TRN2", target_bir_lowering=False, num_devices=1)
    arrays, args = {}, []
    for name in _INS:
        a = _np.ascontiguousarray(laid[name])
        arrays[f"in_{name}_dram"] = a
        args.append(nc.dram_tensor(f"in_{name}_dram", a.shape, _mybir.dt.from_np(a.dtype), kind="ExternalInput").ap())
    out = nc.dram_tensor("out_0_dram", x.shape, _mybir.dt.float32, kind="ExternalOutput").ap()
    block_kernel(nc, *args, out)
    r = _run(nc, [arrays], core_ids=[0])
    return r.results[0]["out_0_dram"]
```
